# Optimizing a Trainium2 kernel written in Bass

```python
import numpy as np
import jax
import jax.numpy as jnp

def _softmax(x, axis=-1):
    return jax.nn.softmax(x, axis=axis)

def _gelu(x):
    return jax.nn.gelu(x, approximate=True)

def _silu(x):
    return jax.nn.silu(x)

def _sigmoid(x):
    return jax.nn.sigmoid(x)

def _layernorm(x, axis=-1, eps=1e-05):
    m = jnp.mean(x, axis=axis, keepdims=True)
    v = jnp.var(x, axis=axis, keepdims=True)
    return (x - m) / jnp.sqrt(v + eps)

def _scatter_add(tgt, idx, src, axis=0):
    return tgt.at[idx].add(src)

def _segment_sum(src, seg, n):
    return jax.ops.segment_sum(src, seg, n)
kernel_name = 'mk_flamingo_gated_d2_seqx_r8_2f1be6'

def setup_inputs(seed: int=0):
    np.random.seed(seed)
    _w = jnp.asarray

    def _rec_inputs():
        import jax
        import jax.numpy as jnp
        _rk = jax.random.key(seed)
        x = -0.0002928 + 1 * jax.random.normal(jax.random.fold_in(_rk, 1), (4, 256, 128), jnp.float32)
        _lenS = 256 - jax.random.randint(jax.random.fold_in(_rk, 7), (4,), 0, max(1, 256 // 4) + 1, jnp.int32)
        _lenS2 = 256 - jax.random.randint(jax.random.fold_in(_rk, 8), (4,), 0, max(1, 256 // 4) + 1, jnp.int32)
        _ctx_1024P = jax.random.normal(jax.random.fold_in(_rk, 11), (4, 16, 128), jnp.float32)
        _ctx_1024c = jax.random.dirichlet(jax.random.fold_in(_rk, 511), 0.3 * jnp.ones((16,), jnp.float32), (4, 256))
        _ctx_1024t = jnp.einsum('bsk,bkd->bsd', _ctx_1024c, _ctx_1024P)
        _ctx_1024t = _ctx_1024t * jax.lax.rsqrt(jnp.mean(jnp.square(_ctx_1024t)) + 1e-12) * 0.953939
        ctx_1024 = -1.39393e-06 + 0.999914 * (_ctx_1024t + 0.3 * jax.random.normal(jax.random.fold_in(_rk, 611), (4, 256, 128), jnp.float32))
        _validS = jnp.arange(256)[None, :] < _lenS[:, None]
        _validS2 = jnp.arange(256)[None, :] < _lenS2[:, None]
        _causal = jnp.tril(jnp.ones((256, 256), dtype=bool))
        mask_BxS2_bf1 = jnp.ones((4, 256), dtype=bool)
        _g = jax.random.normal(jax.random.fold_in(_rk, 9001), (2, 2), jnp.float32)
        _g = jnp.sign(_g) * jnp.maximum(jnp.abs(_g), 1.0) + (_g == 0) * 1.0
        g_xattn = _g[0]
        g_ffn = _g[1]
        return (x, ctx_1024, mask_BxS2_bf1, g_xattn, g_ffn)
    x, ctx_1024, mask_BxS2_bf1, g_xattn, g_ffn = _rec_inputs()

    def _L0_xattn_setup():
        import math
        import jax, jax.numpy as jnp
        import numpy as np
        B, S, H, NH = (2, 256, 128, 4)
        DH = H // NH

        def _mlstm_parallel(qh, kh, vh, ig, fg, eps=1e-06):
            b, nh, s, dh = qh.shape
            log_f = jax.nn.log_sigmoid(fg)
            pcs = jnp.pad(jnp.cumsum(log_f, axis=-1), ((0, 0), (0, 0), (1, 0)))
            mat = pcs[..., :, None] - pcs[..., None, :]
            ltr = jnp.tril(jnp.ones((s, s), dtype=bool))
            log_fg_matrix = jnp.where(ltr, mat[..., 1:, 1:], -jnp.inf)
            log_D = log_fg_matrix + ig[..., None, :]
            max_log_D = jnp.max(log_D, axis=-1, keepdims=True)
            D = jnp.exp(log_D - max_log_D)
            qk = jnp.einsum('bhsd,bhtd->bhst', qh, kh) / math.sqrt(dh)
            C = qk * D
            normalizer = jnp.maximum(jnp.abs(C.sum(axis=-1, keepdims=True)), jnp.exp(-max_log_D))
            Cn = C / (normalizer + eps)
            return jnp.einsum('bhst,bhtd->bhsd', Cn, vh)
        key = jax.random.key(seed)
        ks = jax.random.split(key, 8)
        gate_std = 1.0 / math.sqrt(3 * H)
        return {'q': jax.random.normal(ks[0], (B, S, H), jnp.float32), 'k': jax.random.normal(ks[1], (B, S, H), jnp.float32), 'v': jax.random.normal(ks[2], (B, S, H), jnp.float32), 'w_igate': jax.random.normal(ks[3], (NH, 3 * H), jnp.float32) * gate_std, 'b_igate': jax.random.normal(ks[4], (NH,), jnp.float32) * 0.1, 'w_fgate': jax.random.normal(ks[5], (NH, 3 * H), jnp.float32) * gate_std, 'b_fgate': jnp.linspace(3.4, 6.0, NH, dtype=jnp.float32), 'ln_weight': jnp.zeros((H,), jnp.float32)}
    _L0_xattn_all = _L0_xattn_setup()
    _L0_xattn_in = {k: v for k, v in _L0_xattn_all.items() if k in ('w_igate', 'b_igate', 'w_fgate', 'b_fgate', 'ln_weight')}
    del _L0_xattn_all

    def _L0_ffn_setup():
        import jax, jax.numpy as jnp
        import numpy as np
        B, T, DIM = (4, 128, 128)
        H, E, DH, K = (8, 5, 64, 3)

        def _topk_mask(s, k):
            idx = jax.lax.top_k(s, k)[1]
            return jnp.sum(jax.nn.one_hot(idx, s.shape[-1], dtype=s.dtype), axis=-2)
        key = jax.random.key(seed)
        ks = jax.random.split(key, 6)
        w = lambda k, shape: jax.random.normal(k, shape, jnp.float32) * 0.02
        return {'x': jax.random.normal(ks[0], (B, T, DIM), jnp.float32), 'Wq': w(ks[1], (DIM, H * E * DH)), 'Wkv': w(ks[2], (DIM, 2 * H * E * DH)), 'Ws': w(ks[3], (DIM, H * E)), 'Wd': w(ks[4], (DIM, H * E)), 'Wo': w(ks[5], (DH, E * DIM))}
    _L0_ffn_all = _L0_ffn_setup()
    _L0_ffn_in = {k: v for k, v in _L0_ffn_all.items() if k in ('Wq', 'Wkv', 'Ws', 'Wd', 'Wo')}
    del _L0_ffn_all

    def _L1_xattn_setup():
        import jax, jax.numpy as jnp
        import numpy as np
        DIM = 128
        HEADS = 16
        DIM_HEAD = 64
        INNER = HEADS * DIM_HEAD
        B, F, Q = (16, 512, 64)
        EPS = 1e-05
        SCALE = DIM_HEAD ** (-0.5)

        def _layernorm(x, gamma, beta):
            mu = jnp.mean(x, axis=-1, keepdims=True)
            var = jnp.var(x, axis=-1, keepdims=True)
            return (x - mu) * jax.lax.rsqrt(var + EPS) * gamma + beta
        key = jax.random.key(seed)
        ks = jax.random.split(key, 8)
        features = jax.random.normal(ks[0], (B, F, DIM), dtype=jnp.float32)
        masks = jnp.ones((B, F), dtype=bool)
        latents = jax.random.normal(ks[1], (B, Q, DIM), dtype=jnp.float32)
        Wq = jax.random.normal(ks[2], (DIM, INNER), dtype=jnp.float32) / np.sqrt(DIM)
        Wk = jax.random.normal(ks[3], (DIM, INNER), dtype=jnp.float32) / np.sqrt(DIM)
        Wv = jax.random.normal(ks[4], (DIM, INNER), dtype=jnp.float32) / np.sqrt(DIM)
        Wo = jax.random.normal(ks[5], (INNER, DIM), dtype=jnp.float32) / np.sqrt(INNER)
        gm = jnp.ones((DIM,), jnp.float32)
        bm = jnp.zeros((DIM,), jnp.float32)
        gl = jnp.ones((DIM,), jnp.float32)
        bl = jnp.zeros((DIM,), jnp.float32)
        return {'features': features, 'masks': masks, 'latents': latents, 'gm': gm, 'bm': bm, 'gl': gl, 'bl': bl, 'Wq': Wq, 'Wk': Wk, 'Wv': Wv, 'Wo': Wo}
    _L1_xattn_all = _L1_xattn_setup()
    _L1_xattn_in = {k: v for k, v in _L1_xattn_all.items() if k in ('gm', 'bm', 'gl', 'bl', 'Wq', 'Wk', 'Wv', 'Wo')}
    del _L1_xattn_all

    def _L1_ffn_setup():
        import jax, jax.numpy as jnp
        import numpy as np
        NUM_EXPERTS = 8
        N_EMBD = 128
        D_FF = 4 * N_EMBD
        B, S = (4, 256)
        key = jax.random.key(seed)
        ks = jax.random.split(key, 6)
        x = jax.random.normal(ks[0], (B, S, N_EMBD), dtype=jnp.float32)
        gate_w = jax.random.normal(ks[1], (N_EMBD, NUM_EXPERTS), dtype=jnp.float32) * 0.02
        w1 = jax.random.normal(ks[2], (NUM_EXPERTS, N_EMBD, D_FF), dtype=jnp.float32) * 0.02
        b1 = jnp.zeros((NUM_EXPERTS, D_FF), dtype=jnp.float32)
        w2 = jax.random.normal(ks[3], (NUM_EXPERTS, D_FF, N_EMBD), dtype=jnp.float32) * 0.02
        b2 = jnp.zeros((NUM_EXPERTS, N_EMBD), dtype=jnp.float32)
        return {'x': x, 'gate_w': gate_w, 'w1': w1, 'b1': b1, 'w2': w2, 'b2': b2}
    _L1_ffn_all = _L1_ffn_setup()
    _L1_ffn_in = {k: v for k, v in _L1_ffn_all.items() if k in ('gate_w', 'w1', 'b1', 'w2', 'b2')}
    del _L1_ffn_all
    return {'x': x, 'ctx_1024': ctx_1024, 'mask_BxS2_bf1': mask_BxS2_bf1, 'g_xattn': g_xattn, 'g_ffn': g_ffn, 'L0_xattn_w_igate': _L0_xattn_in['w_igate'], 'L0_xattn_b_igate': _L0_xattn_in['b_igate'], 'L0_xattn_w_fgate': _L0_xattn_in['w_fgate'], 'L0_xattn_b_fgate': _L0_xattn_in['b_fgate'], 'L0_xattn_ln_weight': _L0_xattn_in['ln_weight'], 'L0_ffn_Wq': _L0_ffn_in['Wq'], 'L0_ffn_Wkv': _L0_ffn_in['Wkv'], 'L0_ffn_Ws': _L0_ffn_in['Ws'], 'L0_ffn_Wd': _L0_ffn_in['Wd'], 'L0_ffn_Wo': _L0_ffn_in['Wo'], 'L1_xattn_gm': _L1_xattn_in['gm'], 'L1_xattn_bm': _L1_xattn_in['bm'], 'L1_xattn_gl': _L1_xattn_in['gl'], 'L1_xattn_bl': _L1_xattn_in['bl'], 'L1_xattn_Wq': _L1_xattn_in['Wq'], 'L1_xattn_Wk': _L1_xattn_in['Wk'], 'L1_xattn_Wv': _L1_xattn_in['Wv'], 'L1_xattn_Wo': _L1_xattn_in['Wo'], 'L1_ffn_gate_w': _L1_ffn_in['gate_w'], 'L1_ffn_w1': _L1_ffn_in['w1'], 'L1_ffn_b1': _L1_ffn_in['b1'], 'L1_ffn_w2': _L1_ffn_in['w2'], 'L1_ffn_b2': _L1_ffn_in['b2']}

def reference(x, ctx_1024, mask_BxS2_bf1, g_xattn, g_ffn, L0_xattn_w_igate, L0_xattn_b_igate, L0_xattn_w_fgate, L0_xattn_b_fgate, L0_xattn_ln_weight, L0_ffn_Wq, L0_ffn_Wkv, L0_ffn_Ws, L0_ffn_Wd, L0_ffn_Wo, L1_xattn_gm, L1_xattn_bm, L1_xattn_gl, L1_xattn_bl, L1_xattn_Wq, L1_xattn_Wk, L1_xattn_Wv, L1_xattn_Wo, L1_ffn_gate_w, L1_ffn_w1, L1_ffn_b1, L1_ffn_w2, L1_ffn_b2):
    import jax
    import jax.numpy as jnp

    def _L0_xattn_ref(q, k, v, w_igate, b_igate, w_fgate, b_fgate, ln_weight):
        import math
        import jax, jax.numpy as jnp
        import numpy as np
        B, S, H, NH = (2, 256, 128, 4)
        DH = H // NH

        def _mlstm_parallel(qh, kh, vh, ig, fg, eps=1e-06):
            b, nh, s, dh = qh.shape
            log_f = jax.nn.log_sigmoid(fg)
            pcs = jnp.pad(jnp.cumsum(log_f, axis=-1), ((0, 0), (0, 0), (1, 0)))
            mat = pcs[..., :, None] - pcs[..., None, :]
            ltr = jnp.tril(jnp.ones((s, s), dtype=bool))
            log_fg_matrix = jnp.where(ltr, mat[..., 1:, 1:], -jnp.inf)
            log_D = log_fg_matrix + ig[..., None, :]
            max_log_D = jnp.max(log_D, axis=-1, keepdims=True)
            D = jnp.exp(log_D - max_log_D)
            qk = jnp.einsum('bhsd,bhtd->bhst', qh, kh) / math.sqrt(dh)
            C = qk * D
            normalizer = jnp.maximum(jnp.abs(C.sum(axis=-1, keepdims=True)), jnp.exp(-max_log_D))
            Cn = C / (normalizer + eps)
            return jnp.einsum('bhst,bhtd->bhsd', Cn, vh)
        b, s, h = q.shape
        nh = b_igate.shape[0]
        dh = h // nh
        gin = jnp.concatenate([q, k, v], axis=-1)
        ig = jnp.einsum('bsd,hd->bhs', gin, w_igate) + b_igate[None, :, None]
        fg = jnp.einsum('bsd,hd->bhs', gin, w_fgate) + b_fgate[None, :, None]
        qh = q.reshape(b, s, nh, dh).transpose(0, 2, 1, 3)
        kh = k.reshape(b, s, nh, dh).transpose(0, 2, 1, 3)
        vh = v.reshape(b, s, nh, dh).transpose(0, 2, 1, 3)
        hst = _mlstm_parallel(qh, kh, vh, ig, fg)
        mean = hst.mean(axis=-1, keepdims=True)
        var = hst.var(axis=-1, keepdims=True)
        hn = (hst - mean) / jnp.sqrt(var + 1e-05)
        scale = (1.0 + ln_weight).reshape(nh, dh)
        hn = hn * scale[None, :, None, :]
        return hn.transpose(0, 2, 1, 3).reshape(b, s, h)

    def _L0_ffn_ref(x, Wq, Wkv, Ws, Wd, Wo):
        import jax, jax.numpy as jnp
        import numpy as np
        B, T, DIM = (4, 128, 128)
        H, E, DH, K = (8, 5, 64, 3)

        def _topk_mask(s, k):
            idx = jax.lax.top_k(s, k)[1]
            return jnp.sum(jax.nn.one_hot(idx, s.shape[-1], dtype=s.dtype), axis=-2)
        b, t, _ = x.shape
        scale = DH ** (-0.5)
        ss = jax.nn.sigmoid(x @ Ws).reshape(b, t, H, E)
        sd = jax.nn.sigmoid(x @ Wd).reshape(b, t, H, E)
        ms = _topk_mask(ss, K)
        md = _topk_mask(sd, K)
        ss_g = ss * ms
        sd_g = sd * md
        q5 = (x @ Wq).reshape(b, t, H, E, DH)
        kv = (x @ Wkv).reshape(b, t, 2, H, E, DH)
        k5, v5 = (kv[:, :, 0], kv[:, :, 1])
        q = jnp.einsum('bthed,bthe->bhtd', q5, sd_g)
        k = jnp.einsum('bthed,bthe->bhtd', k5, ss_g)
        v = jnp.einsum('bthed,bthe->bhtd', v5, ss_g)
        attn = jax.nn.softmax(jnp.einsum('bhid,bhjd->bhij', q * scale, k), axis=-1)
        out = jnp.einsum('bhij,bhjd->bihd', attn, v)
        o5 = jnp.einsum('bthd,dm->bthm', out, Wo).reshape(b, t, H, E, DIM)
        return jnp.einsum('bthem,bthe->btm', o5, md)

    def _L1_xattn_ref(features, masks, latents, gm, bm, gl, bl, Wq, Wk, Wv, Wo):
        import jax, jax.numpy as jnp
        import numpy as np
        DIM = 128
        HEADS = 16
        DIM_HEAD = 64
        INNER = HEADS * DIM_HEAD
        B, F, Q = (16, 512, 64)
        EPS = 1e-05
        SCALE = DIM_HEAD ** (-0.5)

        def _layernorm(x, gamma, beta):
            mu = jnp.mean(x, axis=-1, keepdims=True)
            var = jnp.var(x, axis=-1, keepdims=True)
            return (x - mu) * jax.lax.rsqrt(var + EPS) * gamma + beta
        b, f, d = features.shape
        q_len = latents.shape[1]
        x = _layernorm(features, gm, bm)
        lat = _layernorm(latents, gl, bl)
        q = (lat @ Wq).reshape(b, q_len, HEADS, DIM_HEAD).transpose(0, 2, 1, 3)
        kv_input = jnp.concatenate([x, lat], axis=1)
        kv_mask = jnp.concatenate([masks, jnp.ones((b, q_len), dtype=bool)], axis=1)
        kv_mask = kv_mask[:, None, None, :]
        k = (kv_input @ Wk).reshape(b, f + q_len, HEADS, DIM_HEAD).transpose(0, 2, 1, 3)
        v = (kv_input @ Wv).reshape(b, f + q_len, HEADS, DIM_HEAD).transpose(0, 2, 1, 3)
        q = q * SCALE
        sim = jnp.einsum('bhqd,bhfd->bhqf', q, k)
        sim = sim - jax.lax.stop_gradient(jnp.max(sim, axis=-1, keepdims=True))
        sim = jnp.where(kv_mask, sim, -jnp.inf)
        alphas = jax.nn.softmax(sim, axis=-1)
        out = jnp.einsum('bhqf,bhfd->bhqd', alphas, v)
        out = out.transpose(0, 2, 1, 3).reshape(b, q_len, INNER)
        return out @ Wo

    def _L1_ffn_ref(x, gate_w, w1, b1, w2, b2):
        import jax, jax.numpy as jnp
        import numpy as np
        NUM_EXPERTS = 8
        N_EMBD = 128
        D_FF = 4 * N_EMBD
        B, S = (4, 256)
        Bb, Ss, D = x.shape
        x_flat = x.reshape(-1, D)
        router_logits = x_flat @ gate_w
        router_probs = jax.nn.softmax(router_logits, axis=-1)
        expert_idx = jnp.argmax(router_probs, axis=-1)
        expert_w = jnp.take_along_axis(router_probs, expert_idx[:, None], axis=1)[:, 0]
        out = jnp.zeros_like(x_flat)
        for e in range(NUM_EXPERTS):
            h = jax.nn.gelu(x_flat @ w1[e] + b1[e], approximate=False)
            y = h @ w2[e] + b2[e]
            sel = expert_idx == e
            out = out + jnp.where(sel, expert_w, 0.0)[:, None] * y
        return out.reshape(Bb, Ss, D)
    x = x + jnp.tanh(g_xattn[0]) * _L0_xattn_ref(_layernorm(x, axis=-1), ctx_1024, ctx_1024, L0_xattn_w_igate, L0_xattn_b_igate, L0_xattn_w_fgate, L0_xattn_b_fgate, L0_xattn_ln_weight)
    x = x + jnp.tanh(g_ffn[0]) * _L0_ffn_ref(_layernorm(x, axis=-1), L0_ffn_Wq, L0_ffn_Wkv, L0_ffn_Ws, L0_ffn_Wd, L0_ffn_Wo)
    x = x + jnp.tanh(g_xattn[1]) * _L1_xattn_ref(ctx_1024, mask_BxS2_bf1, _layernorm(x, axis=-1), L1_xattn_gm, L1_xattn_bm, L1_xattn_gl, L1_xattn_bl, L1_xattn_Wq, L1_xattn_Wk, L1_xattn_Wv, L1_xattn_Wo)
    x = x + jnp.tanh(g_ffn[1]) * _L1_ffn_ref(_layernorm(x, axis=-1), L1_ffn_gate_w, L1_ffn_w1, L1_ffn_b1, L1_ffn_w2, L1_ffn_b2)
    return x

_drawn_inputs = setup_inputs


def setup_inputs(seed=0):
    import zlib

    import numpy as np

    out = dict(_drawn_inputs(seed))
    spreads = {'g_ffn': (-1.0, 0.6),
     'L0_xattn_ln_weight': (0.0, 0.1),
     'L1_xattn_gm': (1.0, 0.6),
     'L1_xattn_bm': (0.0, 0.504),
     'L1_xattn_gl': (1.0, 0.6),
     'L1_xattn_bl': (0.0, 0.379),
     'L1_ffn_b1': (0.0, 0.8),
     'L1_ffn_b2': (0.0, 0.8)}
    factors = {'L0_xattn_b_igate': 64.0,
     'L0_ffn_Wq': 8.0,
     'L0_ffn_Wkv': 7.254,
     'L0_ffn_Ws': 8.0,
     'L0_ffn_Wd': 8.0,
     'L0_ffn_Wo': 7.428,
     'L1_ffn_gate_w': 5.455,
     'L1_ffn_w1': 8.0,
     'L1_ffn_w2': 8.0}
    for name, (base, spread) in spreads.items():
        noise = np.random.default_rng([zlib.crc32(name.encode()), seed]).standard_normal(out[name].shape)
        drawn = base * np.exp(spread * noise) if base else spread * noise
        out[name] = jnp.asarray(drawn.astype(out[name].dtype))
    for name, factor in factors.items():
        out[name] = (out[name] * factor).astype(out[name].dtype)
    return out
```

```python
from contextlib import ExitStack

import concourse.bass as bass
from concourse import mybir

ALU = mybir.AluOpType
ACT = mybir.ActivationFunctionType
AX = mybir.AxisListType
F32 = mybir.dt.float32
F16 = mybir.dt.float16
BF16 = mybir.dt.bfloat16
U8 = mybir.dt.uint8
U32 = mybir.dt.uint32

P = 128
B, S, D = 4, 256, 128
I = S // P
NT = B * I
BIG = 1e30
EPS = 1e-5

NH0, DH0 = 4, 32
UNITS = B * NH0
W0 = S + P
EPS0 = 1e-6

H1, E1, DH1, TOP = 8, 5, 64, 3
HD1 = H1 * DH1
G1 = H1 * E1
PARTS = ("q", "k", "v")

H2, DH2 = 16, 64
KT = 2 * S // P
HP2 = H2 // 2
INNER = H2 * DH2

E3, FF = 8, 512
FT = FF // P

STAGE = 1280
N_STAGE = 3


def settle(eng, sem):
    eng.sem_inc(sem, 1)


class Names:
    pass


class Chain:

    def __init__(self, eng, sem):
        self.eng, self.sem, self.base, self.k, self.turn, self.per = eng, sem, 0, 0, 0, 0

    def loop(self, turn, per):
        self.base, self.k, self.turn, self.per = self.base + self.k, 0, turn, per

    def end_loop(self, turns):
        assert self.k == self.per, (self.k, self.per)
        self.base, self.k, self.turn, self.per = self.base + turns * self.per, 0, 0, 0

    def link(self, instruction):
        self.k += 1
        instruction.then_inc(self.sem, 1)
        self.eng.wait_ge(self.sem, self.turn * self.per + (self.base + self.k) if self.per else self.base + self.k)


def weight_chunks(m, d):
    out = []
    for c in range(2):
        out.append((d.Wq0[:, c * 1280:(c + 1) * 1280], 1280, m.wq0h[:, c * 1280:(c + 1) * 1280], m.wq0l[:, c * 1280:(c + 1) * 1280]))
    for c in range(4):
        out.append((d.Wkv0[:, c * 1280:(c + 1) * 1280], 1280, m.wkv0h[:, c * 1280:(c + 1) * 1280], m.wkv0l[:, c * 1280:(c + 1) * 1280]))
    for src, hi, lo in ((d.Wv1, m.wv1h, m.wv1l), (d.Wq1, m.wq1h, m.wq1l), (d.Wk1, m.wk1h, m.wk1l)):
        out.append((src, INNER, hi[:, :], lo[:, :]))
    for c in range(E3 // 2):
        out.append((d.w1[2 * c:2 * c + 2, :, :].rearrange("e p n -> p e n"), 2 * FF,
                    m.w1h[:, 2 * c:2 * c + 2, :], m.w1l[:, 2 * c:2 * c + 2, :]))
    for c in range(E3 // 2):
        out.append((d.w2[2 * c:2 * c + 2, :, :].rearrange("e (f p) n -> p (e f) n", p=P), 2 * FT * D,
                    m.w2h[:, 2 * c:2 * c + 2, :, :].rearrange("p e f n -> p (e f) n"),
                    m.w2l[:, 2 * c:2 * c + 2, :, :].rearrange("p e f n -> p (e f) n")))
    return out


N_W0 = 6
N_W1 = 9
N_WALL = 17
DVE_STEPS_B, POOL_STEPS_B, DVE_STEPS_C = 14, 18, 14


def build(nc, x, ctx_in, mask, g_x, g_f, w_i, b_i, w_f, b_f, ln_w, Wq0, Wkv0, Ws, Wd, Wo0,
          gm, bm, gl, bl, Wq1, Wk1, Wv1, Wo1, gate_w, w1, b1, w2, b2, out):
    with ExitStack() as stack:
        m, s, d = Names(), Names(), Names()

        def sb(name, shape, dt=F32):
            return stack.enter_context(nc.sbuf_tensor(name, shape, dt))

        def share(arena, words, *parts):
            area = stack.enter_context(nc.sbuf_tensor(arena, [P, words], F32))
            views = []
            for at, shape, dt in parts:
                n = 1
                for k in shape:
                    n *= k
                used = n if dt == F32 else n // 2
                assert at + used <= words, arena
                v = area[:, at:at + used]
                if dt != F32:
                    v = v.bitcast(dt)
                if len(shape) > 1:
                    names = "abcd"[:len(shape)]
                    v = v.rearrange("p (%s) -> p %s" % (" ".join(names), " ".join(names)), **dict(zip(names, shape)))
                views.append(v)
            return views

        def sem(name):
            return stack.enter_context(nc.semaphore("s_" + name))

        d.Wq0, d.Wkv0, d.Wq1, d.Wk1, d.Wv1, d.w1, d.w2 = Wq0, Wkv0, Wq1, Wk1, Wv1, w1, w2
        bk = [stack.enter_context(nc.psum_tensor(f"bank{i}", [P, 512], F32)) for i in range(8)]

        m.ident = sb("ident", [P, P])
        m.ones = sb("ones", [P, P])
        m.tri = sb("tri", [P, P])
        m.identb = sb("identb", [P, P], BF16)
        m.causal = sb("causal", [P, W0], BF16)
        m.zero16 = sb("zero16", [UNITS, S])
        m.mhalf = sb("mhalf", [P, 16])
        m.iota_i = sb("iota_i", [P, E3], mybir.dt.int32)
        m.iota_f = sb("iota_f", [P, E3])
        m.wi_row = sb("wi_row", [NH0, 3 * D])
        m.wf_row = sb("wf_row", [NH0, 3 * D])
        m.wg = sb("wg", [P, 3, 2 * NH0])
        m.wg_ctx = sb("wg_ctx", [P, 2 * NH0])
        m.bi = sb("bi", [P, NH0])
        m.bf = sb("bf", [P, NH0])
        m.lnw = sb("lnw", [P, D])
        m.gx = sb("gx", [P, 2])
        m.gf = sb("gf", [P, 2])
        m.cols = sb("cols", [P, 4])
        m.mask_u8 = sb("mask_u8", [P, B, S], U8)
        m.maskb = sb("maskb", [P, B, 2 * S], BF16)
        m.maskrow = sb("maskrow", [P, 2 * S], BF16)
        m.wsd = sb("wsd", [P, 2 * G1])
        m.wo0 = sb("wo0", [P, 3, D])
        m.wo1 = sb("wo1", [P, HP2, D])
        m.gate = sb("gate", [P, E3])
        m.b1_row = sb("b1_row", [E3 * FT, P])
        m.b1T = sb("b1T", [P, E3, FT])
        m.b2 = sb("b2", [E3, D])
        m.stage = sb("stage", [P, N_STAGE, STAGE])
        m.wq1h, m.wq1l, m.wk1h, m.wk1l, m.wv1h, m.wv1l = (
            sb(n, [P, INNER], F16) for n in ("wq1h", "wq1l", "wk1h", "wk1l", "wv1h", "wv1l"))
        NQ, NW = H1 * E1 * DH1, E3 * FF // 2
        m.wq0h, m.wq0l, m.wkv0h, m.wkv0l, m.w1h, m.w1l, m.w2h, m.w2l = share("weights", 4 * NW,
              (0, (NQ,), F16), (NQ // 2, (NQ,), F16), (NQ, (2 * NQ,), F16), (2 * NQ, (2 * NQ,), F16),
              (0, (E3, FF), F16), (NW, (E3, FF), F16), (2 * NW, (E3, FT, D), F16), (3 * NW, (E3, FT, D), F16))
        NV = KT * H2 * (DH2 + 1) // 2
        m.prod, m.acc, m.v2h, m.v2l, m.ao, m.hTh, m.hTl, m.hf = share("work", 16 * HD1,
              (0, (2, E1, HD1), F32), (2 * E1 * HD1, (3, I, HD1), F32),
              (0, (KT, H2, DH2 + 1), F16), (NV, (KT, H2, DH2 + 1), F16), (2 * NV, (I, INNER), F32),
              (0, (2, FT, 512), F16), (2048, (2, FT, 512), F16), (4096, (2, 512), F32))
        m.xnT, m.cT, m.vx, m.ho, m.aoT, m.xdTh, m.xdTl = share("work0", 3 * NT * P + NT * NH0,
              (0, (NT, P), F32), (NT * P, (NT, P), F32), (2 * NT * P, (NT, NH0, DH0 + 1), F32),
              (0, (I, HD1), F32), (NT * P, (HP2, P), F32),
              (2 * NT * P, (NT, P), F16), (2 * NT * P + NT * P // 2, (NT, P), F16))
        m.xt = sb("xt", [P, NT, D])
        m.ct = sb("ct", [P, NT, D])
        m.st = sb("st", [P, NT, 6])
        m.mv = sb("mv", [P, NT, 2])
        m.rs = sb("rs", [P, NT])
        m.st2 = sb("st2", [P, NT, 6])
        m.mv2 = sb("mv2", [P, NT, 2])
        m.rs2 = sb("rs2", [P, NT])
        m.kvTh = sb("kvTh", [P, B, 2 * S], F16)
        m.kvTl = sb("kvTl", [P, B, 2 * S], F16)
        m.xbTh = sb("xbTh", [P, NT, P], F16)
        m.xbTl = sb("xbTl", [P, NT, P], F16)
        m.ig, m.fg, m.tmp_a, m.tmp_b, m.logf, m.Ft, m.at, m.mlog, m.en = (
            sb(n, [P, I, B, NH0]) for n in ("ig", "fg", "tmp_a", "tmp_b", "logf", "Ft", "at", "mlog", "en"))
        m.M16 = sb("M16", [UNITS, W0])
        m.Dm = sb("Dm", [P, 2, W0])
        m.C = sb("C", [P, 2, W0])
        m.absc, m.nrm, m.rn, m.s32, m.v32, m.r32 = (
            sb(n, [P, I * NH0]) for n in ("absc", "nrm", "rn", "s32", "v32", "r32"))
        m.hh = sb("hh", [P, I * NH0, DH0])
        m.hc = sb("hc", [P, I * NH0, DH0])
        m.sq = sb("sq", [P, I * NH0, DH0])
        m.sg = sb("sg", [P, I, 2 * G1])
        m.cmp = sb("cmp", [P, I * 2 * H1, E1, E1 - 1], BF16)
        m.cnt = sb("cnt", [P, I * 2 * G1])
        m.topm = sb("topm", [P, NT, 2 * G1])
        m.gatev = sb("gatev", [P, NT, 2 * G1])
        m.qTh = sb("qTh", [P, 4, S], F16)
        m.qTl = sb("qTl", [P, 4, S], F16)
        m.kTh = sb("kTh", [P, 4, S], F16)
        m.kTl = sb("kTl", [P, 4, S], F16)
        m.v1h = sb("v1h", [P, I, H1, DH1 + 1], F16)
        m.v1l = sb("v1l", [P, I, H1, DH1 + 1], F16)
        m.nm = sb("nm", [P, 4, 2])
        m.nmx = sb("nmx", [P, 4, 2])
        m.xn, m.Pr = share("work1", NT * D, (0, (NT, D), F32), (0, (2, 512), F32))
        m.PTh = sb("PTh", [P, 2, 4, P], F16)
        m.PTl = sb("PTl", [P, 2, 4, P], F16)
        m.den = sb("den", [P, 8])
        m.z = sb("z", [P, I, E1 * DH1])
        m.latf = sb("latf", [P, I, P])
        m.zT = sb("zT", [P, 3, P])
        m.xT32 = sb("xT32", [P, I, P])
        m.n2 = sb("n2", [P, I, D])
        m.n3 = sb("n3", [P, I, D])
        m.q2h = sb("q2h", [P, 2, S], F16)
        m.q2l = sb("q2l", [P, 2, S], F16)
        m.k2h = sb("k2h", [P, 2, 2 * S], F16)
        m.k2l = sb("k2l", [P, 2, 2 * S], F16)
        m.sm = sb("sm", [P, 2, 512])
        m.lg = sb("lg", [P, I, E3])
        m.m8 = sb("m8", [P, I, 8])
        m.ix8 = sb("ix8", [P, I, 8], U32)
        m.ixf = sb("ixf", [P, I])
        m.nmax = sb("nmax", [P, I])
        m.ex8 = sb("ex8", [P, I, E3])
        m.sum8 = sb("sum8", [P, I])
        m.wmax = sb("wmax", [P, I])
        m.we1 = sb("we1", [P, I, E3])
        m.we = sb("we", [P, E3, NT])
        m.weT = sb("weT", [E3, NT, P])

        s.x_in = sem("x_in")
        s.ctx_in = sem("ctx_in")
        s.small_in = sem("small_in")
        s.small2_in = sem("small2_in")
        s.w_hi = sem("w_hi")
        s.w_split = sem("w_split")
        s.settled_act = sem("settled_act")
        s.settled_dve = sem("settled_dve")
        s.settled_pool = sem("settled_pool")
        s.const = sem("const")
        s.pool_chain = sem("pool_chain")
        s.dve_chain = sem("dve_chain")
        s.act_chain = sem("act_chain")
        s.out_done = sem("out_done")
        s.x_var = sem("x_var")
        s.x_rstd = sem("x_rstd")
        s.xn_ready = sem("xn_ready")
        s.xT_ready = sem("xT_ready")
        s.cT_ready = sem("cT_ready")
        s.xT_copied = sem("xT_copied")
        s.cT_copied = sem("cT_copied")
        s.wg_T = sem("wg_T")
        s.wg_ready = sem("wg_ready")
        s.gates = sem("gates")
        s.gates_b = sem("gates_b")
        s.softplus = sem("softplus")
        s.logf_ready = sem("logf_ready")
        s.F_ready = sem("F_ready")
        s.a_ready = sem("a_ready")
        s.aT_ready = sem("aT_ready")
        s.M_ready = sem("M_ready")
        s.Mt_ready = sem("Mt_ready")
        s.mlog_ready = sem("mlog_ready")
        s.en_ready = sem("en_ready")
        s.L_ready = sem("L_ready")
        s.S0_ready = sem("S0_ready")
        s.D_ready = sem("D_ready")
        s.C_ready = sem("C_ready")
        s.C_free = sem("C_free")
        s.absc_ready = sem("absc_ready")
        s.O0_free = sem("O0_free")
        s.var0 = sem("var0")
        s.rstd0 = sem("rstd0")
        s.vx_ready = sem("vx_ready")
        s.tanh_ready = sem("tanh_ready")
        s.cn_T = sem("cn_T")
        s.kv_f = sem("kv_f")
        s.kv_free = sem("kv_free")
        s.maskb_ready = sem("maskb_ready")
        s.maskrow_ready = sem("maskrow_ready")
        s.x1_var = sem("x1_var")
        s.x1_rstd = sem("x1_rstd")
        s.x1n_ready = sem("x1n_ready")
        s.x1T_ready = sem("x1T_ready")
        s.x1T_f32 = sem("x1T_f32")
        s.x1T_hi = sem("x1T_hi")
        s.x1T_lo = sem("x1T_lo")
        s.g1_ready = sem("g1_ready")
        s.g1_exp = sem("g1_exp")
        s.gate_ready = sem("gate_ready")
        s.b1T_ready = sem("b1T_ready")
        s.b1T_copied = sem("b1T_copied")
        s.pj_ready = sem("pj_ready")
        s.prod_ready = sem("prod_ready")
        s.prod_free = sem("prod_free")
        s.acc_ready = sem("acc_ready")
        s.pair_ready = sem("pair_ready")
        s.T_ready = sem("T_ready")
        s.T_hi = sem("T_hi")
        s.T_free = sem("T_free")
        s.v1hi_ready = sem("v1hi_ready")
        s.v1lo_ready = sem("v1lo_ready")
        s.S_ready = sem("S_ready")
        s.exp_done = sem("exp_done")
        s.nm_ready = sem("nm_ready")
        s.wo_ready = sem("wo_ready")
        s.O_ready = sem("O_ready")
        s.O_free = sem("O_free")
        s.z_ready = sem("z_ready")
        s.z_sum = sem("z_sum")
        s.zT_copied = sem("zT_copied")
        s.x2_var = sem("x2_var")
        s.x2_rstd = sem("x2_rstd")
        s.x2n_ready = sem("x2n_ready")
        s.lat_ready = sem("lat_ready")
        s.lat_hi = sem("lat_hi")
        s.c_pj_ready = sem("c_pj_ready")
        s.c_pj_hi = sem("c_pj_hi")
        s.c_pj_free = sem("c_pj_free")
        s.c_S_ready = sem("c_S_ready")
        s.c_max_done = sem("c_max_done")
        s.c_exp_done = sem("c_exp_done")
        s.c_T_ready = sem("c_T_ready")
        s.c_T_hi = sem("c_T_hi")
        s.c_T_free = sem("c_T_free")
        s.c_O_ready = sem("c_O_ready")
        s.c_O_free = sem("c_O_free")
        s.v2_ones = sem("v2_ones")
        s.c_wo_ready = sem("c_wo_ready")
        s.x3_var = sem("x3_var")
        s.x3_rstd = sem("x3_rstd")
        s.x3n_ready = sem("x3n_ready")
        s.xd_f32 = sem("xd_f32")
        s.xd_hi = sem("xd_hi")
        s.rt_ready = sem("rt_ready")
        s.rt_nmax = sem("rt_nmax")
        s.rt_exp = sem("rt_exp")
        s.we_ready = sem("we_ready")
        s.h_ready = sem("h_ready")
        s.gelu_done = sem("gelu_done")
        s.h_hi = sem("h_hi")
        s.h_lo = sem("h_lo")
        s.y_ready = sem("y_ready")
        s.y_free = sem("y_free")
        s.out_ready = sem("out_ready")

        stage_in = [stack.enter_context(nc.semaphore(f"s_stage_in{n}")) for n in range(N_STAGE)]
        N_SMALL, N_SMALL2 = 9, 4 + 1 + E1 + 4
        block = stack.enter_context(nc.Block())
        chunks = weight_chunks(m, d)
        xf = x.rearrange("b (i p) c -> p (b i) c", p=P)
        cf = ctx_in.rearrange("b (i p) c -> p (b i) c", p=P)
        outf = out.rearrange("b (i p) c -> p (b i) c", p=P)

        RING = 2
        T1, O1, X1 = 4 + H1 + 2 * I, H1 // 2 + I, len(PARTS) * I * E1
        STEPS = H1 + 2
        bank_pj, bank_S, bank_T, bank_O = bk[0:2], bk[2:4], bk[4:6], bk[6:8]
        wq0 = [w.rearrange("p (h e c) -> p h e c", h=H1, e=E1) for w in (m.wq0h, m.wq0l)]
        wkv0 = [w.rearrange("p (a h e c) -> p a h e c", a=2, h=H1, e=E1) for w in (m.wkv0h, m.wkv0l)]

        def chunk(c):
            return c // (I * E1), c // E1 % I, c % E1

        def chunks_of(step):
            a = 3 * step
            return [a], [a + 1, a + 2]

        def heads8(a):
            return a.rearrange("p (h c) -> p h c", h=H1)

        def wide(a, n):
            return a.unsqueeze(2).to_broadcast([P, a.shape[1], n])

        def pe_b(pe, turn):
            pe.sem_inc(s.O_ready, RING)
            pe.wait_ge(s.kv_f, B)
            pe.wait_ge(s.b1T_copied, 1)
            pe.wait_ge(s.O0_free, B)
            pe.wait_ge(s.x1T_lo, B)
            pe.wait_ge(s.g1_exp, B)

            def project(b, c):
                part, i, e = chunk(c)
                if c >= 2 or not isinstance(b, int) or b > 0:
                    pe.wait_ge(s.prod_ready, b * X1 + (c - 1))
                wh, wl = (w[:, :, e, :] for w in wq0) if part == 0 else (w[:, part - 1, :, e, :] for w in wkv0)
                o = heads8(bank_pj[c % 2][:, :])
                xh, xl = m.xbTh[:, b * I + i, :], m.xbTl[:, b * I + i, :]
                pe.matmul(o, xh, wh, start=True, stop=False)
                pe.matmul(o, xh, wl, start=False, stop=False)
                pe.matmul(o, xl, wh, start=False, stop=True).then_inc(s.pj_ready, 1)

            def take_T(b, k):
                pe.wait_ge(s.T_free, b * T1 + (k + 1))
                return bank_T[k % 2]

            def attend(b, more):
                for k in range(4):
                    pe.wait_ge(s.acc_ready, b * 6 + (k + 1))
                    bank = take_T(b, k)
                    for hp in range(4):
                        ins = turn(bank[:, hp * P:(hp + 1) * P], m.acc[:, k // I, k % I, hp * P:(hp + 1) * P])
                    ins.then_inc(s.T_ready, 1)
                for h in range(STEPS):
                    before, after = chunks_of(h)
                    if h < H1:
                        if h == 0:
                            pe.wait_ge(s.T_free, b * T1 + (4 + RING))
                        pe.wait_ge(s.exp_done, b * H1 + (h + 1))
                        r = slice(DH1 * (h % 2), DH1 * (h % 2) + DH1)
                        for i in range(I):
                            o = bank_S[h % 2][:, i * S:(i + 1) * S]
                            qh, ql = (q[r, h // 2, i * P:(i + 1) * P] for q in (m.qTh, m.qTl))
                            kh, kl = (k[r, h // 2, :] for k in (m.kTh, m.kTl))
                            pe.matmul(o, qh, kh, start=True, stop=False)
                            pe.matmul(o, qh, kl, start=False, stop=False)
                            ins = pe.matmul(o, ql, kh, start=False, stop=True)
                        ins.then_inc(s.S_ready, 1)
                    if more:
                        for c in before:
                            project(b + 1, c)
                    if 1 <= h <= H1:
                        g = h - 1
                        pe.wait_ge(s.exp_done, b * H1 + (g + 1 + RING))
                        bank = take_T(b, 4 + g)
                        for i in range(I):
                            for j in range(I):
                                ins = turn(bank[:, (j * I + i) * P:(j * I + i + 1) * P], m.Pr[:, g % 2, i * S + j * P:i * S + (j + 1) * P])
                        ins.then_inc(s.T_ready, 1)
                    if more:
                        for c in after:
                            project(b + 1, c)
                    if h >= 2:
                        g = h - 2
                        pe.wait_ge(s.T_free, b * T1 + (4 + g + 1 + RING))
                        if g == 0:
                            pe.wait_ge(s.v1lo_ready, b * I + I)
                        if g % 2 == 0:
                            pe.wait_ge(s.O_free, b * O1 + (g // 2 + 1))
                        for i in range(I):
                            col = (g % 2 * I + i) * (DH1 + 1)
                            o = bank_O[g // 2 % 2][:, col:col + DH1 + 1]
                            for j in range(I):
                                ph, pl = (p[:, g % 2, j * I + i, :] for p in (m.PTh, m.PTl))
                                vh, vl = (v[:, j, g, :] for v in (m.v1h, m.v1l))
                                pe.matmul(o, ph, vh, start=(j == 0), stop=False)
                                pe.matmul(o, ph, vl, start=False, stop=False)
                                ins = pe.matmul(o, pl, vh, start=False, stop=(j == I - 1))
                        ins.then_inc(s.O_ready, 1)
                for i in range(I):
                    pe.wait_ge(s.z_sum, b * I + (i + 1))
                    bank = take_T(b, 4 + H1 + i)
                    for c in range(3):
                        w = min(P, E1 * DH1 - c * P)
                        ins = turn(bank[0:w, c * P:(c + 1) * P], m.z[:, i, c * P:c * P + w])
                    ins.then_inc(s.T_ready, 1)
                    pe.wait_ge(s.zT_copied, b * I + (i + 1))
                    pe.wait_ge(s.O_free, b * O1 + (H1 // 2 + i + 1))
                    for c in range(3):
                        w = min(P, E1 * DH1 - c * P)
                        ins = pe.matmul(bank_O[i][:, 0:D], m.zT[0:w, c, :], m.wo0[0:w, c, :], start=(c == 0), stop=(c == 2))
                    ins.then_inc(s.wo_ready, 1)
                for i in range(I):
                    pe.wait_ge(s.x2n_ready, 2 * b + 2)
                    bank = take_T(b, 4 + H1 + I + i)
                    turn(bank[:, 0:P], m.n3[:, i, :]).then_inc(s.T_ready, 1)

            for n in range(N_W0):
                pe.wait_ge(s.w_split, n + 1)
            for c in range(X1):
                project(0, c)
            with pe.Fori(0, B - 1) as b:
                attend(b, True)
            attend(B - 1, False)

        def act_b(act):
            act.sem_inc(s.exp_done, RING)

            def attend(b):
                for k in range(4):
                    act.wait_ge(s.T_ready, b * T1 + (k + 1))
                    dst = (m.qTh, m.kTh)[k // I][:, :, (k % I) * P:(k % I + 1) * P]
                    act.activation(dst, bank_T[k % 2][:, :].rearrange("p (h c) -> p h c", h=4), ACT.Copy).then_inc(s.T_hi, 1)
                for i in range(I):
                    act.wait_ge(s.acc_ready, b * 6 + (4 + i + 1))
                    act.activation(m.v1h[:, i, :, 0:DH1], heads8(m.acc[:, 2, i, :]), ACT.Copy).then_inc(s.v1hi_ready, 1)
                for h in range(H1 + 1):
                    if h < H1:
                        act.wait_ge(s.nm_ready, b * H1 + (h + 1))
                        act.wait_ge(s.T_ready, b * T1 + (4 + h - 1))
                        for i in range(I):
                            ins = act.activation(m.Pr[:, h % 2, i * S:(i + 1) * S], bank_S[h % 2][:, i * S:(i + 1) * S], ACT.Exp,
                                                 scale=DH1 ** -0.5, bias=m.nmx[:, h % 4, i:i + 1])
                        ins.then_inc(s.exp_done, 1)
                    if h >= 1:
                        g = h - 1
                        act.wait_ge(s.T_ready, b * T1 + (4 + g + 1))
                        act.wait_ge(s.O_ready, b * H1 + (g + 1))
                        act.activation(m.PTh[:, g % 2, :, :].rearrange("p n c -> p (n c)"), bank_T[g % 2][:, :], ACT.Copy).then_inc(s.T_hi, 1)
                for i in range(I):
                    act.wait_ge(s.lat_ready, b * I + (i + 1))
                    act.activation(m.kvTh[:, b, S + i * P:S + (i + 1) * P], m.latf[:, i, :], ACT.Copy).then_inc(s.lat_hi, 1)

            with act.Fori(0, B - 1) as b:
                attend(b)
            attend(B - 1)

        def dve_b(dve, ch, stats):
            dve.sem_inc(s.T_free, RING)
            dve.sem_inc(s.O_free, RING)
            dve.wait_ge(s.gate_ready, B)

            def gate_products(b, c, group):
                part, i, e = chunk(c)
                sel = G1 if part == 0 else 0
                dve.wait_ge(s.pj_ready, b * X1 + (c + 1))
                if e == 0 and (group >= 2 if isinstance(group, int) else True):
                    dve.wait_ge(s.prod_free, group + (-1))
                k = c // E1 % 2
                g = m.gatev[:, b * I + i, sel:sel + G1].rearrange("p (h e) -> p h e", h=H1)[:, :, e]
                dve.tensor_tensor(heads8(m.prod[:, k, e, :]), heads8(bank_pj[c % 2][:, :]), wide(g, DH1), ALU.mult).then_inc(s.prod_ready, 1)
                if e == E1 - 1:
                    dve.wait_ge(s.prod_ready, b * X1 + (c + 1))
                    dve.tensor_tensor(m.prod[:, k, 3, :], m.prod[:, k, 3, :], m.prod[:, k, 4, :], ALU.add).then_inc(s.pair_ready, 1)

            def attend(b, more):
                for k in range(4):
                    dve.wait_ge(s.T_hi, b * (4 + H1) + (k + 1))
                    hi, lo = ((m.qTh, m.qTl), (m.kTh, m.kTl))[k // I]
                    r = slice((k % I) * P, (k % I + 1) * P)
                    dve.tensor_tensor(lo[:, :, r], bank_T[k % 2][:, :].rearrange("p (h c) -> p h c", h=4), hi[:, :, r], ALU.subtract).then_inc(s.T_free, 1)
                for i in range(I):
                    dve.wait_ge(s.v1hi_ready, b * I + (i + 1))
                    dve.tensor_tensor(m.v1l[:, i, :, 0:DH1], heads8(m.acc[:, 2, i, :]), m.v1h[:, i, :, 0:DH1], ALU.subtract).then_inc(s.v1lo_ready, 1)
                for h in range(STEPS):
                    before, after = chunks_of(h)
                    if h < H1:
                        dve.wait_ge(s.S_ready, b * H1 + (h + 1))
                        ch.link(dve.tensor_reduce(m.nm[:, h % 4, :], bank_S[h % 2][:, :].rearrange("p (i c) -> p i c", i=I), AX.X, ALU.max, negate=True))
                        dve.tensor_scalar(m.nmx[:, h % 4, :], m.nm[:, h % 4, :], DH1 ** -0.5, None, ALU.mult).then_inc(s.nm_ready, 1)
                    if more:
                        for c in before:
                            gate_products(b + 1, c, 6 + b * 8 + c // E1)
                    if 1 <= h <= H1:
                        g = h - 1
                        dve.wait_ge(s.T_hi, b * (4 + H1) + (4 + g + 1))
                        dve.tensor_tensor(m.PTl[:, g % 2, :, :].rearrange("p n c -> p (n c)"), bank_T[g % 2][:, :],
                                          m.PTh[:, g % 2, :, :].rearrange("p n c -> p (n c)"), ALU.subtract).then_inc(s.T_free, 1)
                    if more:
                        for c in after:
                            gate_products(b + 1, c, 6 + b * 8 + c // E1)
                    if h >= 3 and h % 2 == 1:
                        o = (h - 3) // 2
                        dve.wait_ge(s.O_ready, b * H1 + (2 * o + 2 + RING))
                        O = bank_O[o % 2][:, 0:4 * (DH1 + 1)].rearrange("p (h i c) -> p h i c", h=2, i=I)
                        den = m.den[:, 4 * (o % 2):4 * (o % 2) + 4]
                        ch.link(dve.reciprocal(den.rearrange("p (h i) -> p h i", h=2), O[:, :, :, DH1]))
                        dst = m.ho[:, :, 2 * o * DH1:(2 * o + 2) * DH1].rearrange("p i (h c) -> p h i c", h=2)
                        for hh in range(2):
                            ins = dve.tensor_tensor(dst[:, hh, :, :], O[:, hh, :, 0:DH1], wide(den[:, 2 * hh:2 * hh + 2], DH1), ALU.mult)
                        ins.then_inc(s.O_free, 1)
                dve.wait_ge(s.O_free, b * O1 + (H1 // 2 + RING))
                for i in range(I):
                    z_group = 6 + b * 8 + (6 if more else 0) + i
                    dve.wait_ge(s.prod_free, z_group + (-1))
                    md = m.topm[:, b * I + i, G1:2 * G1].rearrange("p (h e) -> p h e", h=H1)
                    for e in range(E1):
                        ins = dve.tensor_tensor(heads8(m.prod[:, i, e, :]), heads8(m.ho[:, i, :]), wide(md[:, :, e], DH1), ALU.mult)
                    ins.then_inc(s.z_ready, 1)
                for i in range(I):
                    dve.wait_ge(s.T_ready, b * T1 + (4 + H1 + i + 1))
                    if i > 0:
                        dve.wait_ge(s.wo_ready, b * I + i)
                    dve.tensor_copy(m.zT[:, 0:2, :].rearrange("p n c -> p (n c)"), bank_T[i][:, 0:2 * P])
                    dve.tensor_copy(m.zT[0:DH1, 2, :], bank_T[i][0:DH1, 2 * P:3 * P]).then_inc(s.T_free, 1)
                    dve.wait_ge(s.T_free, b * T1 + (4 + H1 + i + 1 + RING))
                    dve.sem_inc(s.zT_copied, 1)
                    dve.wait_ge(s.wo_ready, b * I + (i + 1))
                    xi = m.xt[:, b * I + i, :]
                    dve.scalar_tensor_tensor(xi, bank_O[i][:, 0:D], m.gf[:, 0:1], xi, ALU.mult, ALU.add).then_inc(s.O_free, 1)
                dve.wait_ge(s.O_free, b * O1 + (O1 + RING))
                stats(lambda i: m.xt[:, b * I + i, :], I, m.st, m.mv, s.x2_var)
                dve.wait_ge(s.x2_rstd, 2 * b + 1)
                for i in range(I):
                    ins = dve.tensor_scalar(m.n2[:, i, :], m.xt[:, b * I + i, :], m.mv[:, i, 0:1], m.rs[:, i:i + 1], ALU.subtract, ALU.mult)
                ins.then_inc(s.x2n_ready, 1)
                dve.wait_ge(s.x2n_ready, 2 * b + 1)
                stats(lambda i: m.n2[:, i, :], I, m.st, m.mv, s.x2_var)
                dve.wait_ge(s.x2_rstd, 2 * b + 2)
                for i in range(I):
                    ins = dve.tensor_scalar(m.n3[:, i, :], m.n2[:, i, :], m.mv[:, i, 0:1], m.rs[:, i:i + 1], ALU.subtract, ALU.mult)
                ins.then_inc(s.x2n_ready, 1)
                for i in range(I):
                    dve.wait_ge(s.T_ready, b * T1 + (4 + H1 + I + i + 1))
                    dve.tensor_scalar(m.latf[:, i, :], bank_T[i][:, 0:P], m.cols[:, 2:3], m.cols[:, 3:4], ALU.mult, ALU.add).then_inc(s.lat_ready, 1)
                for i in range(I):
                    dve.wait_ge(s.lat_hi, b * I + (i + 1))
                    r = slice(S + i * P, S + (i + 1) * P)
                    dve.tensor_tensor(m.kvTl[:, b, r], m.latf[:, i, :], m.kvTh[:, b, r], ALU.subtract).then_inc(s.T_free, 1)

            dve.wait_ge(s.small2_in, 16 * N_SMALL2)
            for c in range(X1):
                gate_products(0, c, c // E1)
            with dve.Fori(0, B - 1) as b:
                ch.loop(b, DVE_STEPS_B)
                attend(b, True)
            ch.end_loop(B - 1)
            attend(B - 1, False)

        def pool_b(pool, ch, rstd, split):
            def sums(b, k, group):
                kk = k % 2
                pr, acc = m.prod[:, kk, :, :], m.acc[:, k // I, k % I, :]
                pool.wait_ge(s.prod_ready, b * X1 + (k * E1 + 2))
                if not (isinstance(b, int) and b == 0):
                    if k < 4:
                        pool.wait_ge(s.T_ready, (b + (-1)) * T1 + (k + 1))
                    else:
                        pool.wait_ge(s.v1lo_ready, (b + (-1)) * I + (k - 4 + 1))
                ch.link(pool.tensor_tensor(acc, pr[:, 0, :], pr[:, 1, :], ALU.add))
                pool.wait_ge(s.prod_ready, b * X1 + (k * E1 + 3))
                ch.link(pool.tensor_tensor(acc, acc, pr[:, 2, :], ALU.add))
                pool.wait_ge(s.pair_ready, b * 6 + (k + 1))
                pool.tensor_tensor(acc, acc, pr[:, 3, :], ALU.add).then_inc(s.acc_ready, 1)
                pool.wait_ge(s.acc_ready, b * 6 + (k + 1))
                pool.sem_inc(s.prod_free, 1)

            def attend(b, more):
                if more:
                    for k in range(6):
                        sums(b + 1, k, None)
                for i in range(I):
                    pool.wait_ge(s.z_ready, b * I + (i + 1))
                    t = m.prod[:, i, :, :].rearrange("p e (h c) -> p e h c", h=H1)
                    ch.link(pool.tensor_tensor(t[:, :, 0:4, :], t[:, :, 0:4, :], t[:, :, 4:8, :], ALU.add))
                    ch.link(pool.tensor_tensor(t[:, :, 0:2, :], t[:, :, 0:2, :], t[:, :, 2:4, :], ALU.add))
                    pool.tensor_tensor(m.z[:, i, :].rearrange("p (e c) -> p e c", e=E1), t[:, :, 0, :], t[:, :, 1, :], ALU.add).then_inc(s.z_sum, 1)
                    pool.wait_ge(s.z_sum, b * I + (i + 1))
                    pool.sem_inc(s.prod_free, 1)
                for k in range(2):
                    rstd(2 * b + (k + 1), m.mv[:, 0:I, 1], m.rs[:, 0:I], s.x2_var, s.x2_rstd)

            for k in range(6):
                sums(0, k, None)
            with pool.Fori(0, B - 1) as b:
                ch.loop(b, POOL_STEPS_B)
                attend(b, True)
            ch.end_loop(B - 1)
            for n in range(N_W0, N_W1):
                split(n)
            attend(B - 1, False)

        UN = H2 * I
        TC, OC, PJ = UN + 4 + 2 * I, HP2 + 2 * I, 2 * KT + 2 * HP2
        heads2 = lambda a: a.rearrange("p (h c) -> p h c", h=H2 // 2)

        def pe_c(pe, turn):
            pe.sem_inc(s.c_T_ready, RING)
            pe.sem_inc(s.c_O_ready, RING)
            pe.wait_ge(s.T_free, B * T1 + RING)
            pe.wait_ge(s.O_free, B * O1 + RING)
            for n in range(N_W0, N_W1):
                pe.wait_ge(s.w_split, n + 1)
            pe.wait_ge(s.kv_free, B)

            def three(o, ah, al, bh, bl):
                pe.matmul(o, ah, bh, start=True, stop=False)
                pe.matmul(o, ah, bl, start=False, stop=False)
                return pe.matmul(o, al, bh, start=False, stop=True)

            def take_T(b, k):
                pe.wait_ge(s.c_T_free, b * TC + (k + 1))
                return bank_T[k % 2]

            def project_v(b, k):
                j, half = k // 2, k % 2
                pe.wait_ge(s.c_pj_free, b * PJ + (k + 1))
                r, w = slice(j * P, (j + 1) * P), slice(half * 512, (half + 1) * 512)
                three(bank_pj[k % 2][:, :], m.kvTh[:, b, r], m.kvTl[:, b, r], m.wv1h[:, w], m.wv1l[:, w]).then_inc(s.c_pj_ready, 1)

            def project_qk(b, hp, k):
                n = 2 * KT + 2 * hp + k
                pe.wait_ge(s.c_pj_free, b * PJ + (n + 1))
                w = slice(hp * P, (hp + 1) * P)
                wh, wl = (m.wq1h, m.wq1l) if k == 0 else (m.wk1h, m.wk1l)
                cols = slice(S, 2 * S) if k == 0 else slice(0, 2 * S)
                o = bank_pj[k][:, 0:S] if k == 0 else bank_pj[k][:, :]
                three(o, wh[:, w], wl[:, w], m.kvTh[:, b, cols], m.kvTl[:, b, cols]).then_inc(s.c_pj_ready, 1)

            with pe.Fori(0, B) as b:
                for k in range(2 * KT):
                    project_v(b, k)
                for k in range(2):
                    project_qk(b, 0, k)
                for t in range(UN + 2):
                    if t < UN:
                        hp, hh, i = t // 4, t // 2 % 2, t % 2
                        if t % 4 == 0:
                            pe.wait_ge(s.c_pj_free, b * PJ + (2 * KT + 2 * hp + 2 + RING))
                        pe.wait_ge(s.c_max_done, b * UN + (t + 1))
                        r, q = slice(DH2 * hh, DH2 * hh + DH2), slice(i * P, (i + 1) * P)
                        three(bank_S[t % 2][:, :], m.q2h[r, hp % 2, q], m.q2l[r, hp % 2, q], m.k2h[r, hp % 2, :], m.k2l[r, hp % 2, :])\
                            .then_inc(s.c_S_ready, 1)
                    if t % 4 in (1, 2) and t // 4 + 1 < HP2:
                        project_qk(b, t // 4 + 1, t % 4 - 1)
                    if 1 <= t <= UN:
                        u = t - 1
                        pe.wait_ge(s.c_exp_done, b * UN + (u + 1 + RING))
                        bank = take_T(b, u)
                        for j in range(KT):
                            ins = turn(bank[:, j * P:(j + 1) * P], m.Pr[:, u % 2, j * P:(j + 1) * P])
                        ins.then_inc(s.c_T_ready, 1)
                    if t >= 2:
                        u = t - 2
                        hp, hh, i = u // 4, u // 2 % 2, u % 2
                        pe.wait_ge(s.c_T_free, b * TC + (u + 1 + RING))
                        if u % 4 == 0:
                            pe.wait_ge(s.c_O_free, b * OC + (hp + 1))
                        o = bank_O[hp % 2][:, (u % 4) * (DH2 + 1):(u % 4 + 1) * (DH2 + 1)]
                        for j in range(KT):
                            ph, pl = (p[:, u % 2, j, :] for p in (m.PTh, m.PTl))
                            vh, vl = (v[:, j, u // 2, :] for v in (m.v2h, m.v2l))
                            pe.matmul(o, ph, vh, start=(j == 0), stop=False)
                            pe.matmul(o, ph, vl, start=False, stop=False)
                            ins = pe.matmul(o, pl, vh, start=False, stop=(j == KT - 1))
                        ins.then_inc(s.c_O_ready, 1)
                pe.wait_ge(s.c_O_free, b * OC + (HP2 + RING))
                for i in range(I):
                    for half in range(2):
                        bank = take_T(b, UN + 2 * i + half)
                        for j in range(4):
                            c = 4 * half + j
                            ins = turn(bank[:, j * P:(j + 1) * P], m.ao[:, i, c * P:(c + 1) * P])
                        ins.then_inc(s.c_T_ready, 1)
                    pe.wait_ge(s.c_T_free, b * TC + (UN + 2 * i + 2 + RING))
                    pe.wait_ge(s.c_O_free, b * OC + (HP2 + i + 1))
                    for c in range(HP2):
                        ins = pe.matmul(bank_O[i][:, 0:D], m.aoT[:, c, :], m.wo1[:, c, :], start=(c == 0), stop=(c == HP2 - 1))
                    ins.then_inc(s.c_wo_ready, 1)
                pe.wait_ge(s.x3n_ready, b + 1)
                for i in range(I):
                    bank = take_T(b, UN + 4 + i)
                    turn(bank[:, 0:P], m.n2[:, i, :]).then_inc(s.c_T_ready, 1)
                for i in range(I):
                    pe.wait_ge(s.xd_f32, b * I + (i + 1))
                    pe.wait_ge(s.c_O_free, b * OC + (HP2 + I + i + 1))
                    pe.matmul(bank_O[i][:, 0:E3], m.xT32[:, i, :], m.gate[:, :], start=True, stop=True).then_inc(s.rt_ready, 1)
                for i in range(I):
                    pe.wait_ge(s.we_ready, b * I + (i + 1))
                    bank = take_T(b, UN + 4 + I + i)
                    turn(bank[0:E3, 0:P], m.we1[:, i, :]).then_inc(s.c_T_ready, 1)

        def act_c(act):
            act.sem_inc(s.c_exp_done, RING)

            def high(b, n, dst, src):
                act.wait_ge(s.c_pj_ready, b * PJ + (n + 1))
                act.activation(dst, src, ACT.Copy).then_inc(s.c_pj_hi, 1)

            def high_qk(b, hp, k):
                dst, w = ((m.q2h, S), (m.k2h, 2 * S))[k]
                high(b, 2 * KT + 2 * hp + k, dst[:, hp % 2, :], bank_pj[k][:, 0:w])

            with act.Fori(0, B) as b:
                for k in range(2 * KT):
                    half = k % 2
                    high(b, k, m.v2h[:, k // 2, half * 8:half * 8 + 8, 0:DH2], heads2(bank_pj[k % 2][:, :]))
                for k in range(2):
                    high_qk(b, 0, k)
                for t in range(UN + 1):
                    if t < UN:
                        act.wait_ge(s.c_max_done, b * UN + (t + 1 + RING))
                        act.wait_ge(s.c_T_ready, b * TC + (t + 1))
                        act.activation(m.Pr[:, t % 2, :], m.sm[:, t % 2, :], ACT.Exp, scale=-1.0, bias=m.nm[:, t % 4, 0:1]).then_inc(s.c_exp_done, 1)
                    if t % 4 in (1, 2) and t // 4 + 1 < HP2:
                        high_qk(b, t // 4 + 1, t % 4 - 1)
                    if t >= 1:
                        u = t - 1
                        act.wait_ge(s.c_T_ready, b * TC + (u + 1 + RING))
                        act.wait_ge(s.c_O_ready, b * UN + (u + 1))
                        act.activation(m.PTh[:, u % 2, :, :].rearrange("p n c -> p (n c)"), bank_T[u % 2][:, :], ACT.Copy).then_inc(s.c_T_hi, 1)
                for i in range(I):
                    act.wait_ge(s.c_T_ready, b * TC + (UN + 4 + i + 1 + RING))
                    act.activation(m.xT32[:, i, :], bank_T[i][:, 0:P], ACT.Copy).then_inc(s.xd_f32, 1)
                    act.activation(m.xdTh[:, b * I + i, :], bank_T[i][:, 0:P], ACT.Copy).then_inc(s.xd_hi, 1)
                for i in range(I):
                    act.wait_ge(s.rt_nmax, b * I + (i + 1))
                    act.activation(m.ex8[:, i, :], m.lg[:, i, :], ACT.Exp, bias=m.nmax[:, i:i + 1], accum_out=m.sum8[:, i:i + 1]).then_inc(s.rt_exp, 1)

        def dve_c(dve, ch, stats):
            dve.sem_inc(s.c_pj_free, RING)
            dve.sem_inc(s.c_max_done, RING)
            dve.sem_inc(s.c_T_free, RING)
            dve.sem_inc(s.c_O_free, RING)
            dve.wait_ge(s.maskb_ready, 1)
            dve.wait_ge(s.v2_ones, 1)
            dve.wait_ge(s.tanh_ready, 1)

            def low(b, n, dst, src, hi):
                dve.wait_ge(s.c_pj_hi, b * PJ + (n + 1))
                dve.tensor_tensor(dst, src, hi, ALU.subtract).then_inc(s.c_pj_free, 1)

            def low_qk(b, hp, k):
                hi, lo, w = ((m.q2h, m.q2l, S), (m.k2h, m.k2l, 2 * S))[k]
                low(b, 2 * KT + 2 * hp + k, lo[:, hp % 2, :], bank_pj[k][:, 0:w], hi[:, hp % 2, :])

            with dve.Fori(0, B) as b:
                ch.loop(b, DVE_STEPS_C)
                dve.tensor_copy(m.maskrow[:, :], m.maskb[:, b, :]).then_inc(s.maskrow_ready, 1)
                for k in range(2 * KT):
                    v = (slice(None), k // 2, slice(k % 2 * 8, k % 2 * 8 + 8), slice(0, DH2))
                    low(b, k, m.v2l[v], heads2(bank_pj[k % 2][:, :]), m.v2h[v])
                for k in range(2):
                    low_qk(b, 0, k)
                dve.wait_ge(s.maskrow_ready, b + 1)
                for t in range(UN + 2):
                    if t < UN:
                        dve.wait_ge(s.c_S_ready, b * UN + (t + 1))
                        dve.wait_ge(s.c_exp_done, b * UN + (t + 1))
                        settle(dve, s.settled_dve)
                        dve.tensor_tensor_reduce(m.sm[:, t % 2, :], bank_S[t % 2][:, :], m.maskrow[:, :], -(DH2 ** -0.5), 3e38,
                                                 ALU.add, ALU.min, m.nm[:, t % 4, 0:1]).then_inc(s.c_max_done, 1)
                    if t % 4 in (1, 2) and t // 4 + 1 < HP2:
                        low_qk(b, t // 4 + 1, t % 4 - 1)
                    if 1 <= t <= UN:
                        u = t - 1
                        dve.wait_ge(s.c_T_hi, b * UN + (u + 1))
                        dve.tensor_tensor(m.PTl[:, u % 2, :, :].rearrange("p n c -> p (n c)"), bank_T[u % 2][:, :],
                                          m.PTh[:, u % 2, :, :].rearrange("p n c -> p (n c)"), ALU.subtract).then_inc(s.c_T_free, 1)
                    if t >= 5 and t % 4 == 1:
                        hp = (t - 5) // 4
                        dve.wait_ge(s.c_O_ready, b * UN + (4 * hp + 4 + RING))
                        O = bank_O[hp % 2][:, 0:4 * (DH2 + 1)].rearrange("p (h i c) -> p h i c", h=2, i=I)
                        den = m.den[:, 4 * (hp % 2):4 * (hp % 2) + 4]
                        ch.link(dve.reciprocal(den.rearrange("p (h i) -> p h i", h=2), O[:, :, :, DH2]))
                        dst = m.ao[:, :, hp * P:(hp + 1) * P].rearrange("p i (h c) -> p h i c", h=2)
                        for hh in range(2):
                            ins = dve.tensor_tensor(dst[:, hh, :, :], O[:, hh, :, 0:DH2], wide(den[:, 2 * hh:2 * hh + 2], DH2), ALU.mult)
                        ins.then_inc(s.c_O_free, 1)
                for i in range(I):
                    if i > 0:
                        dve.wait_ge(s.c_wo_ready, b * I + i)
                    for half in range(2):
                        dve.wait_ge(s.c_T_ready, b * TC + (UN + 2 * i + half + 1 + RING))
                        dve.tensor_copy(m.aoT[:, 4 * half:4 * half + 4, :].rearrange("p n c -> p (n c)"), bank_T[half][:, :]).then_inc(s.c_T_free, 1)
                    dve.wait_ge(s.c_wo_ready, b * I + (i + 1))
                    xi = m.xt[:, b * I + i, :]
                    dve.scalar_tensor_tensor(xi, bank_O[i][:, 0:D], m.gx[:, 1:2], xi, ALU.mult, ALU.add).then_inc(s.c_O_free, 1)
                dve.wait_ge(s.c_O_free, b * OC + (HP2 + I + RING))
                stats(lambda i: m.xt[:, b * I + i, :], I, m.st, m.mv, s.x3_var)
                dve.wait_ge(s.x3_rstd, b + 1)
                for i in range(I):
                    ins = dve.tensor_scalar(m.n2[:, i, :], m.xt[:, b * I + i, :], m.mv[:, i, 0:1], m.rs[:, i:i + 1], ALU.subtract, ALU.mult)
                ins.then_inc(s.x3n_ready, 1)
                for i in range(I):
                    dve.wait_ge(s.xd_hi, b * I + (i + 1))
                    dve.tensor_tensor(m.xdTl[:, b * I + i, :], bank_T[i][:, 0:P], m.xdTh[:, b * I + i, :], ALU.subtract).then_inc(s.c_T_free, 1)
                for i in range(I):
                    dve.wait_ge(s.rt_ready, b * I + (i + 1))
                    ins = dve.tensor_copy(m.lg[:, i, :], bank_O[i][:, 0:E3])
                    ins.then_inc(s.c_O_free, 1)
                dve.wait_ge(s.c_O_free, b * OC + (OC + RING))
                settle(dve, s.settled_dve)
                for i in range(I):
                    ins = dve.max(m.m8[:, i, :], m.lg[:, i, :])
                ch.link(ins)
                for i in range(I):
                    dve.tensor_scalar(m.nmax[:, i:i + 1], m.m8[:, i, 0:1], -1.0, None, ALU.mult).then_inc(s.rt_nmax, 1)
                for i in range(I):
                    ins = dve.max_index(m.ix8[:, i, :], m.m8[:, i, :], m.lg[:, i, :])
                ch.link(ins)
                ch.link(dve.tensor_copy(m.ixf[:, :], m.ix8[:, :, 0]))
                dve.wait_ge(s.rt_exp, b * I + I)
                ch.link(dve.reciprocal(m.wmax[:, :], m.sum8[:, :]))
                ch.link(dve.tensor_scalar(m.wmax[:, :], m.wmax[:, :], m.gf[:, 1:2], None, ALU.mult))
                for i in range(I):
                    dve.tensor_scalar(m.we1[:, i, :], m.iota_f[:, :], m.ixf[:, i:i + 1], m.wmax[:, i:i + 1], ALU.is_equal, ALU.mult).then_inc(s.we_ready, 1)
                dve.wait_ge(s.we_ready, b * I + I)
                for i in range(I):
                    dve.tensor_copy(m.we[:, :, b * I + i], m.we1[:, i, :])
                for i in range(I):
                    dve.wait_ge(s.c_T_ready, b * TC + (UN + 4 + I + i + 1 + RING))
                    dve.tensor_copy(m.weT[:, b * I + i, :], bank_T[i][0:E3, 0:P]).then_inc(s.c_T_free, 1)
            ch.end_loop(B)

        def pool_c(pool, ch, rstd, split):
            pool.wait_ge(s.z_sum, B * I)
            pool.memset(m.v2h[:, :, :, DH2], 1.0)
            pool.memset(m.v2l[:, :, :, DH2], 0.0).then_inc(s.v2_ones, 1)
            pool.wait_ge(s.pj_ready, B * X1)
            for n in range(N_W1, N_WALL):
                split(n)
            with pool.Fori(0, B) as b:
                ch.loop(b, 1)
                rstd(b + 1, m.mv[:, 0:I, 1], m.rs[:, 0:I], s.x3_var, s.x3_rstd)
            ch.end_loop(B)

        HALF = NT // 2
        YR = 4
        bank_h, bank_y = bk[0:2], bk[4:8]

        def pe_d(pe, turn):
            pe.wait_ge(s.c_pj_free, B * PJ + RING)
            pe.wait_ge(s.c_T_free, B * TC + RING)
            pe.wait_ge(s.c_O_free, B * OC + RING)
            for n in range(N_W1, N_WALL):
                pe.wait_ge(s.w_split, n + 1)

            def hidden(e, a):
                for f in range(FT):
                    use = a * FT + f
                    pe.wait_ge(s.gelu_done, e * 2 * FT + (use + 1))
                    o, w = bank_h[use % 2][:, :], slice(f * P, (f + 1) * P)
                    xh, xl = (x_[:, a * HALF:(a + 1) * HALF, :].rearrange("p t c -> p (t c)") for x_ in (m.xdTh, m.xdTl))
                    pe.matmul(o, m.w1h[:, e, w], xh, start=True, stop=False)
                    pe.matmul(o, m.w1h[:, e, w], xl, start=False, stop=False)
                    pe.matmul(o, m.w1l[:, e, w], xh, start=False, stop=True).then_inc(s.h_ready, 1)

            def outputs(e, a):
                for t in range(HALF):
                    use = a * HALF + t
                    pe.wait_ge(s.y_free, e * NT + (NT + use + 1))
                    o = bank_y[use % YR][:, 0:D]
                    for f in range(FT):
                        if t == 0:
                            pe.wait_ge(s.h_lo, e * 2 * FT + (a * FT + f + 1 + RING))
                        hh, hl = (h_[:, a, f, t * P:(t + 1) * P] for h_ in (m.hTh, m.hTl))
                        pe.matmul(o, hh, m.w2h[:, e, f, :], start=(f == 0), stop=False)
                        pe.matmul(o, hh, m.w2l[:, e, f, :], start=False, stop=False)
                        ins = pe.matmul(o, hl, m.w2h[:, e, f, :], start=False, stop=(f == FT - 1))
                    ins.then_inc(s.y_ready, 1)

            for t in range(NT):
                pe.wait_ge(s.y_free, t + 1)
                pe.matmul(bank_y[t % YR][:, 0:D], m.weT[:, t, :], m.b2[:, :], start=True, stop=True).then_inc(s.y_ready, 1)
            hidden(0, 0)
            with pe.Fori(0, E3 - 1) as e:
                hidden(e, 1)
                outputs(e, 0)
                hidden(e + 1, 0)
                outputs(e, 1)
            hidden(E3 - 1, 1)
            outputs(E3 - 1, 0)
            outputs(E3 - 1, 1)

        def act_d(act):
            act.sem_inc(s.gelu_done, RING)
            with act.Fori(0, E3) as e:
                for use in range(2 * FT):
                    act.wait_ge(s.h_ready, e * 2 * FT + (use + 1))
                    act.wait_ge(s.h_lo, e * 2 * FT + (use + 1))
                    settle(act, s.settled_act)
                    act.activation(m.hf[:, use % 2, :], bank_h[use % 2][:, :], ACT.Gelu, bias=m.b1T[:, e, use % FT:use % FT + 1]).then_inc(s.gelu_done, 1)

        def pool_d(pool):
            pool.wait_ge(s.c_O_ready, B * UN + RING)
            with pool.Fori(0, E3) as e:
                for use in range(2 * FT):
                    pool.wait_ge(s.gelu_done, e * 2 * FT + (use + 1 + RING))
                    if use % FT == 0:
                        pool.wait_ge(s.y_ready, e * NT + (use // FT * HALF + HALF))
                    settle(pool, s.settled_pool)
                    pool.tensor_scalar(m.hTh[:, use // FT, use % FT, :], m.hf[:, use % 2, :], 1.0, 0.0, ALU.mult, ALU.add).then_inc(s.h_hi, 1)

        def dve_d(dve, ch):
            dve.sem_inc(s.h_lo, RING)
            dve.sem_inc(s.y_free, YR)

            def low(e, a):
                for f in range(FT):
                    use = a * FT + f
                    dve.wait_ge(s.h_hi, e * 2 * FT + (use + 1))
                    dve.tensor_tensor(m.hTl[:, a, f, :], m.hf[:, use % 2, :], m.hTh[:, a, f, :], ALU.subtract).then_inc(s.h_lo, 1)

            def add(e, a):
                for t in range(a * HALF, (a + 1) * HALF):
                    dve.wait_ge(s.y_ready, e * NT + (NT + t + 1))
                    dve.scalar_tensor_tensor(m.xt[:, t, :], bank_y[t % YR][:, 0:D], m.we[:, e, t:t + 1], m.xt[:, t, :], ALU.mult, ALU.add)\
                        .then_inc(s.y_free, 1)

            for t in range(NT):
                dve.wait_ge(s.y_ready, t + 1)
                dve.tensor_tensor(m.xt[:, t, :], m.xt[:, t, :], bank_y[t % YR][:, 0:D], ALU.add).then_inc(s.y_free, 1)
            low(0, 0)
            with dve.Fori(0, E3 - 1) as e:
                low(e, 1)
                add(e, 0)
                low(e + 1, 0)
                add(e, 1)
            low(E3 - 1, 1)
            add(E3 - 1, 0)
            add(E3 - 1, 1)

        @block.sync
        def _(sp):
            sp.dma_start(m.xt[:, :, :], xf).then_inc(s.x_in, 16)
            sp.dma_start(m.ct[:, :, :], cf).then_inc(s.ctx_in, 16)
            for n, (src, w, _, _) in enumerate(chunks):
                if n >= N_STAGE:
                    sp.wait_ge(s.w_split, n - N_STAGE + 1)
                dst = m.stage[:, n % N_STAGE, 0:w]
                if len(src.shape) == 3:
                    dst = dst.rearrange("p (e n) -> p e n", e=src.shape[1])
                sp.dma_start(dst, src).then_inc(stage_in[n % N_STAGE], 16)
            sp.wait_ge(s.out_ready, 1)
            sp.dma_start(outf, m.xt[:, :, :]).then_inc(s.out_done, 16)
            sp.wait_ge(s.out_done, 16)

        @block.scalar
        def _(act):
            SMALL = [(m.wi_row[:, :], w_i), (m.wf_row[:, :], w_f),
                     (m.bi[:, :], b_i.partition_broadcast(P)), (m.bf[:, :], b_f.partition_broadcast(P)),
                     (m.lnw[:, :], ln_w.partition_broadcast(P)), (m.gx[:, :], g_x.partition_broadcast(P)),
                     (m.gf[:, :], g_f.partition_broadcast(P)),
                     (m.wsd[:, 0:G1], Ws), (m.wsd[:, G1:2 * G1], Wd)]
            for dst, src in SMALL:
                act.dma_start(dst, src).then_inc(s.small_in, 16)
            for c, v in enumerate((gm, bm, gl, bl)):
                act.dma_start(m.cols[:, c:c + 1], v.rearrange("(p a) -> p a", a=1)).then_inc(s.small2_in, 16)
            act.dma_start(m.mask_u8[:, :, :], mask.partition_broadcast(P)).then_inc(s.small2_in, 16)
            wo = Wo0.rearrange("d (e n) -> e d n", e=E1)
            for e in range(E1):
                act.dma_start(m.wo0[DH1 * (e % 2):DH1 * (e % 2) + DH1, e // 2, :], wo[e, :, :]).then_inc(s.small2_in, 16)
            act.dma_start(m.wo1[:, :, :], Wo1.rearrange("(t p) n -> p t n", p=P)).then_inc(s.small2_in, 16)
            act.dma_start(m.gate[:, :], gate_w).then_inc(s.small2_in, 16)
            act.dma_start(m.b1_row[:, :], b1.rearrange("e (f p) -> (e f) p", p=P)).then_inc(s.small2_in, 16)
            act.dma_start(m.b2[:, :], b2).then_inc(s.small2_in, 16)

            act.wait_ge(s.small_in, 16 * N_SMALL)
            act.activation(m.gx[:, :], m.gx[:, :], ACT.Tanh)
            act.activation(m.gf[:, :], m.gf[:, :], ACT.Tanh).then_inc(s.tanh_ready, 1)
            for j in range(2):
                act.wait_ge(s.xT_ready, j + 1)
                act.activation(m.xnT[:, 4 * j:4 * j + 4, :].rearrange("p t c -> p (t c)"), bk[j][:, :], ACT.Copy).then_inc(s.xT_copied, 1)
            act.wait_ge(s.gates_b, 1)
            act.activation(m.tmp_a[:, :, :, :], m.fg[:, :, :, :], ACT.Abs).then_inc(s.act_chain, 1)
            act.wait_ge(s.act_chain, 1)
            act.activation(m.tmp_b[:, :, :, :], m.tmp_a[:, :, :, :], ACT.Exp, scale=-1.0).then_inc(s.act_chain, 1)
            act.wait_ge(s.act_chain, 2)
            act.activation(m.tmp_a[:, :, :, :], m.tmp_b[:, :, :, :], ACT.Ln, bias=1.0).then_inc(s.softplus, 1)
            act.wait_ge(s.mlog_ready, 1)
            act.activation(m.en[:, :, :, :], m.mlog[:, :, :, :], ACT.Exp, scale=-1.0).then_inc(s.en_ready, 1)

            def decay(u):
                b, h = divmod(u, NH0)
                act.wait_ge(s.L_ready, u + 1)
                if u >= 2:
                    act.wait_ge(s.C_ready, u - 1)
                act.activation(m.Dm[:, u % 2, 0:S], bk[u % 2][:, 0:S], ACT.Exp, scale=-1.0, bias=m.at[:, 0, b, h:h + 1])
                act.activation(m.Dm[:, u % 2, S:W0], bk[u % 2][:, S:W0], ACT.Exp, scale=-1.0, bias=m.at[:, 1, b, h:h + 1]).then_inc(s.D_ready, 1)

            def after_x1(b):
                act.wait_ge(s.x1T_ready, b + 1)
                if b >= 1:
                    act.wait_ge(s.g1_ready, b)
                src = bk[6][:, 0:S]
                act.activation(m.xT32[:, :, :].rearrange("p i c -> p (i c)"), src, ACT.Copy).then_inc(s.x1T_f32, 1)
                act.activation(m.xbTh[:, I * b:I * b + I, :].rearrange("p i c -> p (i c)"), src, ACT.Copy).then_inc(s.x1T_hi, 1)

            def gate_exp(b):
                act.wait_ge(s.g1_ready, b + 1)
                if b >= 1:
                    act.wait_ge(s.gate_ready, b)
                act.activation(m.sg[:, :, :].rearrange("p i g -> p (i g)"), bk[7][:, 0:I * 2 * G1], ACT.Exp, scale=-1.0).then_inc(s.g1_exp, 1)

            for u in range(UNITS):
                decay(u)
                if u % NH0 == 3 and u > NH0:
                    gate_exp(u // NH0 - 1)
                if u % NH0 == 3:
                    b = u // NH0
                    act.wait_ge(s.C_free, NH0 * (b + 1))
                    if b >= 1:
                        act.wait_ge(s.O0_free, b)
                    act.activation(m.absc[:, :], bk[4 + b % 2][:, 0:264].rearrange("p (n c) -> p n c", c=33)[:, :, 32], ACT.Abs).then_inc(s.absc_ready, 1)
                if u % NH0 == 1 and u > NH0:
                    after_x1(u // NH0 - 1)
            act.wait_ge(s.small2_in, 16 * N_SMALL2)
            after_x1(B - 1)
            gate_exp(B - 1)
            for j in range(2):
                act.wait_ge(s.cn_T, j + 1)
                for c in range(2):
                    b = 2 * j + c
                    if b >= 1:
                        act.wait_ge(s.kv_free, b)
                    act.activation(m.sm[:, 0, 0:S], bk[j][:, c * S:(c + 1) * S], ACT.Identity, scale=m.cols[:, 0:1], bias=m.cols[:, 1:2]).then_inc(s.kv_f, 1)
            act_b(act)
            act_c(act)
            act_d(act)

        @block.gpsimd
        def _(pool):
            ch = Chain(pool, s.pool_chain)
            pool.memset(m.ident[:, :], 0.0)
            pool.memset(m.identb[:, :], 0.0)
            pool.memset(m.tri[:, :], 1.0)
            pool.memset(m.causal[:, :], 0.0)
            ch.link(pool.memset(m.mhalf[:, :], -0.5))
            pool.affine_select(out=m.ident[:, :], in_=m.ident[:, :], compare_op=ALU.not_equal, fill=1.0, base=0,
                               pattern=[[-1, P]], channel_multiplier=1).then_inc(s.const, 1)
            pool.memset(m.ones[:, :], 1.0)
            pool.memset(m.zero16[:, :], 0.0)
            pool.memset(m.maskb[:, :, :], 0.0)
            pool.affine_select(out=m.identb[:, :], in_=m.identb[:, :], compare_op=ALU.not_equal, fill=1.0, base=0,
                               pattern=[[-1, P]], channel_multiplier=1)

            def rstd(k, src, dst, ready, done, n=None):
                pool.wait_ge(ready, k)
                settle(pool, s.settled_pool)
                ch.link(pool.tensor_scalar(dst, src, 1.0, EPS, ALU.mult, ALU.add))
                pool.tensor_tensor(dst, dst, m.mhalf[:, 0:dst.shape[1]], ALU.pow).then_inc(done, 1)

            rstd(1, m.mv[:, :, 1], m.rs[:, :], s.x_var, s.x_rstd)
            pool.affine_select(out=m.tri[:, :], in_=m.tri[:, :], compare_op=ALU.is_ge, fill=0.0, base=0,
                               pattern=[[1, P]], channel_multiplier=-1)
            for c in (0, S):
                pool.affine_select(out=m.causal[:, c:c + P], in_=m.causal[:, c:c + P], compare_op=ALU.is_ge, fill=BIG,
                                   base=0, pattern=[[1, P]], channel_multiplier=-1)
            pool.memset(m.vx[:, :, :, :], 1.0).then_inc(s.const, 1)
            rstd(2, m.mv2[:, :, 1], m.rs2[:, :], s.x_var, s.x_rstd)
            pool.wait_ge(s.const, 2)
            pool.tensor_scalar(m.vx[:, :, :, 0:DH0], m.ct[:, :, :].rearrange("p t (h c) -> p t h c", h=NH0), 1.0, 0.0,
                               ALU.mult, ALU.add).then_inc(s.vx_ready, 1)

            def split(n):
                src, w, hi, lo = chunks[n]
                raw = m.stage[:, n % N_STAGE, 0:w]
                if len(src.shape) == 3:
                    raw = raw.rearrange("p (e n) -> p e n", e=src.shape[1])
                pool.wait_ge(stage_in[n % N_STAGE], 16 * (n // N_STAGE + 1))
                pool.tensor_scalar(hi, raw, 1.0, 0.0, ALU.mult, ALU.add).then_inc(s.w_hi, 1)
                pool.wait_ge(s.w_hi, n + 1)
                pool.tensor_tensor(lo, raw, hi, ALU.subtract).then_inc(s.w_split, 1)

            for n in range(3):
                split(n)
            for b in range(B):
                rstd(b + 1, m.v32[:, :], m.r32[:, :], s.var0, s.rstd0)
                rstd(b + 1, m.mv[:, 0:I, 1], m.rs[:, 0:I], s.x1_var, s.x1_rstd)
                if b < 3:
                    split(3 + b)
            pool.wait_ge(s.small2_in, 16 * N_SMALL2)
            pool.tensor_scalar(m.maskb[:, :, 0:S], m.mask_u8[:, :, :], BIG, -BIG, ALU.mult, ALU.add).then_inc(s.maskb_ready, 1)
            pool.iota(m.iota_i[:, :], pattern=[[1, E3]], base=0, channel_multiplier=0).then_inc(s.const, 1)
            pool.wait_ge(s.const, 3)
            pool.tensor_copy(m.iota_f[:, :], m.iota_i[:, :])
            for b in range(B):
                pool.wait_ge(s.kv_f, b + 1)
                hi, lo = m.kvTh[:, b, 0:S], m.kvTl[:, b, 0:S]
                ch.link(pool.tensor_scalar(hi, m.sm[:, 0, 0:S], 1.0, 0.0, ALU.mult, ALU.add))
                pool.tensor_tensor(lo, m.sm[:, 0, 0:S], hi, ALU.subtract).then_inc(s.kv_free, 1)
            pool.memset(m.v1h[:, :, :, DH1], 1.0)
            pool.memset(m.v1l[:, :, :, DH1], 0.0).then_inc(s.const, 1)
            pool_b(pool, ch, rstd, split)
            pool_c(pool, ch, rstd, split)
            pool_d(pool)

        @block.tensor
        def _(pe):
            def turn(dst, src):
                return pe.transpose(dst, src, m.ident[0:src.shape[0], 0:src.shape[0]])

            pe.wait_ge(s.const, 1)
            pe.wait_ge(s.small_in, 16 * N_SMALL)
            for c in range(3):
                for g, row in enumerate((m.wi_row, m.wf_row)):
                    t = turn(bk[7][:, c * 8 + 4 * g:c * 8 + 4 * g + 4], row[:, c * D:(c + 1) * D])
            t.then_inc(s.wg_T, 1)
            pe.wait_ge(s.ctx_in, 16)
            for t in range(NT):
                ins = turn(bk[2 + t // 4][:, t % 4 * P:(t % 4 + 1) * P], m.ct[:, t, :])
                if t % 4 == 3:
                    ins.then_inc(s.cT_ready, 1)
            for t in range(NT):
                pe.wait_ge(s.xn_ready, t + 1)
                ins = turn(bk[t // 4][:, t % 4 * P:(t % 4 + 1) * P], m.xn[:, t, :])
                if t % 4 == 3:
                    ins.then_inc(s.xT_ready, 1)
            pe.wait_ge(s.wg_ready, 1)
            pe.wait_ge(s.cT_copied, 2)
            pe.wait_ge(s.xT_copied, 2)
            for t in range(NT):
                g = bk[6][:, t * 8:t * 8 + 8]
                pe.matmul(g, m.xnT[:, t, :], m.wg[:, 0, :], start=True, stop=False)
                ins = pe.matmul(g, m.cT[:, t, :], m.wg_ctx[:, :], start=False, stop=True)
            ins.then_inc(s.gates, 1)
            pe.wait_ge(s.const, 2)
            pe.wait_ge(s.logf_ready, 1)
            lf = [m.logf[:, i, :, :].rearrange("p b h -> p (b h)") for i in range(I)]
            pe.matmul(bk[7][:, 0:16], m.tri[:, :], lf[0], start=True, stop=True)
            pe.matmul(bk[7][:, 16:32], m.tri[:, :], lf[1], start=True, stop=False)
            pe.matmul(bk[7][:, 16:32], m.ones[:, :], lf[0], start=False, stop=True).then_inc(s.F_ready, 1)
            pe.wait_ge(s.a_ready, 1)
            for i in range(I):
                ins = turn(bk[7][0:UNITS, 128 + i * P:128 + (i + 1) * P], m.at[:, i, :, :].rearrange("p b h -> p (b h)"))
            ins.then_inc(s.aT_ready, 1)
            pe.wait_ge(s.M_ready, 1)
            for i in range(I):
                ins = turn(bk[6][:, 128 + 16 * i:144 + 16 * i], m.M16[:, i * P:(i + 1) * P])
            ins.then_inc(s.Mt_ready, 1)

            def scores(u):
                b, h = divmod(u, NH0)
                if u >= 2:
                    pe.wait_ge(s.D_ready, u - 1)
                L = bk[u % 2][:, 0:W0]
                pe.matmul(L, m.ident[0:UNITS, u:u + 1].to_broadcast([UNITS, P]), m.M16[:, :], start=True, stop=False)
                pe.matmul(L, m.identb[:, :], m.causal[:, :], start=False, stop=True).then_inc(s.L_ready, 1)
                if u >= 2:
                    pe.wait_ge(s.C_ready, u - 1)
                r = slice(DH0 * h, DH0 * (h + 1))
                q = m.xnT[r, I * b:I * b + I, :].rearrange("p i c -> p (i c)")
                Sb = bk[2 + u % 2]
                pe.matmul(Sb[:, 0:S], m.cT[r, I * b, :], q, start=True, stop=True)
                pe.matmul(Sb[:, S:W0], m.cT[r, I * b + 1, :], m.xnT[r, I * b + 1, :], start=True, stop=True).then_inc(s.S0_ready, 1)

            def values(u):
                b, h = divmod(u, NH0)
                if h == 0 and b >= 2:
                    pe.wait_ge(s.O0_free, b - 1)
                pe.wait_ge(s.C_ready, u + 1)
                C = m.C[:, u % 2, :]
                O = bk[4 + b % 2][:, 0:264].rearrange("p (i h c) -> p i h c", i=I, h=NH0)
                pe.matmul(O[:, 0, h, :], C[:, 0:P], m.vx[:, I * b, h, :], start=True, stop=True)
                pe.matmul(O[:, 1, h, :], C[:, P:S], m.vx[:, I * b, h, :], start=True, stop=False)
                ins = pe.matmul(O[:, 1, h, :], C[:, S:W0], m.vx[:, I * b + 1, h, :], start=False, stop=True)
                ins.then_inc(s.C_free, 1)

            def x1_turn(b):
                pe.wait_ge(s.x1n_ready, b + 1)
                if b >= 1:
                    pe.wait_ge(s.x1T_lo, b)
                if b == 0:
                    pe.wait_ge(s.mlog_ready, 1)
                for i in range(I):
                    ins = turn(bk[6][:, i * P:(i + 1) * P], m.n2[:, i, :])
                ins.then_inc(s.x1T_ready, 1)

            def x1_gates(b):
                pe.wait_ge(s.x1T_f32, b + 1)
                if b >= 1:
                    pe.wait_ge(s.g1_exp, b)
                for i in range(I):
                    ins = pe.matmul(bk[7][:, i * 2 * G1:(i + 1) * 2 * G1], m.xT32[:, i, :], m.wsd[:, :], start=True, stop=True)
                ins.then_inc(s.g1_ready, 1)

            pe.wait_ge(s.vx_ready, 1)
            scores(0)
            for u in range(UNITS):
                if u + 1 < UNITS:
                    scores(u + 1)
                values(u)
                if u % NH0 == 1 and u > NH0:
                    x1_turn(u // NH0 - 1)
                if u % NH0 == 2 and u > NH0:
                    x1_gates(u // NH0 - 1)
            pe.wait_ge(s.D_ready, UNITS)
            pe.wait_ge(s.xn_ready, NT + 1)
            for t in range(NT):
                ins = turn(bk[t // 4][:, t % 4 * P:(t % 4 + 1) * P], m.xn[:, t, :])
                if t % 4 == 3:
                    ins.then_inc(s.cn_T, 1)
            x1_turn(B - 1)
            x1_gates(B - 1)
            pe.wait_ge(s.small2_in, 16 * N_SMALL2)
            pe.wait_ge(s.C_ready, UNITS)
            turn(bk[2][:, 0:E3 * FT], m.b1_row[:, :]).then_inc(s.b1T_ready, 1)
            pe_b(pe, turn)
            pe_c(pe, turn)
            pe_d(pe, turn)

        @block.vector
        def _(dve):
            ch = Chain(dve, s.dve_chain)

            def stats(src, n, st, mv, done):
                settle(dve, s.settled_dve)
                for t in range(n):
                    ins = dve.bn_stats(st[:, t, :], src(t))
                ch.link(ins)
                settle(dve, s.settled_dve)
                for t in range(n):
                    ins = dve.bn_aggr(mv[:, t, :], st[:, t, :])
                ins.then_inc(done, 1)

            dve.wait_ge(s.x_in, 16)
            stats(lambda t: m.xt[:, t, :], NT, m.st, m.mv, s.x_var)
            dve.wait_ge(s.ctx_in, 16)
            stats(lambda t: m.ct[:, t, :], NT, m.st2, m.mv2, s.x_var)
            dve.wait_ge(s.wg_T, 1)
            ch.link(dve.tensor_copy(m.wg[:, :, :].rearrange("p c g -> p (c g)"), bk[7][:, 0:24]))
            dve.tensor_tensor(m.wg_ctx[:, :], m.wg[:, 1, :], m.wg[:, 2, :], ALU.add).then_inc(s.wg_ready, 1)
            dve.wait_ge(s.wg_ready, 1)
            dve.wait_ge(s.x_var, 2)
            dve.wait_ge(s.x_rstd, 1)
            for t in range(NT):
                dve.tensor_scalar(m.xn[:, t, :], m.xt[:, t, :], m.mv[:, t, 0:1], m.rs[:, t:t + 1], ALU.subtract, ALU.mult).then_inc(s.xn_ready, 1)
            for j in range(2):
                dve.wait_ge(s.cT_ready, j + 1)
                dve.tensor_copy(m.cT[:, 4 * j:4 * j + 4, :].rearrange("p t c -> p (t c)"), bk[2 + j][:, :]).then_inc(s.cT_copied, 1)
            dve.wait_ge(s.tanh_ready, 1)
            dve.tensor_scalar(m.lnw[:, :], m.lnw[:, :], 1.0, m.gx[:, 0:1], ALU.add, ALU.mult)
            dve.wait_ge(s.gates, 1)
            G = bk[6][:, 0:64].rearrange("p (b i g) -> p b i g", b=B, i=I)

            def by_bi(a):
                return a[:, :, :, :].rearrange("p i b h -> p b i h")

            def bias(a):
                return a[:, :].unsqueeze(1).unsqueeze(1).to_broadcast([P, B, I, NH0])

            dve.tensor_tensor(by_bi(m.fg), G[:, :, :, NH0:2 * NH0], bias(m.bf), ALU.add).then_inc(s.gates_b, 1)
            ch.link(dve.tensor_tensor(by_bi(m.ig), G[:, :, :, 0:NH0], bias(m.bi), ALU.add))
            dve.wait_ge(s.softplus, 1)
            flat = lambda a: a[:, :, :, :].rearrange("p i b h -> p (i b h)")
            dve.scalar_tensor_tensor(flat(m.logf), flat(m.fg), 0.0, flat(m.tmp_a), ALU.min, ALU.subtract).then_inc(s.logf_ready, 1)
            dve.wait_ge(s.F_ready, 1)
            ch.link(dve.tensor_copy(flat(m.Ft), bk[7][:, 0:32]))
            dve.tensor_tensor(flat(m.at), flat(m.ig), flat(m.Ft), ALU.subtract).then_inc(s.a_ready, 1)
            dve.wait_ge(s.const, 2)
            dve.wait_ge(s.aT_ready, 1)
            ch.link(dve.tensor_tensor_scan(m.M16[:, 0:S], m.zero16[:, :], bk[7][0:UNITS, 128:128 + S], -3e38, ALU.add, ALU.max))
            dve.tensor_copy(m.M16[:, S:W0], m.M16[:, P:S]).then_inc(s.M_ready, 1)
            dve.wait_ge(s.Mt_ready, 1)
            dve.tensor_tensor(flat(m.mlog), flat(m.Ft), bk[6][:, 128:160], ALU.add).then_inc(s.mlog_ready, 1)

            def weigh(u):
                dve.wait_ge(s.S0_ready, u + 1)
                dve.wait_ge(s.D_ready, u + 1)
                if u >= 2:
                    dve.wait_ge(s.C_free, u - 1)
                dve.scalar_tensor_tensor(m.C[:, u % 2, :], bk[2 + u % 2][:, 0:W0], DH0 ** -0.5, m.Dm[:, u % 2, :],
                                         ALU.mult, ALU.mult).then_inc(s.C_ready, 1)

            def finish(b):
                O = bk[4 + b % 2][:, 0:264].rearrange("p (n c) -> p n c", c=DH0 + 1)
                wide = lambda a: a.unsqueeze(2).to_broadcast([P, I * NH0, DH0])
                nrm, en = m.nrm[:, :].rearrange("p (i h) -> p i h", i=I), m.en[:, :, b, :]
                dve.wait_ge(s.en_ready, 1)
                dve.wait_ge(s.absc_ready, b + 1)
                ch.link(dve.tensor_tensor(nrm, m.absc[:, :].rearrange("p (i h) -> p i h", i=I), en, ALU.max))
                ch.link(dve.tensor_scalar(m.nrm[:, :], m.nrm[:, :], EPS0, None, ALU.add))
                ch.link(dve.reciprocal(m.rn[:, :], m.nrm[:, :]))
                ins = dve.tensor_tensor(m.hh[:, :, :], O[:, :, 0:DH0], wide(m.rn[:, :]), ALU.mult)
                ins.then_inc(s.O0_free, 1)
                dve.wait_ge(s.O0_free, b + 1)
                ch.link(dve.tensor_reduce(m.s32[:, :], m.hh[:, :, :], AX.X, ALU.add))
                ch.link(dve.scalar_tensor_tensor(m.hc[:, :, :], wide(m.s32[:, :]), -1.0 / DH0, m.hh[:, :, :], ALU.mult, ALU.add))
                ch.link(dve.tensor_tensor(m.sq[:, :, :], m.hc[:, :, :], m.hc[:, :, :], ALU.mult))
                ch.link(dve.tensor_reduce(m.s32[:, :], m.sq[:, :, :], AX.X, ALU.add))
                dve.tensor_scalar(m.v32[:, :], m.s32[:, :], 1.0 / DH0, None, ALU.mult).then_inc(s.var0, 1)
                dve.wait_ge(s.rstd0, b + 1)
                ch.link(dve.tensor_tensor(m.sq[:, :, :], m.hc[:, :, :], wide(m.r32[:, :]), ALU.mult))
                y = m.sq[:, :, :].rearrange("p (i h) c -> p i (h c)", i=I)
                ch.link(dve.tensor_tensor(y, y, m.lnw[:, :].unsqueeze(1).to_broadcast([P, I, D]), ALU.mult))
                xb = m.xt[:, I * b:I * b + I, :]
                ch.link(dve.tensor_tensor(xb, xb, y, ALU.add))
                stats(lambda t: m.xt[:, I * b + t, :], I, m.st, m.mv, s.x1_var)
                dve.wait_ge(s.x1_rstd, b + 1)
                if b >= 1:
                    dve.wait_ge(s.x1T_ready, b)
                for i in range(I):
                    ins = dve.tensor_scalar(m.n2[:, i, :], m.xt[:, I * b + i, :], m.mv[:, i, 0:1], m.rs[:, i:i + 1], ALU.subtract, ALU.mult)
                ins.then_inc(s.x1n_ready, 1)

            def x1_low(b):
                dve.wait_ge(s.x1T_hi, b + 1)
                dve.tensor_tensor(m.xbTl[:, I * b:I * b + I, :].rearrange("p i c -> p (i c)"), bk[6][:, 0:S],
                                  m.xbTh[:, I * b:I * b + I, :].rearrange("p i c -> p (i c)"), ALU.subtract).then_inc(s.x1T_lo, 1)

            def top3(b):
                dve.wait_ge(s.g1_exp, b + 1)
                sgf = m.sg[:, :, :].rearrange("p i g -> p (i g)")
                ch.link(dve.tensor_scalar(sgf, sgf, 1.0, None, ALU.add))
                ch.link(dve.reciprocal(sgf, sgf))
                sg = sgf.rearrange("p (n e) -> p n e", e=E1)
                N = I * 2 * H1
                for e in range(E1):
                    if e > 0:
                        ins = dve.tensor_tensor(m.cmp[:, :, e, 0:e], sg[:, :, 0:e], sg[:, :, e:e + 1].to_broadcast([P, N, e]), ALU.is_ge)
                    if e < E1 - 1:
                        ins = dve.tensor_tensor(m.cmp[:, :, e, e:E1 - 1], sg[:, :, e + 1:E1], sg[:, :, e:e + 1].to_broadcast([P, N, E1 - 1 - e]), ALU.is_gt)
                ch.link(ins)
                ch.link(dve.tensor_reduce(m.cnt[:, :], m.cmp[:, :, :, :].rearrange("p n e c -> p (n e) c"), AX.X, ALU.add))
                g = slice(I * b, I * b + I)
                dve.tensor_scalar(m.topm[:, g, :].rearrange("p i g -> p (i g)"), m.cnt[:, :], TOP - 0.5, None, ALU.is_lt)
                dve.scalar_tensor_tensor(m.gatev[:, g, :].rearrange("p i g -> p (i g)"), m.cnt[:, :], TOP - 0.5, sgf,
                                         ALU.is_lt, ALU.mult).then_inc(s.gate_ready, 1)

            for u in range(UNITS):
                weigh(u)
                if u % NH0 == 0 and u > 0:
                    finish(u // NH0 - 1)
                if u % NH0 == 2 and u > NH0:
                    x1_low(u // NH0 - 1)
                if u % NH0 == 3 and u > NH0:
                    top3(u // NH0 - 1)
            dve.wait_ge(s.x_rstd, 2)
            for t in range(NT):
                ins = dve.tensor_scalar(m.xn[:, t, :], m.ct[:, t, :], m.mv2[:, t, 0:1], m.rs2[:, t:t + 1], ALU.subtract, ALU.mult)
            ins.then_inc(s.xn_ready, 1)
            finish(B - 1)
            x1_low(B - 1)
            top3(B - 1)
            dve.wait_ge(s.b1T_ready, 1)
            dve.tensor_copy(m.b1T[:, :, :].rearrange("p e f -> p (e f)"), bk[2][:, 0:E3 * FT]).then_inc(s.b1T_copied, 1)
            dve_b(dve, ch, stats)
            dve_c(dve, ch, stats)
            dve_d(dve, ch)
            dve.wait_ge(s.y_free, NT * (E3 + 1) + YR)
            dve.sem_inc(s.out_ready, 1)


INS = ["x", "ctx_1024", "mask_BxS2_bf1", "g_xattn", "g_ffn", "L0_xattn_w_igate", "L0_xattn_b_igate", "L0_xattn_w_fgate",
       "L0_xattn_b_fgate", "L0_xattn_ln_weight", "L0_ffn_Wq", "L0_ffn_Wkv", "L0_ffn_Ws", "L0_ffn_Wd", "L0_ffn_Wo",
       "L1_xattn_gm", "L1_xattn_bm", "L1_xattn_gl", "L1_xattn_bl", "L1_xattn_Wq", "L1_xattn_Wk", "L1_xattn_Wv", "L1_xattn_Wo",
       "L1_ffn_gate_w", "L1_ffn_w1", "L1_ffn_b1", "L1_ffn_w2", "L1_ffn_b2"]


OUTS = [((B, S, D), "float32")]


def kernel(**inputs):
    import numpy as np
    import concourse.bacc as bacc
    from concourse.bass_utils import run_bass_kernel_spmd as run

    nc = bacc.Bacc("TRN2", target_bir_lowering=False, num_devices=1)
    arrays, args = {}, []
    for name in INS:
        a = np.ascontiguousarray(inputs[name])
        arrays[f"in_{name}"] = a
        args.append(nc.dram_tensor(f"in_{name}", a.shape, mybir.dt.from_np(a.dtype), kind="ExternalInput").ap())
    for i, (shape, dtype) in enumerate(OUTS):
        args.append(nc.dram_tensor(f"out_{i}", shape, mybir.dt.from_np(np.dtype(dtype)), kind="ExternalOutput").ap())
    build(nc, *args)
    r = run(nc, [arrays], core_ids=[0])
    return r.results[0]["out_0"]
```

```python
from contextlib import ExitStack

import concourse.bass as bass
from concourse import mybir

ALU = mybir.AluOpType
ACT = mybir.ActivationFunctionType
AX = mybir.AxisListType
F32 = mybir.dt.float32
F16 = mybir.dt.float16
BF16 = mybir.dt.bfloat16
U8 = mybir.dt.uint8
U32 = mybir.dt.uint32

P = 128
B, S, D = 4, 256, 128
I = S // P
NT = B * I
BIG = 1e30
EPS = 1e-5

NH0, DH0 = 4, 32
UNITS = B * NH0
W0 = S + P
EPS0 = 1e-6
PART_AT = 32
M_ROWS = 2 * PART_AT + UNITS

H1, E1, DH1, TOP = 8, 5, 64, 3
HD1 = H1 * DH1
G1 = H1 * E1
PARTS = ("q", "k", "v")

H2, DH2 = 16, 64
KT = 2 * S // P
HP2 = H2 // 2
INNER = H2 * DH2

E3, FF = 8, 512
FT = FF // P

STAGE = 1280
N_STAGE = 3


def settle(eng, sem):
    eng.sem_inc(sem, 1)


class Names:
    pass


class Chain:

    def __init__(self, eng, sem):
        self.eng, self.sem, self.base, self.k, self.turn, self.per = eng, sem, 0, 0, 0, 0

    def loop(self, turn, per):
        self.base, self.k, self.turn, self.per = self.base + self.k, 0, turn, per

    def end_loop(self, turns):
        assert self.k == self.per, (self.k, self.per)
        self.base, self.k, self.turn, self.per = self.base + turns * self.per, 0, 0, 0

    def link(self, instruction):
        self.k += 1
        instruction.then_inc(self.sem, 1)
        self.eng.wait_ge(self.sem, self.turn * self.per + (self.base + self.k) if self.per else self.base + self.k)


def weight_chunks(m, d):
    out = []
    for c in range(2):
        out.append((d.Wq0[:, c * 1280:(c + 1) * 1280], 1280, m.wq0h[:, c * 1280:(c + 1) * 1280], m.wq0l[:, c * 1280:(c + 1) * 1280]))
    for c in range(4):
        out.append((d.Wkv0[:, c * 1280:(c + 1) * 1280], 1280, m.wkv0h[:, c * 1280:(c + 1) * 1280], m.wkv0l[:, c * 1280:(c + 1) * 1280]))
    for src, hi, lo in ((d.Wv1, m.wv1h, m.wv1l), (d.Wq1, m.wq1h, m.wq1l), (d.Wk1, m.wk1h, m.wk1l)):
        out.append((src, INNER, hi[:, :], lo[:, :]))
    for c in range(E3 // 2):
        out.append((d.w1[2 * c:2 * c + 2, :, :].rearrange("e p n -> p e n"), 2 * FF,
                    m.w1h[:, 2 * c:2 * c + 2, :], m.w1l[:, 2 * c:2 * c + 2, :]))
    for c in range(E3 // 2):
        out.append((d.w2[2 * c:2 * c + 2, :, :].rearrange("e (f p) n -> p (e f) n", p=P), 2 * FT * D,
                    m.w2h[:, 2 * c:2 * c + 2, :, :].rearrange("p e f n -> p (e f) n"),
                    m.w2l[:, 2 * c:2 * c + 2, :, :].rearrange("p e f n -> p (e f) n")))
    return out


N_W0 = 6
N_W1 = 9
N_WALL = 17
DVE_STEPS_B, POOL_STEPS_B, DVE_STEPS_C = 12, 16, 8


def build(nc, x, ctx_in, mask, g_x, g_f, w_i, b_i, w_f, b_f, ln_w, Wq0, Wkv0, Ws, Wd, Wo0,
          gm, bm, gl, bl, Wq1, Wk1, Wv1, Wo1, gate_w, w1, b1, w2, b2, out):
    with ExitStack() as stack:
        m, s, d = Names(), Names(), Names()

        def sb(name, shape, dt=F32):
            return stack.enter_context(nc.sbuf_tensor(name, shape, dt))

        def share(arena, words, *parts):
            area = stack.enter_context(nc.sbuf_tensor(arena, [P, words], F32))
            views = []
            for at, shape, dt in parts:
                n = 1
                for k in shape:
                    n *= k
                used = n if dt == F32 else n // 2
                assert at + used <= words, arena
                v = area[:, at:at + used]
                if dt != F32:
                    v = v.bitcast(dt)
                if len(shape) > 1:
                    names = "abcd"[:len(shape)]
                    v = v.rearrange("p (%s) -> p %s" % (" ".join(names), " ".join(names)), **dict(zip(names, shape)))
                views.append(v)
            return views

        def sem(name):
            return stack.enter_context(nc.semaphore("s_" + name))

        d.Wq0, d.Wkv0, d.Wq1, d.Wk1, d.Wv1, d.w1, d.w2 = Wq0, Wkv0, Wq1, Wk1, Wv1, w1, w2
        bk = [stack.enter_context(nc.psum_tensor(f"bank{i}", [P, 512], F32)) for i in range(8)]

        m.ident = sb("ident", [P, P])
        m.ones = sb("ones", [P, P])
        m.tri = sb("tri", [P, P])
        m.identb = sb("identb", [P, P], BF16)
        m.causal = sb("causal", [P, W0], BF16)
        m.zero16 = sb("zero16", [M_ROWS, S])
        m.mhalf = sb("mhalf", [P, 16])
        m.iota_i = sb("iota_i", [P, E3], mybir.dt.int32)
        m.iota_f = sb("iota_f", [P, E3])
        m.wi_row = sb("wi_row", [NH0, 3 * D])
        m.wf_row = sb("wf_row", [NH0, 3 * D])
        m.wg = sb("wg", [P, 3, 2 * NH0])
        m.wg_ctx = sb("wg_ctx", [P, 2 * NH0])
        m.bi = sb("bi", [P, NH0])
        m.bf = sb("bf", [P, NH0])
        m.lnw = sb("lnw", [P, D])
        m.gx = sb("gx", [P, 2])
        m.gf = sb("gf", [P, 2])
        m.cols = sb("cols", [P, 4])
        m.mask_u8 = sb("mask_u8", [P, B, S], U8)
        m.maskb = sb("maskb", [P, B, 2 * S], BF16)
        m.maskrow = sb("maskrow", [P, 2 * S], BF16)
        m.wsd = sb("wsd", [P, 2 * G1])
        m.wo0 = sb("wo0", [P, 3, D])
        m.wo1 = sb("wo1", [P, HP2, D])
        m.gate = sb("gate", [P, E3])
        m.b1_row = sb("b1_row", [E3 * FT, P])
        m.b1T = sb("b1T", [P, E3, FT])
        m.b2 = sb("b2", [E3, D])
        m.stage = sb("stage", [P, N_STAGE, STAGE])
        m.wq1h, m.wq1l, m.wk1h, m.wk1l, m.wv1h, m.wv1l = (
            sb(n, [P, INNER], F16) for n in ("wq1h", "wq1l", "wk1h", "wk1l", "wv1h", "wv1l"))
        NQ, NW = H1 * E1 * DH1, E3 * FF // 2
        m.wq0h, m.wq0l, m.wkv0h, m.wkv0l, m.w1h, m.w1l, m.w2h, m.w2l = share("weights", 4 * NW,
              (0, (NQ,), F16), (NQ // 2, (NQ,), F16), (NQ, (2 * NQ,), F16), (2 * NQ, (2 * NQ,), F16),
              (0, (E3, FF), F16), (NW, (E3, FF), F16), (2 * NW, (E3, FT, D), F16), (3 * NW, (E3, FT, D), F16))
        NV = KT * H2 * (DH2 + 1) // 2
        m.prod, m.acc, m.v2h, m.v2l, m.ao, m.hTh, m.hTl, m.hf, *work_early = share("work", 16 * HD1,
              (0, (2, E1, HD1), F32), (2 * E1 * HD1, (3, I, HD1), F32),
              (0, (KT, H2, DH2 + 1), F16), (NV, (KT, H2, DH2 + 1), F16), (2 * NV, (I, INNER), F32),
              (0, (2, FT, 512), F16), (2048, (2, FT, 512), F16), (4096, (4, 512), F32),
              (0, (I, M_ROWS), F32), (I * M_ROWS, (W0,), F32), (I * M_ROWS + W0, (2, W0), F32), (I * M_ROWS + 3 * W0, (3, W0), BF16))
        m.xnT, m.cT, m.vx, m.ho, m.aoT, m.xdTh, m.xdTl = share("work0", 3 * NT * P + NT * NH0,
              (0, (NT, P), F32), (NT * P, (NT, P), F32), (2 * NT * P, (NT, NH0, DH0 + 1), F32),
              (0, (I, HD1), F32), (0, (I, HP2, P), F32),
              (2 * NT * P, (NT, P), F16), (2 * NT * P + NT * P // 2, (NT, P), F16))
        m.xt = sb("xt", [P, NT, D])
        m.ct = sb("ct", [P, NT, D])
        m.st = sb("st", [P, NT, 6])
        m.mv = sb("mv", [P, NT, 2])
        m.rs = sb("rs", [P, NT])
        m.st2 = sb("st2", [P, NT, 6])
        m.mv2 = sb("mv2", [P, NT, 2])
        m.rs2 = sb("rs2", [P, NT])
        m.kvTh = sb("kvTh", [P, B, 2 * S], F16)
        m.kvTl = sb("kvTl", [P, B, 2 * S], F16)
        m.xbTh = sb("xbTh", [P, NT, P], F16)
        m.xbTl = sb("xbTl", [P, NT, P], F16)
        m.ig, m.fg, m.tmp_a, m.tmp_b, m.logf, m.Ft, m.at, m.mlog, m.en = (
            sb(n, [P, I, B, NH0]) for n in ("ig", "fg", "tmp_a", "tmp_b", "logf", "Ft", "at", "mlog", "en"))
        m.a3, m.M16, m.M_rest, m.Mp = work_early
        m.M16, m.M_rest, m.Mp = (a[0:M_ROWS] for a in (m.M16, m.M_rest, m.Mp))
        m.M3 = sb("M3", [M_ROWS, W0], BF16)
        m.sel3 = sb("sel3", [M_ROWS, PART_AT], BF16)
        m.Dm = sb("Dm", [P, 2, W0])
        m.C = sb("C", [P, 2, W0])
        m.absc, m.nrm, m.rn, m.s32, m.v32, m.r32 = (
            sb(n, [P, I * NH0]) for n in ("absc", "nrm", "rn", "s32", "v32", "r32"))
        m.hh = sb("hh", [P, I * NH0, DH0])
        m.hc = sb("hc", [P, I * NH0, DH0])
        m.sq = sb("sq", [P, I * NH0, DH0])
        m.sg = sb("sg", [P, I, 2 * G1])
        m.cmp = sb("cmp", [P, I * 2 * H1, E1, E1 - 1], BF16)
        m.cnt = sb("cnt", [P, I * 2 * G1])
        m.topm = sb("topm", [P, NT, 2 * G1])
        m.gatev = sb("gatev", [P, NT, 2 * G1])
        m.qTh = sb("qTh", [P, 4, S], F16)
        m.qTl = sb("qTl", [P, 4, S], F16)
        m.kTh = sb("kTh", [P, 4, S], F16)
        m.kTl = sb("kTl", [P, 4, S], F16)
        m.v1h = sb("v1h", [P, I, H1, DH1 + 1], F16)
        m.v1l = sb("v1l", [P, I, H1, DH1 + 1], F16)
        m.nm = sb("nm", [P, 4, 2])
        m.nmx = sb("nmx", [P, 4, 2])
        m.xn, m.Pr = share("work1", NT * D, (0, (NT, D), F32), (0, (2, 512), F32))
        m.PTh = sb("PTh", [P, 2, 4, P], F16)
        m.PTl = sb("PTl", [P, 2, 4, P], F16)
        m.den = sb("den", [P, 8])
        m.z = sb("z", [P, I, E1 * DH1])
        m.zT = sb("zT", [P, 3, P])
        m.xT32 = sb("xT32", [P, I, P])
        m.n2 = sb("n2", [P, I, D])
        m.q2h = sb("q2h", [P, 2, S], F16)
        m.q2l = sb("q2l", [P, 2, S], F16)
        m.k2h = sb("k2h", [P, 2, 2 * S], F16)
        m.k2l = sb("k2l", [P, 2, 2 * S], F16)
        m.sm = sb("sm", [P, 2, 512])
        m.lg = sb("lg", [P, NT, E3])
        m.m8 = sb("m8", [P, NT, 8])
        m.ix8 = sb("ix8", [P, NT, 8], U32)
        m.ixf = sb("ixf", [P, NT])
        m.lgm = sb("lgm", [P, NT, E3])
        m.ex8 = sb("ex8", [P, NT, E3])
        m.sum8 = sb("sum8", [P, NT])
        m.wmax = sb("wmax", [P, NT])
        m.we1 = sb("we1", [P, NT, E3])
        m.we = sb("we", [P, E3, NT])
        m.weT = sb("weT", [E3, NT, P])

        s.x_in = sem("x_in")
        s.ctx_in = sem("ctx_in")
        s.small_in = sem("small_in")
        s.small2_in = sem("small2_in")
        s.w_hi = sem("w_hi")
        s.w_split = sem("w_split")
        s.settled_act = sem("settled_act")
        s.settled_dve = sem("settled_dve")
        s.settled_pool = sem("settled_pool")
        s.const = sem("const")
        s.pool_chain = sem("pool_chain")
        s.dve_chain = sem("dve_chain")
        s.act_chain = sem("act_chain")
        s.out_done = sem("out_done")
        s.x_var = sem("x_var")
        s.x_rstd = sem("x_rstd")
        s.xn_ready = sem("xn_ready")
        s.xT_ready = sem("xT_ready")
        s.cT_ready = sem("cT_ready")
        s.xT_copied = sem("xT_copied")
        s.cT_copied = sem("cT_copied")
        s.wg_T = sem("wg_T")
        s.wg_ready = sem("wg_ready")
        s.gates = sem("gates")
        s.gates_b = sem("gates_b")
        s.softplus = sem("softplus")
        s.logf_ready = sem("logf_ready")
        s.F_ready = sem("F_ready")
        s.a_ready = sem("a_ready")
        s.aT_ready = sem("aT_ready")
        s.M_ready = sem("M_ready")
        s.M3_ready = sem("M3_ready")
        s.Mt_ready = sem("Mt_ready")
        s.mlog_ready = sem("mlog_ready")
        s.en_ready = sem("en_ready")
        s.L_ready = sem("L_ready")
        s.S0_ready = sem("S0_ready")
        s.D_ready = sem("D_ready")
        s.C_ready = sem("C_ready")
        s.C_free = sem("C_free")
        s.absc_ready = sem("absc_ready")
        s.O0_free = sem("O0_free")
        s.var0 = sem("var0")
        s.rstd0 = sem("rstd0")
        s.vx_ready = sem("vx_ready")
        s.tanh_ready = sem("tanh_ready")
        s.cn_T = sem("cn_T")
        s.kv_f = sem("kv_f")
        s.kv_free = sem("kv_free")
        s.maskb_ready = sem("maskb_ready")
        s.maskrow_ready = sem("maskrow_ready")
        s.x1_var = sem("x1_var")
        s.x1_rstd = sem("x1_rstd")
        s.x1n_ready = sem("x1n_ready")
        s.x1T_ready = sem("x1T_ready")
        s.x1T_f32 = sem("x1T_f32")
        s.x1T_hi = sem("x1T_hi")
        s.x1T_lo = sem("x1T_lo")
        s.g1_ready = sem("g1_ready")
        s.g1_exp = sem("g1_exp")
        s.gate_ready = sem("gate_ready")
        s.b1T_ready = sem("b1T_ready")
        s.b1T_copied = sem("b1T_copied")
        s.pj_ready = sem("pj_ready")
        s.prod_ready = sem("prod_ready")
        s.prod_free = sem("prod_free")
        s.acc_ready = sem("acc_ready")
        s.pair_ready = sem("pair_ready")
        s.T_ready = sem("T_ready")
        s.T_hi = sem("T_hi")
        s.T_free = sem("T_free")
        s.v1hi_ready = sem("v1hi_ready")
        s.v1lo_ready = sem("v1lo_ready")
        s.S_ready = sem("S_ready")
        s.exp_done = sem("exp_done")
        s.nm_ready = sem("nm_ready")
        s.wo_ready = sem("wo_ready")
        s.O_ready = sem("O_ready")
        s.O_free = sem("O_free")
        s.z_ready = sem("z_ready")
        s.z_sum = sem("z_sum")
        s.z_last = sem("z_last")
        s.zT_ready = sem("zT_ready")
        s.zT_copied = sem("zT_copied")
        s.x2_ready = sem("x2_ready")
        s.latT_ready = sem("latT_ready")
        s.lat_lo = sem("lat_lo")
        s.x2_var = sem("x2_var")
        s.x2_rstd = sem("x2_rstd")
        s.x2n_ready = sem("x2n_ready")
        s.lat_ready = sem("lat_ready")
        s.lat_hi = sem("lat_hi")
        s.c_pj_ready = sem("c_pj_ready")
        s.c_pj_hi = sem("c_pj_hi")
        s.c_pj_free = sem("c_pj_free")
        s.c_S_ready = sem("c_S_ready")
        s.c_max_done = sem("c_max_done")
        s.c_exp_done = sem("c_exp_done")
        s.c_T_ready = sem("c_T_ready")
        s.c_T_hi = sem("c_T_hi")
        s.c_T_free = sem("c_T_free")
        s.c_O_ready = sem("c_O_ready")
        s.c_O_free = sem("c_O_free")
        s.v2_ones = sem("v2_ones")
        s.c_wo_ready = sem("c_wo_ready")
        s.ao_copied = sem("ao_copied")
        s.xdT_ready = sem("xdT_ready")
        s.xd_lo = sem("xd_lo")
        s.weT_ready = sem("weT_ready")
        s.weT_copied = sem("weT_copied")
        s.x3_var = sem("x3_var")
        s.x3_rstd = sem("x3_rstd")
        s.x3n_ready = sem("x3n_ready")
        s.xd_f32 = sem("xd_f32")
        s.xd_hi = sem("xd_hi")
        s.rt_ready = sem("rt_ready")
        s.rt_nmax = sem("rt_nmax")
        s.rt_exp = sem("rt_exp")
        s.we_ready = sem("we_ready")
        s.h_ready = sem("h_ready")
        s.gelu_done = sem("gelu_done")
        s.h_hi = sem("h_hi")
        s.h_lo = sem("h_lo")
        s.y_ready = sem("y_ready")
        s.y_free = sem("y_free")
        s.out_ready = sem("out_ready")

        stage_in = [stack.enter_context(nc.semaphore(f"s_stage_in{n}")) for n in range(N_STAGE)]
        N_SMALL, N_SMALL2 = 11, 2 + 1 + E1 + 4
        block = stack.enter_context(nc.Block())
        chunks = weight_chunks(m, d)
        xf = x.rearrange("b (i p) c -> p (b i) c", p=P)
        cf = ctx_in.rearrange("b (i p) c -> p (b i) c", p=P)
        outf = out.rearrange("b (i p) c -> p (b i) c", p=P)

        RING = 2
        T1, O1, X1 = 4 + H1, H1 // 2, len(PARTS) * I * E1
        STEPS = H1 + 4
        HEAD_STEPS = 6
        bank_pj, bank_S, bank_T, bank_O = bk[0:2], bk[2:4], bk[4:6], bk[6:8]
        wq0 = [w.rearrange("p (h e c) -> p h e c", h=H1, e=E1) for w in (m.wq0h, m.wq0l)]
        wkv0 = [w.rearrange("p (a h e c) -> p a h e c", a=2, h=H1, e=E1) for w in (m.wkv0h, m.wkv0l)]

        def chunk(c):
            return c // (I * E1), c // E1 % I, c % E1

        def chunks_of(step):
            k, n = step - HEAD_STEPS, X1 // (STEPS - HEAD_STEPS)
            mine = list(range(X1))[k * n:(k + 1) * n]
            return mine[:2], mine[2:3], mine[3:]

        def turns_of(step):
            return {STEPS - 3: (0, 1), STEPS - 2: (2,), STEPS - 1: (3,)}.get(step, ())

        def heads8(a):
            return a.rearrange("p (h c) -> p h c", h=H1)

        def wide(a, n):
            return a.unsqueeze(2).to_broadcast([P, a.shape[1], n])

        def pe_b(pe, turn, between):
            pe.sem_inc(s.O_ready, RING)
            pe.sem_inc(s.wo_ready, 1)
            def project(b, c):
                part, i, e = chunk(c)
                if c >= 2 or not isinstance(b, int) or b > 0:
                    pe.wait_ge(s.prod_ready, b * X1 + (c - 1))
                wh, wl = (w[:, :, e, :] for w in wq0) if part == 0 else (w[:, part - 1, :, e, :] for w in wkv0)
                o = heads8(bank_pj[c % 2][:, :])
                xh, xl = m.xbTh[:, b * I + i, :], m.xbTl[:, b * I + i, :]
                pe.matmul(o, xh, wh, start=True, stop=False)
                pe.matmul(o, xh, wl, start=False, stop=False)
                pe.matmul(o, xl, wh, start=False, stop=True).then_inc(s.pj_ready, 1)

            def take_T(b, k):
                pe.wait_ge(s.T_free, b * T1 + (k + 1))
                return bank_T[k % 2]

            def turn_qk(b, k):
                pe.wait_ge(s.acc_ready, b * 6 + (k + 1))
                bank = take_T(b, k)
                for hp in range(4):
                    ins = turn(bank[:, hp * P:(hp + 1) * P], m.acc[:, k // I, k % I, hp * P:(hp + 1) * P])
                ins.then_inc(s.T_ready, 1)

            def scores(b, h):
                if h == 0:
                    pe.wait_ge(s.T_free, b * T1 + (4 + RING))
                pe.wait_ge(s.nm_ready, b * H1 + (h + 1))
                pe.wait_ge(s.exp_done, b * H1 + (h + 1))
                r = slice(DH1 * (h % 2), DH1 * (h % 2) + DH1)
                for i in range(I):
                    o = bank_S[h % 2][:, i * S:(i + 1) * S]
                    qh, ql = (q[r, h // 2, i * P:(i + 1) * P] for q in (m.qTh, m.qTl))
                    kh, kl = (k[r, h // 2, :] for k in (m.kTh, m.kTl))
                    pe.matmul(o, qh, kh, start=True, stop=False)
                    pe.matmul(o, qh, kl, start=False, stop=False)
                    ins = pe.matmul(o, ql, kh, start=False, stop=True)
                ins.then_inc(s.S_ready, 1)

            def step(b, h, more):
                chunks3 = chunks_of(h) if more else ((), (), ())
                if h + 1 < H1:
                    scores(b, h + 1)
                for c in chunks3[0]:
                    project(b + 1, c)
                if 3 <= h < H1 + 3:
                    g = h - 3
                    pe.wait_ge(s.T_free, b * T1 + (4 + g + 1 + RING))
                    if g == 0:
                        pe.wait_ge(s.v1lo_ready, b * I + I)
                    if g % 2 == 0:
                        pe.wait_ge(s.O_free, b * O1 + (g // 2 + 1))
                    for i in range(I):
                        col = (g % 2 * I + i) * (DH1 + 1)
                        o = bank_O[g // 2 % 2][:, col:col + DH1 + 1]
                        for j in range(I):
                            ph, pl = (p[:, g % 2, j * I + i, :] for p in (m.PTh, m.PTl))
                            vh, vl = (v[:, j, g, :] for v in (m.v1h, m.v1l))
                            pe.matmul(o, ph, vh, start=(j == 0), stop=False)
                            pe.matmul(o, ph, vl, start=False, stop=False)
                            ins = pe.matmul(o, pl, vh, start=False, stop=(j == I - 1))
                    ins.then_inc(s.O_ready, 1)
                for c in chunks3[1]:
                    project(b + 1, c)
                if 1 <= h <= H1:
                    g = h - 1
                    pe.wait_ge(s.exp_done, b * H1 + (g + 1 + RING))
                    bank = take_T(b, 4 + g)
                    for i in range(I):
                        for j in range(I):
                            ins = turn(bank[:, (j * I + i) * P:(j * I + i + 1) * P], m.Pr[:, g % 2, i * S + j * P:i * S + (j + 1) * P])
                    ins.then_inc(s.T_ready, 1)
                for c in chunks3[2]:
                    project(b + 1, c)
                if more:
                    for k in turns_of(h):
                        turn_qk(b + 1, k)

            def turn_z(b, i):
                if isinstance(b, int) and i == 1:
                    pe.wait_ge(s.z_last, 1)
                else:
                    pe.wait_ge(s.z_sum, b * I + (i + 1))
                for c in range(3):
                    w = min(P, E1 * DH1 - c * P)
                    ins = turn(bank_pj[i][0:w, c * P:(c + 1) * P], m.z[:, i, c * P:c * P + w])
                ins.then_inc(s.zT_ready, 1)

            def project_z(b, i):
                pe.wait_ge(s.zT_copied, b * I + (i + 1))
                for c in range(3):
                    w = min(P, E1 * DH1 - c * P)
                    ins = pe.matmul(bank_pj[i][:, 3 * P:3 * P + D], m.zT[0:w, c, :], m.wo0[0:w, c, :], start=(c == 0), stop=(c == 2))
                ins.then_inc(s.wo_ready, 1)

            def turn_latents(batches):
                pe.wait_ge(s.exp_done, B * H1 + RING)
                pe.wait_ge(s.x2n_ready, 2)
                for b in batches:
                    if b >= I:
                        pe.wait_ge(s.lat_ready, b - I + 1)
                    turn_latent(pe, turn, b, bank_S[b % 2])

            for c in range(X1):
                if c in between:
                    between[c]()
                if c % (I * E1) == 0:
                    pe.wait_ge(s.w_split, 2 * chunk(c)[0] + 2)
                project(0, c)
            pe.wait_ge(s.b1T_copied, 1)
            pe.wait_ge(s.O0_free, B)
            pe.wait_ge(s.x1T_lo, B)
            pe.wait_ge(s.g1_exp, B)
            for k in range(4):
                turn_qk(0, k)
            scores(0, 0)
            for h in range(HEAD_STEPS):
                step(0, h, False)
            with pe.Fori(0, B - 1) as b:
                pe.wait_ge(s.x2_ready, b * I + I)
                for h in range(HEAD_STEPS, STEPS):
                    step(b, h, True)
                scores(b + 1, 0)
                for h in range(HEAD_STEPS):
                    step(b + 1, h, False)
                    if h == 3:
                        turn_z(b, 0)
                    if h == 4:
                        project_z(b, 0)
                    if h == 5:
                        turn_z(b, 1)
                        project_z(b, 1)
            for h in range(HEAD_STEPS, STEPS):
                step(B - 1, h, False)
                if h == STEPS - 1:
                    turn_latents(range(B - 1))
            pe.wait_ge(s.x2_ready, B * I)
            for i in range(I):
                turn_z(B - 1, i)
                project_z(B - 1, i)

        def turn_latent(pe, turn, b, bank):
            for i in range(I):
                ins = turn(bank[:, i * P:(i + 1) * P], m.ct[:, b * I + i, :])
            ins.then_inc(s.latT_ready, 1)

        def act_b(act):
            act.sem_inc(s.exp_done, RING)

            def high_qk(b, k):
                act.wait_ge(s.T_ready, b * T1 + (k + 1))
                dst = (m.qTh, m.kTh)[k // I][:, :, (k % I) * P:(k % I + 1) * P]
                act.activation(dst, bank_T[k % 2][:, :].rearrange("p (h c) -> p h c", h=4), ACT.Copy).then_inc(s.T_hi, 1)

            def high_v(b):
                act.wait_ge(s.O_ready, b * H1 + RING)
                for i in range(I):
                    act.wait_ge(s.acc_ready, b * 6 + (4 + i + 1))
                    act.activation(m.v1h[:, i, :, 0:DH1], heads8(m.acc[:, 2, i, :]), ACT.Copy).then_inc(s.v1hi_ready, 1)

            def step(b, h, more):
                if 2 <= h < H1 + 2:
                    g = h - 2
                    act.wait_ge(s.T_ready, b * T1 + (4 + g + 1))
                    act.wait_ge(s.O_ready, b * H1 + (g + 1))
                    act.activation(m.PTh[:, g % 2, :, :].rearrange("p n c -> p (n c)"), bank_T[g % 2][:, :], ACT.Copy).then_inc(s.T_hi, 1)
                if h < H1:
                    act.wait_ge(s.nm_ready, b * H1 + (h + 1 + RING))
                    act.wait_ge(s.T_ready, b * T1 + (4 + h - 1))
                    for i in range(I):
                        ins = act.activation(m.Pr[:, h % 2, i * S:(i + 1) * S], bank_S[h % 2][:, i * S:(i + 1) * S], ACT.Exp,
                                             scale=DH1 ** -0.5, bias=m.nmx[:, h % 4, i:i + 1])
                    ins.then_inc(s.exp_done, 1)
                if more:
                    for k in turns_of(h):
                        high_qk(b + 1, k)

            def copy_z(b, i):
                act.wait_ge(s.zT_ready, b * I + (i + 1))
                act.wait_ge(s.wo_ready, b * I + (i + 1))
                act.activation(m.zT[:, 0:2, :].rearrange("p n c -> p (n c)"), bank_pj[i][:, 0:2 * P], ACT.Copy)
                act.activation(m.zT[0:DH1, 2, :], bank_pj[i][0:DH1, 2 * P:3 * P], ACT.Copy).then_inc(s.zT_copied, 1)

            for k in range(4):
                high_qk(0, k)
            high_v(0)
            for h in range(HEAD_STEPS):
                step(0, h, False)
            with act.Fori(0, B - 1) as b:
                for h in range(HEAD_STEPS, STEPS):
                    step(b, h, True)
                for h in range(HEAD_STEPS):
                    step(b + 1, h, False)
                    if h == 0:
                        high_v(b + 1)
                    if h == 3:
                        copy_z(b, 0)
                    if h == 5:
                        copy_z(b, 1)
            for h in range(HEAD_STEPS, STEPS):
                step(B - 1, h, False)
                if h == STEPS - 1:
                    for b in range(B - 1):
                        latent_high(act, b)
            for i in range(I):
                copy_z(B - 1, i)

        def latent_high(act, b):
            act.wait_ge(s.lat_ready, b + 1)
            act.activation(m.kvTh[:, b, S:2 * S], m.ct[:, b * I:(b + 1) * I, :].rearrange("p i c -> p (i c)"), ACT.Copy).then_inc(s.lat_hi, 1)

        def latent_stats(dve, stats, batches, k):
            tiles = range(batches[0] * I, (batches[-1] + 1) * I)
            if k % 2 == 0:
                dve.wait_ge(s.x2_ready, I + tiles[-1] + 1)
            else:
                dve.wait_ge(s.x2n_ready, k)
            src = m.ct if k % 2 else m.xt
            stats(lambda t: src[:, tiles[t], :], len(tiles), m.st, m.mv, s.x2_var)

        def latent_norm(dve, batches, k):
            tiles = range(batches[0] * I, (batches[-1] + 1) * I)
            src = m.ct if k % 2 else m.xt
            dve.wait_ge(s.x2_var, k + 1)
            dve.wait_ge(s.x2_rstd, k + 1)
            for t in range(len(tiles)):
                ins = dve.tensor_scalar(m.ct[:, tiles[t], :], src[:, tiles[t], :], m.mv[:, t, 0:1], m.rs[:, t:t + 1], ALU.subtract, ALU.mult)
            ins.then_inc(s.x2n_ready, 1)

        def latent_split(dve, b, bank):
            dve.wait_ge(s.latT_ready, b + 1)
            lat = m.ct[:, b * I:(b + 1) * I, :].rearrange("p i c -> p (i c)")
            dve.tensor_scalar(lat, bank[:, 0:S], m.cols[:, 2:3], m.cols[:, 3:4], ALU.mult, ALU.add).then_inc(s.lat_ready, 1)
            dve.wait_ge(s.lat_hi, b + 1)
            dve.tensor_tensor(m.kvTl[:, b, S:2 * S], lat, m.kvTh[:, b, S:2 * S], ALU.subtract).then_inc(s.lat_lo, 1)

        def dve_b(dve, ch, stats, between):
            dve.sem_inc(s.T_free, RING)
            dve.sem_inc(s.O_free, RING)
            dve.sem_inc(s.nm_ready, RING)
            dve.wait_ge(s.gate_ready, 1)

            def gate_products(b, c, group):
                part, i, e = chunk(c)
                sel = G1 if part == 0 else 0
                dve.wait_ge(s.pj_ready, b * X1 + (c + 1))
                if e == 0 and (group >= 2 if isinstance(group, int) else True):
                    dve.wait_ge(s.prod_free, group + (-1))
                k = c // E1 % 2
                g = m.gatev[:, b * I + i, sel:sel + G1].rearrange("p (h e) -> p h e", h=H1)[:, :, e]
                dve.tensor_tensor(heads8(m.prod[:, k, e, :]), heads8(bank_pj[c % 2][:, :]), wide(g, DH1), ALU.mult).then_inc(s.prod_ready, 1)
                if e == E1 - 1:
                    dve.wait_ge(s.prod_ready, b * X1 + (c + 1))
                    dve.tensor_tensor(m.prod[:, k, 3, :], m.prod[:, k, 3, :], m.prod[:, k, 4, :], ALU.add).then_inc(s.pair_ready, 1)

            def split_qk(b, k):
                dve.wait_ge(s.T_hi, b * T1 + (k + 1))
                hi, lo = ((m.qTh, m.qTl), (m.kTh, m.kTl))[k // I]
                r = slice((k % I) * P, (k % I + 1) * P)
                dve.tensor_tensor(lo[:, :, r], bank_T[k % 2][:, :].rearrange("p (h c) -> p h c", h=4), hi[:, :, r], ALU.subtract).then_inc(s.T_free, 1)

            def split_v(b):
                for i in range(I):
                    dve.wait_ge(s.v1hi_ready, b * I + (i + 1))
                    dve.tensor_tensor(m.v1l[:, i, :, 0:DH1], heads8(m.acc[:, 2, i, :]), m.v1h[:, i, :, 0:DH1], ALU.subtract).then_inc(s.v1lo_ready, 1)

            def step(b, h, more):
                chunks3 = chunks_of(h) if more else ((), (), ())
                if h < H1:
                    dve.wait_ge(s.S_ready, b * H1 + (h + 1))
                    ch.link(dve.tensor_reduce(m.nm[:, h % 4, :], bank_S[h % 2][:, :].rearrange("p (i c) -> p i c", i=I), AX.X, ALU.max, negate=True))
                    dve.tensor_scalar(m.nmx[:, h % 4, :], m.nm[:, h % 4, :], DH1 ** -0.5, None, ALU.mult).then_inc(s.nm_ready, 1)
                for c in chunks3[0]:
                    gate_products(b + 1, c, 6 + b * 8 + c // E1)
                if 2 <= h < H1 + 2:
                    g = h - 2
                    dve.wait_ge(s.T_hi, b * T1 + (4 + g + 1))
                    dve.tensor_tensor(m.PTl[:, g % 2, :, :].rearrange("p n c -> p (n c)"), bank_T[g % 2][:, :],
                                      m.PTh[:, g % 2, :, :].rearrange("p n c -> p (n c)"), ALU.subtract).then_inc(s.T_free, 1)
                for c in chunks3[1]:
                    gate_products(b + 1, c, 6 + b * 8 + c // E1)
                if h >= 5 and h % 2 == 1:
                    o = (h - 5) // 2
                    dve.wait_ge(s.O_ready, b * H1 + (2 * o + 2 + RING))
                    O = bank_O[o % 2][:, 0:4 * (DH1 + 1)].rearrange("p (h i c) -> p h i c", h=2, i=I)
                    den = m.den[:, 4 * (o % 2):4 * (o % 2) + 4]
                    ch.link(dve.reciprocal(den.rearrange("p (h i) -> p h i", h=2), O[:, :, :, DH1]))
                    dst = m.ho[:, :, 2 * o * DH1:(2 * o + 2) * DH1].rearrange("p i (h c) -> p h i c", h=2)
                    for hh in range(2):
                        ins = dve.tensor_tensor(dst[:, hh, :, :], O[:, hh, :, 0:DH1], wide(den[:, 2 * hh:2 * hh + 2], DH1), ALU.mult)
                    ins.then_inc(s.O_free, 1)
                for c in chunks3[2]:
                    gate_products(b + 1, c, 6 + b * 8 + c // E1)
                if more:
                    for k in turns_of(h):
                        split_qk(b + 1, k)

            def copies_z(b, i, z_group):
                if i == 0:
                    dve.wait_ge(s.O_free, b * O1 + (O1 + RING))
                dve.wait_ge(s.prod_free, z_group + (-1))
                md = m.topm[:, b * I + i, G1:2 * G1].rearrange("p (h e) -> p h e", h=H1)
                for e in range(E1):
                    ins = dve.tensor_tensor(heads8(m.prod[:, i, e, :]), heads8(m.ho[:, i, :]), wide(md[:, :, e], DH1), ALU.mult)
                ins.then_inc(s.z_ready, 1)

            def add_x2(b, i):
                dve.wait_ge(s.wo_ready, b * I + (i + 1 + 1))
                xi = m.xt[:, b * I + i, :]
                dve.scalar_tensor_tensor(xi, bank_pj[i][:, 3 * P:3 * P + D], m.gf[:, 0:1], xi, ALU.mult, ALU.add).then_inc(s.x2_ready, 1)

            dve.sem_inc(s.x2_ready, I)
            for c in range(X1):
                if c in between:
                    between[c]()
                gate_products(0, c, c // E1)
            dve.wait_ge(s.gate_ready, B)
            dve.wait_ge(s.small2_in, 16 * N_SMALL2)
            for k in range(4):
                split_qk(0, k)
            split_v(0)
            for h in range(HEAD_STEPS):
                step(0, h, False)
            with dve.Fori(0, B - 1) as b:
                ch.loop(b, DVE_STEPS_B)
                for h in range(HEAD_STEPS, STEPS):
                    step(b, h, True)
                z_group = 6 + b * 8 + 6
                copies_z(b, 0, z_group)
                for h in range(HEAD_STEPS):
                    step(b + 1, h, False)
                    if h == 0:
                        copies_z(b, 1, z_group + 1)
                    if h == 1:
                        split_v(b + 1)
                    if h == 5:
                        add_x2(b, 0)
                add_x2(b, 1)
            ch.end_loop(B - 1)
            early = range(B - 1)
            for h in range(HEAD_STEPS, STEPS):
                step(B - 1, h, False)
                k = (h - HEAD_STEPS) // 2
                if h % 2 == 0 and k > 0:
                    latent_norm(dve, early, k - 1)
                if h % 2 == 0 and k < 2:
                    latent_stats(dve, stats, early, k)
            z_group = 6 + (B - 1) * 8
            for i in range(I):
                copies_z(B - 1, i, z_group + i)
            dve.wait_ge(s.z_ready, B * I)
            t = m.prod[:, 1, :, :].rearrange("p e (h c) -> p e h c", h=H1)
            ch.link(dve.tensor_tensor(t[:, :, 0:4, :], t[:, :, 0:4, :], t[:, :, 4:8, :], ALU.add))
            ch.link(dve.tensor_tensor(t[:, :, 0:2, :], t[:, :, 0:2, :], t[:, :, 2:4, :], ALU.add))
            dve.tensor_tensor(m.z[:, 1, :].rearrange("p (e c) -> p e c", e=E1), t[:, :, 0, :], t[:, :, 1, :], ALU.add).then_inc(s.z_last, 1)
            for b in early:
                latent_split(dve, b, bank_S[b % 2])
            for i in range(I):
                add_x2(B - 1, i)

        def pool_b(pool, ch, rstd, split):
            def sums(b, k, group):
                kk = k % 2
                pr, acc = m.prod[:, kk, :, :], m.acc[:, k // I, k % I, :]
                pool.wait_ge(s.prod_ready, b * X1 + (k * E1 + 2))
                if not (isinstance(b, int) and b == 0):
                    if k < 4:
                        pool.wait_ge(s.T_ready, (b + (-1)) * T1 + (k + 1))
                    else:
                        pool.wait_ge(s.v1lo_ready, (b + (-1)) * I + (k - 4 + 1))
                ch.link(pool.tensor_tensor(acc, pr[:, 0, :], pr[:, 1, :], ALU.add))
                pool.wait_ge(s.prod_ready, b * X1 + (k * E1 + 3))
                ch.link(pool.tensor_tensor(acc, acc, pr[:, 2, :], ALU.add))
                pool.wait_ge(s.pair_ready, b * 6 + (k + 1))
                pool.tensor_tensor(acc, acc, pr[:, 3, :], ALU.add).then_inc(s.acc_ready, 1)
                pool.wait_ge(s.acc_ready, b * 6 + (k + 1))
                pool.sem_inc(s.prod_free, 1)

            def latent_rstd(k):
                n = (B - 1) * I if k < 2 else I
                rstd(k + 1, m.mv[:, 0:n, 1], m.rs[:, 0:n], s.x2_var, s.x2_rstd)

            def attend(b, more):
                if more:
                    for k in range(6):
                        sums(b + 1, k, None)
                else:
                    latent_rstd(0)
                    latent_rstd(1)
                for i in range(I if more else 1):
                    pool.wait_ge(s.z_ready, b * I + (i + 1))
                    t = m.prod[:, i, :, :].rearrange("p e (h c) -> p e h c", h=H1)
                    ch.link(pool.tensor_tensor(t[:, :, 0:4, :], t[:, :, 0:4, :], t[:, :, 4:8, :], ALU.add))
                    ch.link(pool.tensor_tensor(t[:, :, 0:2, :], t[:, :, 0:2, :], t[:, :, 2:4, :], ALU.add))
                    pool.tensor_tensor(m.z[:, i, :].rearrange("p (e c) -> p e c", e=E1), t[:, :, 0, :], t[:, :, 1, :], ALU.add).then_inc(s.z_sum, 1)
                    pool.wait_ge(s.z_sum, b * I + (i + 1))
                    pool.sem_inc(s.prod_free, 1)

            for k in range(6):
                sums(0, k, None)
            with pool.Fori(0, B - 1) as b:
                ch.loop(b, POOL_STEPS_B)
                attend(b, True)
            ch.end_loop(B - 1)
            for n in range(N_W0, N_W1):
                split(n)
            attend(B - 1, False)
            return latent_rstd

        HALF = NT // 2

        UN = H2 * I
        SPLIT_AT = UN // 2
        TILES_AO = I * 2
        TC, OC = UN + TILES_AO, HP2
        TURN_AO_AFTER = (3, 4, 6, 7)
        LAT_AT = 3
        ADD_PAIR = 1
        heads2 = lambda a: a.rearrange("p (h c) -> p h c", h=H2 // 2)

        def T_use(u, first):
            seen = TILES_AO if first else sum(after < u for after in TURN_AO_AFTER)
            return u + seen - TILES_AO

        def ao_use(p):
            return TURN_AO_AFTER[p] + 1 + p - TILES_AO

        PJ0, PJ_GROUP = KT + 2, 3
        PJ = UN // 4 * PJ_GROUP

        def pj_use(g, r, last):
            return PJ0 + g * PJ_GROUP + r - (max(0, g - KT) if last else 0)

        def projection(t, last):
            g, r = t // 4, t % 4
            if r == 2 or t >= UN:
                return None
            use = pj_use(g, min(r, 2), last)
            if r < 2:
                return use, "qk", (g + 1) // HP2, (g + 1) % HP2, r
            return use, "v", g // KT, g % KT, 1 - g // KT

        def jobs(t, last):
            job = projection(t, last)
            return [job] if job and not (last and job[2]) else []

        FIRST_JOBS = [(n, "v", 0, n, 0) for n in range(KT - 1)] + [(KT - 1, "qk", 0, 0, 0), (KT, "qk", 0, 0, 1), (KT + 1, "v", 0, KT - 1, 0)]

        def pe_c(pe, turn):
            pe.sem_inc(s.c_T_ready, RING)
            pe.sem_inc(s.c_O_ready, RING)
            pe.wait_ge(s.T_free, B * T1 + RING)
            pe.wait_ge(s.O_free, B * O1 + RING)
            pe.wait_ge(s.x2_ready, I + B * I)
            pe.wait_ge(s.lat_lo, B - 1)
            for n in range(N_W0, N_W1):
                pe.wait_ge(s.w_split, n + 1)
            pe.wait_ge(s.kv_free, 2)

            def three(o, ah, al, bh, bl):
                pe.matmul(o, ah, bh, start=True, stop=False)
                pe.matmul(o, ah, bl, start=False, stop=False)
                return pe.matmul(o, al, bh, start=False, stop=True)

            def project(b, job):
                n, kind, on, a, k = job
                pe.wait_ge(s.c_pj_free, b * PJ + (n + 1))
                if kind == "v":
                    r, w = slice(a * P, (a + 1) * P), slice(k * 512, (k + 1) * 512)
                    ins = three(bank_pj[n % 2][:, :], m.kvTh[:, b + on, r], m.kvTl[:, b + on, r], m.wv1h[:, w], m.wv1l[:, w])
                else:
                    w = slice(a * P, (a + 1) * P)
                    wh, wl = (m.wq1h, m.wq1l) if k == 0 else (m.wk1h, m.wk1l)
                    cols = slice(S, 2 * S) if k == 0 else slice(0, 2 * S)
                    o = bank_pj[n % 2][:, 0:S] if k == 0 else bank_pj[n % 2][:, :]
                    ins = three(o, wh[:, w], wl[:, w], m.kvTh[:, b + on, cols], m.kvTl[:, b + on, cols])
                ins.then_inc(s.c_pj_ready, 1)

            def scores(b, t, last=False):
                hp, hh, i = t // 4, t // 2 % 2, t % 2
                if t % 4 == 0:
                    pe.wait_ge(s.c_pj_free, b * PJ + (pj_use(hp - 1, 1, last) + 1 + RING))
                pe.wait_ge(s.c_max_done, b * UN + (t + 1))
                r, q = slice(DH2 * hh, DH2 * hh + DH2), slice(i * P, (i + 1) * P)
                three(bank_S[t % 2][:, :], m.q2h[r, hp % 2, q], m.q2l[r, hp % 2, q], m.k2h[r, hp % 2, :], m.k2l[r, hp % 2, :])\
                    .then_inc(s.c_S_ready, 1)

            def turn_ao(b, p, use):
                pe.wait_ge(s.c_O_free, b * OC + (-1 + 1 + RING))
                pe.wait_ge(s.c_T_free, b * TC + (use + 1))
                bank = bank_T[use % 2]
                for j in range(4):
                    c = 4 * (p // I) + j
                    ins = turn(bank[:, j * P:(j + 1) * P], m.ao[:, p % I, c * P:(c + 1) * P])
                ins.then_inc(s.c_T_ready, 1)

            def project_ao(b, i, bank):
                pe.wait_ge(s.ao_copied, b * TILES_AO + (i + I + 1 - TILES_AO))
                for c in range(HP2):
                    ins = pe.matmul(bank[:, 4 * (DH2 + 1):4 * (DH2 + 1) + D], m.aoT[:, i, c, :], m.wo1[:, c, :], start=(c == 0), stop=(c == HP2 - 1))
                ins.then_inc(s.c_wo_ready, 1)

            def step(b, t, first=False, last=False):
                if t + 1 < UN or not last:
                    scores(b, t + 1, last)
                for job in jobs(t, last):
                    project(b, job)
                u = t - 3
                if u < UN and (u >= 0 or not first):
                    hp = u // 4
                    pe.wait_ge(s.c_T_free, b * TC + (T_use(u, first) + 1 + RING))
                    if u % 4 == 0:
                        pe.wait_ge(s.c_O_free, b * OC + (hp + 1))
                    if u % 4 == 3 and not first and hp - ADD_PAIR in range(I):
                        project_ao(b, hp - ADD_PAIR, bank_O[hp % 2])
                    o = bank_O[hp % 2][:, (u % 4) * (DH2 + 1):(u % 4 + 1) * (DH2 + 1)]
                    for j in range(KT):
                        ph, pl = (p[:, u % 2, j, :] for p in (m.PTh, m.PTl))
                        vh, vl = (v[:, j, u // 2 % H2, :] for v in (m.v2h, m.v2l))
                        pe.matmul(o, ph, vh, start=(j == 0), stop=False)
                        pe.matmul(o, ph, vl, start=False, stop=False)
                        ins = pe.matmul(o, pl, vh, start=False, stop=(j == KT - 1))
                    ins.then_inc(s.c_O_ready, 1)
                u = t - 1
                if u < UN and (u >= 0 or not first):
                    use = T_use(u, first)
                    pe.wait_ge(s.c_exp_done, b * UN + (u + 1 + RING))
                    pe.wait_ge(s.c_T_free, b * TC + (use + 1))
                    bank = bank_T[use % 2]
                    for j in range(KT):
                        ins = turn(bank[:, j * P:(j + 1) * P], m.Pr[:, u % 2, j * P:(j + 1) * P])
                    ins.then_inc(s.c_T_ready, 1)
                    if not first and u in TURN_AO_AFTER:
                        p = TURN_AO_AFTER.index(u)
                        turn_ao(b, p, ao_use(p))

            for job in FIRST_JOBS:
                project(0, job)
            scores(0, 0)
            for t in range(SPLIT_AT):
                step(0, t, first=True)
                if t == LAT_AT + 1:
                    pe.wait_ge(s.x2n_ready, 4)
                    turn_latent(pe, turn, B - 1, bank_O[1])
                if t == 6:
                    pe.wait_ge(s.lat_lo, B)
            with pe.Fori(0, B - 1) as b:
                for t in range(SPLIT_AT, UN):
                    step(b, t)
                for t in range(SPLIT_AT):
                    step(b + 1, t)
            for t in range(SPLIT_AT, UN + 3):
                step(B - 1, t, last=True)
            for p in range(TILES_AO):
                turn_ao(B, p, p - TILES_AO)
            for i in range(I):
                pe.wait_ge(s.c_O_free, B * OC + (i + 1))
                project_ao(B, i, bank_O[i])

            pe.wait_ge(s.x3n_ready, 1)
            for t in range(NT):
                ins = turn(bank_S[t // HALF][:, t % HALF * P:(t % HALF + 1) * P], m.xn[:, t, :])
                if t % HALF == HALF - 1:
                    ins.then_inc(s.xdT_ready, 1)
            for t in range(NT):
                if t % HALF == 0:
                    pe.wait_ge(s.xd_f32, t // HALF + 1)
                ins = pe.matmul(bank_O[0][:, t * E3:(t + 1) * E3], m.ct[:, t, :], m.gate[:, :], start=True, stop=True)
            ins.then_inc(s.rt_ready, 1)

        def act_c(act):
            act.sem_inc(s.c_exp_done, RING)

            def high(b, job):
                n, kind, on, a, k = job
                act.wait_ge(s.c_pj_ready, b * PJ + (n + 1))
                if kind == "v":
                    dst, src = m.v2h[:, a, k * 8:k * 8 + 8, 0:DH2], heads2(bank_pj[n % 2][:, :])
                    act.wait_ge(s.c_O_ready, b * UN + (UN // 2 * on + RING))
                else:
                    dst, w = ((m.q2h, S), (m.k2h, 2 * S))[k]
                    dst, src = dst[:, a % 2, :], bank_pj[n % 2][:, 0:w]
                act.activation(dst, src, ACT.Copy).then_inc(s.c_pj_hi, 1)

            def copy_ao(b, p, use):
                act.wait_ge(s.c_T_ready, b * TC + (use + 1 + RING))
                c = 4 * (p // I)
                act.activation(m.aoT[:, p % I, c:c + 4, :].rearrange("p n c -> p (n c)"), bank_T[use % 2][:, :], ACT.Copy).then_inc(s.ao_copied, 1)

            def step(b, t, first=False, last=False):
                u = t - 2
                if u < UN and (u >= 0 or not first):
                    use = T_use(u, first)
                    act.wait_ge(s.c_T_ready, b * TC + (use + 1 + RING))
                    act.wait_ge(s.c_O_ready, b * UN + (u + 1))
                    act.activation(m.PTh[:, u % 2, :, :].rearrange("p n c -> p (n c)"), bank_T[use % 2][:, :], ACT.Copy).then_inc(s.c_T_hi, 1)
                if t < UN:
                    act.wait_ge(s.c_max_done, b * UN + (t + 1 + RING))
                    act.wait_ge(s.c_T_ready, b * TC + (T_use(u, first) + 1 + RING))
                    act.activation(m.Pr[:, t % 2, :], m.sm[:, t % 2, :], ACT.Exp, scale=-1.0, bias=m.nm[:, t % 4, 0:1]).then_inc(s.c_exp_done, 1)
                if not first and u in TURN_AO_AFTER:
                    p = TURN_AO_AFTER.index(u)
                    copy_ao(b, p, ao_use(p))
                for job in jobs(t, last):
                    high(b, job)

            for job in FIRST_JOBS:
                high(0, job)
            for t in range(SPLIT_AT):
                step(0, t, first=True)
                if t == LAT_AT + 2:
                    latent_high(act, B - 1)
            with act.Fori(0, B - 1) as b:
                for t in range(SPLIT_AT, UN):
                    step(b, t)
                for t in range(SPLIT_AT):
                    step(b + 1, t)
            for t in range(SPLIT_AT, UN + 2):
                step(B - 1, t, last=True)
            for p in range(TILES_AO):
                copy_ao(B, p, p - TILES_AO)

            for a in range(2):
                act.wait_ge(s.xdT_ready, a + 1)
                tiles = slice(a * HALF, (a + 1) * HALF)
                act.activation(m.ct[:, tiles, :].rearrange("p t c -> p (t c)"), bank_S[a][:, :], ACT.Copy).then_inc(s.xd_f32, 1)
                act.activation(m.xdTh[:, tiles, :].rearrange("p t c -> p (t c)"), bank_S[a][:, :], ACT.Copy).then_inc(s.xd_hi, 1)
            act.wait_ge(s.rt_nmax, 1)
            act.activation(m.ex8[:, :, :], m.lgm[:, :, :], ACT.Exp).then_inc(s.rt_exp, 1)

        def dve_c(dve, ch, stats):
            dve.sem_inc(s.c_pj_free, RING)
            dve.sem_inc(s.c_max_done, RING)
            dve.sem_inc(s.c_T_free, RING)
            dve.sem_inc(s.c_O_free, RING)
            dve.wait_ge(s.maskb_ready, 1)
            dve.wait_ge(s.v2_ones, 1)
            dve.wait_ge(s.tanh_ready, 1)

            def low(b, job):
                n, kind, on, a, k = job
                dve.wait_ge(s.c_pj_hi, b * PJ + (n + 1))
                if kind == "v":
                    v = (slice(None), a, slice(k * 8, k * 8 + 8), slice(0, DH2))
                    dst, src, hi = m.v2l[v], heads2(bank_pj[n % 2][:, :]), m.v2h[v]
                else:
                    hi, lo, w = ((m.q2h, m.q2l, S), (m.k2h, m.k2l, 2 * S))[k]
                    dst, src, hi = lo[:, a % 2, :], bank_pj[n % 2][:, 0:w], hi[:, a % 2, :]
                dve.tensor_tensor(dst, src, hi, ALU.subtract).then_inc(s.c_pj_free, 1)

            def take_mask(b):
                dve.wait_ge(s.c_max_done, b * UN + RING)
                dve.tensor_copy(m.maskrow[:, :], m.maskb[:, b, :]).then_inc(s.maskrow_ready, 1)
                dve.wait_ge(s.maskrow_ready, b + 1)

            def free_ao(b, p, use):
                dve.wait_ge(s.c_T_free, b * TC + (use + RING))
                dve.wait_ge(s.ao_copied, b * TILES_AO + (p + 1 - TILES_AO))
                dve.sem_inc(s.c_T_free, 1)

            def add_x3(b, i, bank):
                dve.wait_ge(s.c_wo_ready, b * I + (i + 1 - I))
                xi = m.xt[:, b * I + (i - I), :]
                return dve.scalar_tensor_tensor(xi, bank[:, 4 * (DH2 + 1):4 * (DH2 + 1) + D], m.gx[:, 1:2], xi, ALU.mult, ALU.add)

            def step(b, t, first=False, last=False):
                if t < UN:
                    dve.wait_ge(s.c_S_ready, b * UN + (t + 1))
                    dve.wait_ge(s.c_exp_done, b * UN + (t + 1))
                    settle(dve, s.settled_dve)
                    dve.tensor_tensor_reduce(m.sm[:, t % 2, :], bank_S[t % 2][:, :], m.maskrow[:, :], -(DH2 ** -0.5), 3e38,
                                             ALU.add, ALU.min, m.nm[:, t % 4, 0:1]).then_inc(s.c_max_done, 1)
                u = t - 2
                if u < UN and (u >= 0 or not first):
                    use = T_use(u, first)
                    dve.wait_ge(s.c_T_hi, b * UN + (u + 1))
                    dve.tensor_tensor(m.PTl[:, u % 2, :, :].rearrange("p n c -> p (n c)"), bank_T[use % 2][:, :],
                                      m.PTh[:, u % 2, :, :].rearrange("p n c -> p (n c)"), ALU.subtract).then_inc(s.c_T_free, 1)
                for job in jobs(t, last):
                    low(b, job)
                if not first and u in TURN_AO_AFTER:
                    p = TURN_AO_AFTER.index(u)
                    free_ao(b, p, ao_use(p))
                hp = (t - 7) // 4
                if t % 4 == 3 and (hp >= 0 or not first):
                    dve.wait_ge(s.c_O_ready, b * UN + (4 * hp + 4 + RING))
                    O = bank_O[hp % 2][:, 0:4 * (DH2 + 1)].rearrange("p (h i c) -> p h i c", h=2, i=I)
                    den = m.den[:, 4 * (hp % 2):4 * (hp % 2) + 4]
                    ch.link(dve.reciprocal(den.rearrange("p (h i) -> p h i", h=2), O[:, :, :, DH2]))
                    at = hp % HP2 * P
                    dst = m.ao[:, :, at:at + P].rearrange("p i (h c) -> p h i c", h=2)
                    for hh in range(2):
                        ins = dve.tensor_tensor(dst[:, hh, :, :], O[:, hh, :, 0:DH2], wide(den[:, 2 * hh:2 * hh + 2], DH2), ALU.mult)
                    if not first and t < SPLIT_AT and hp - ADD_PAIR in range(I):
                        ins = add_x3(b, hp - ADD_PAIR, bank_O[hp % 2])
                    ins.then_inc(s.c_O_free, 1)

            for job in FIRST_JOBS:
                low(0, job)
            take_mask(0)
            for t in range(SPLIT_AT):
                step(0, t, first=True)
                if LAT_AT - 2 <= t <= LAT_AT:
                    if t > LAT_AT - 2:
                        latent_norm(dve, [B - 1], 1 + t - LAT_AT + 2)
                    if t < LAT_AT:
                        latent_stats(dve, stats, [B - 1], 2 + t - LAT_AT + 2)
                if t == LAT_AT + 2:
                    latent_split(dve, B - 1, bank_O[1])
            with dve.Fori(0, B - 1) as b:
                ch.loop(b, DVE_STEPS_C)
                for t in range(SPLIT_AT, UN):
                    step(b, t)
                take_mask(b + 1)
                for t in range(SPLIT_AT):
                    step(b + 1, t)
            ch.end_loop(B - 1)
            for t in range(SPLIT_AT, UN + 4):
                step(B - 1, t, last=True)
            for p in range(TILES_AO):
                free_ao(B, p, p - TILES_AO)
            for i in range(I):
                ins = add_x3(B, i, bank_O[i])
            ch.link(ins)

            stats(lambda t: m.xt[:, t, :], NT, m.st, m.mv, s.x3_var)
            dve.wait_ge(s.x3_var, 1)
            dve.wait_ge(s.x3_rstd, 1)
            for t in range(NT):
                ins = dve.tensor_scalar(m.xn[:, t, :], m.xt[:, t, :], m.mv[:, t, 0:1], m.rs[:, t:t + 1], ALU.subtract, ALU.mult)
            ins.then_inc(s.x3n_ready, 1)
            for a in range(2):
                dve.wait_ge(s.xd_hi, a + 1)
                tiles = slice(a * HALF, (a + 1) * HALF)
                dve.tensor_tensor(m.xdTl[:, tiles, :].rearrange("p t c -> p (t c)"), bank_S[a][:, :],
                                  m.xdTh[:, tiles, :].rearrange("p t c -> p (t c)"), ALU.subtract).then_inc(s.xd_lo, 1)
            dve.wait_ge(s.rt_ready, 1)
            ch.link(dve.tensor_copy(m.lg[:, :, :].rearrange("p t e -> p (t e)"), bank_O[0][:, 0:NT * E3]))
            for t in range(NT):
                ins = dve.max(m.m8[:, t, :], m.lg[:, t, :])
            ch.link(ins)
            dve.tensor_tensor(m.lgm[:, :, :], m.lg[:, :, :], m.m8[:, :, 0:1].to_broadcast([P, NT, E3]), ALU.subtract).then_inc(s.rt_nmax, 1)
            for t in range(NT):
                ins = dve.max_index(m.ix8[:, t, :], m.m8[:, t, :], m.lg[:, t, :])
            ch.link(ins)
            ch.link(dve.tensor_copy(m.ixf[:, :], m.ix8[:, :, 0]))
            ch.link(dve.tensor_tensor(m.we1[:, :, :], m.iota_f[:, :].unsqueeze(1).to_broadcast([P, NT, E3]), wide(m.ixf[:, :], E3), ALU.is_equal))
            dve.wait_ge(s.rt_exp, 1)
            ch.link(dve.tensor_reduce(m.sum8[:, :], m.ex8[:, :, :], AX.X, ALU.add))
            ch.link(dve.reciprocal(m.wmax[:, :], m.sum8[:, :]))
            ch.link(dve.tensor_scalar(m.wmax[:, :], m.wmax[:, :], m.gf[:, 1:2], None, ALU.mult))
            dve.tensor_tensor(m.we[:, :, :].rearrange("p e t -> p t e"), m.we1[:, :, :], wide(m.wmax[:, :], E3), ALU.mult).then_inc(s.we_ready, 1)
            for a in range(2):
                dve.wait_ge(s.weT_ready, a + 1)
                dve.tensor_copy(m.weT[:, a * HALF:(a + 1) * HALF, :].rearrange("p t c -> p (t c)"), bank_T[a][0:E3, :]).then_inc(s.weT_copied, 1)
            dve.wait_ge(s.we_ready, 1)

        def pool_c(pool, ch, rstd, split, latent_rstd):
            pool.wait_ge(s.z_sum, B * I - 1)
            pool.wait_ge(s.z_last, 1)
            pool.memset(m.v2h[:, :, :, DH2], 1.0)
            pool.memset(m.v2l[:, :, :, DH2], 0.0).then_inc(s.v2_ones, 1)
            latent_rstd(2)
            latent_rstd(3)
            pool.wait_ge(s.pj_ready, B * X1)
            for n in range(N_W1, N_WALL):
                split(n)
            rstd(1, m.mv[:, :, 1], m.rs[:, :], s.x3_var, s.x3_rstd)

        YR = 4
        HR = 4
        bank_h, bank_y = bk[0:HR], bk[4:8]

        def pe_d(pe, turn):
            pe.wait_ge(s.c_pj_free, B * PJ + RING)
            pe.wait_ge(s.c_T_free, B * TC + RING)
            pe.wait_ge(s.xd_lo, 2)
            for n in range(N_W1, N_WALL):
                pe.wait_ge(s.w_split, n + 1)

            def hidden(e, a):
                for f in range(FT):
                    use = a * FT + f
                    pe.wait_ge(s.gelu_done, e * 2 * FT + (use + 1))
                    o, w = bank_h[use % HR][:, :], slice(f * P, (f + 1) * P)
                    xh, xl = (x_[:, a * HALF:(a + 1) * HALF, :].rearrange("p t c -> p (t c)") for x_ in (m.xdTh, m.xdTl))
                    pe.matmul(o, m.w1h[:, e, w], xh, start=True, stop=False)
                    pe.matmul(o, m.w1h[:, e, w], xl, start=False, stop=False)
                    pe.matmul(o, m.w1l[:, e, w], xh, start=False, stop=True).then_inc(s.h_ready, 1)

            def outputs(e, a):
                for t in range(HALF):
                    use = a * HALF + t
                    pe.wait_ge(s.y_free, e * NT + (NT + use + 1))
                    o = bank_y[use % YR][:, 0:D]
                    for f in range(FT):
                        if t == 0:
                            pe.wait_ge(s.h_lo, e * 2 * FT + (a * FT + f + 1 + HR))
                        hh, hl = (h_[:, a, f, t * P:(t + 1) * P] for h_ in (m.hTh, m.hTl))
                        pe.matmul(o, hh, m.w2h[:, e, f, :], start=(f == 0), stop=False)
                        pe.matmul(o, hh, m.w2l[:, e, f, :], start=False, stop=False)
                        ins = pe.matmul(o, hl, m.w2h[:, e, f, :], start=False, stop=(f == FT - 1))
                    ins.then_inc(s.y_ready, 1)

            hidden(0, 0)
            pe.wait_ge(s.we_ready, 1)
            for t in range(NT):
                ins = turn(bank_T[t // HALF][0:E3, t % HALF * P:(t % HALF + 1) * P], m.we[:, :, t])
                if t % HALF == HALF - 1:
                    ins.then_inc(s.weT_ready, 1)
            pe.wait_ge(s.weT_copied, 2)
            for t in range(NT):
                pe.wait_ge(s.y_free, t + 1)
                pe.matmul(bank_y[t % YR][:, 0:D], m.weT[:, t, :], m.b2[:, :], start=True, stop=True).then_inc(s.y_ready, 1)
            with pe.Fori(0, E3 - 1) as e:
                hidden(e, 1)
                outputs(e, 0)
                hidden(e + 1, 0)
                outputs(e, 1)
            hidden(E3 - 1, 1)
            outputs(E3 - 1, 0)
            outputs(E3 - 1, 1)

        def act_d(act):
            act.sem_inc(s.gelu_done, HR)
            with act.Fori(0, E3) as e:
                for use in range(2 * FT):
                    act.wait_ge(s.h_ready, e * 2 * FT + (use + 1))
                    act.wait_ge(s.h_lo, e * 2 * FT + (use + 1))
                    settle(act, s.settled_act)
                    act.activation(m.hf[:, use % HR, :], bank_h[use % HR][:, :], ACT.Gelu, bias=m.b1T[:, e, use % FT:use % FT + 1]).then_inc(s.gelu_done, 1)

        def pool_d(pool):
            pool.wait_ge(s.c_O_ready, B * UN + RING)
            with pool.Fori(0, E3) as e:
                for use in range(2 * FT):
                    pool.wait_ge(s.gelu_done, e * 2 * FT + (use + 1 + HR))
                    if use % FT == 0:
                        pool.wait_ge(s.y_ready, e * NT + (use // FT * HALF + HALF))
                    settle(pool, s.settled_pool)
                    pool.tensor_scalar(m.hTh[:, use // FT, use % FT, :], m.hf[:, use % HR, :], 1.0, 0.0, ALU.mult, ALU.add).then_inc(s.h_hi, 1)

        def dve_d(dve, ch):
            dve.sem_inc(s.h_lo, HR)
            dve.sem_inc(s.y_free, YR)

            def low(e, a):
                for f in range(FT):
                    use = a * FT + f
                    dve.wait_ge(s.h_hi, e * 2 * FT + (use + 1))
                    dve.tensor_tensor(m.hTl[:, a, f, :], m.hf[:, use % HR, :], m.hTh[:, a, f, :], ALU.subtract).then_inc(s.h_lo, 1)

            def add(e, a):
                for t in range(a * HALF, (a + 1) * HALF):
                    dve.wait_ge(s.y_ready, e * NT + (NT + t + 1))
                    dve.scalar_tensor_tensor(m.xt[:, t, :], bank_y[t % YR][:, 0:D], m.we[:, e, t:t + 1], m.xt[:, t, :], ALU.mult, ALU.add)\
                        .then_inc(s.y_free, 1)

            for t in range(NT):
                dve.wait_ge(s.y_ready, t + 1)
                dve.tensor_tensor(m.xt[:, t, :], m.xt[:, t, :], bank_y[t % YR][:, 0:D], ALU.add).then_inc(s.y_free, 1)
            low(0, 0)
            with dve.Fori(0, E3 - 1) as e:
                low(e, 1)
                add(e, 0)
                low(e + 1, 0)
                add(e, 1)
            low(E3 - 1, 1)
            add(E3 - 1, 0)
            add(E3 - 1, 1)

        @block.sync
        def _(sp):
            sp.dma_start(m.xt[:, :, :], xf).then_inc(s.x_in, 16)
            sp.dma_start(m.ct[:, :, :], cf).then_inc(s.ctx_in, 16)
            for n, (src, w, _, _) in enumerate(chunks):
                if n >= N_STAGE:
                    sp.wait_ge(s.w_split, n - N_STAGE + 1)
                dst = m.stage[:, n % N_STAGE, 0:w]
                if len(src.shape) == 3:
                    dst = dst.rearrange("p (e n) -> p e n", e=src.shape[1])
                sp.dma_start(dst, src).then_inc(stage_in[n % N_STAGE], 16)
            sp.wait_ge(s.out_ready, 1)
            sp.dma_start(outf, m.xt[:, :, :]).then_inc(s.out_done, 16)
            sp.wait_ge(s.out_done, 16)

        @block.scalar
        def _(act):
            SMALL = [(m.wi_row[:, :], w_i), (m.wf_row[:, :], w_f),
                     (m.bi[:, :], b_i.partition_broadcast(P)), (m.bf[:, :], b_f.partition_broadcast(P)),
                     (m.lnw[:, :], ln_w.partition_broadcast(P)), (m.gx[:, :], g_x.partition_broadcast(P)),
                     (m.gf[:, :], g_f.partition_broadcast(P)),
                     (m.cols[:, 0:1], gm.rearrange("(p a) -> p a", a=1)), (m.cols[:, 1:2], bm.rearrange("(p a) -> p a", a=1)),
                     (m.wsd[:, 0:G1], Ws), (m.wsd[:, G1:2 * G1], Wd)]
            for dst, src in SMALL:
                act.dma_start(dst, src).then_inc(s.small_in, 16)
            for c, v in enumerate((gl, bl)):
                act.dma_start(m.cols[:, 2 + c:3 + c], v.rearrange("(p a) -> p a", a=1)).then_inc(s.small2_in, 16)
            act.dma_start(m.mask_u8[:, :, :], mask.partition_broadcast(P)).then_inc(s.small2_in, 16)
            wo = Wo0.rearrange("d (e n) -> e d n", e=E1)
            for e in range(E1):
                act.dma_start(m.wo0[DH1 * (e % 2):DH1 * (e % 2) + DH1, e // 2, :], wo[e, :, :]).then_inc(s.small2_in, 16)
            act.dma_start(m.wo1[:, :, :], Wo1.rearrange("(t p) n -> p t n", p=P)).then_inc(s.small2_in, 16)
            act.dma_start(m.gate[:, :], gate_w).then_inc(s.small2_in, 16)
            act.dma_start(m.b1_row[:, :], b1.rearrange("e (f p) -> (e f) p", p=P)).then_inc(s.small2_in, 16)
            act.dma_start(m.b2[:, :], b2).then_inc(s.small2_in, 16)

            act.wait_ge(s.small_in, 16 * N_SMALL)
            act.activation(m.gx[:, :], m.gx[:, :], ACT.Tanh)
            act.activation(m.gf[:, :], m.gf[:, :], ACT.Tanh).then_inc(s.tanh_ready, 1)
            for j in range(2):
                act.wait_ge(s.xT_ready, j + 1)
                act.activation(m.xnT[:, 4 * j:4 * j + 4, :].rearrange("p t c -> p (t c)"), bk[j][:, :], ACT.Copy).then_inc(s.xT_copied, 1)
            act.wait_ge(s.gates_b, 1)
            act.activation(m.tmp_a[:, :, :, :], m.fg[:, :, :, :], ACT.Abs).then_inc(s.act_chain, 1)
            act.wait_ge(s.act_chain, 1)
            act.activation(m.tmp_b[:, :, :, :], m.tmp_a[:, :, :, :], ACT.Exp, scale=-1.0).then_inc(s.act_chain, 1)
            act.wait_ge(s.act_chain, 2)
            act.activation(m.tmp_a[:, :, :, :], m.tmp_b[:, :, :, :], ACT.Ln, bias=1.0).then_inc(s.softplus, 1)
            for j in range(2):
                act.wait_ge(s.cn_T, j + 1)
                act.activation(m.sm[:, j, :], bk[j][:, :], ACT.Identity, scale=m.cols[:, 0:1], bias=m.cols[:, 1:2]).then_inc(s.kv_f, 1)
            act.wait_ge(s.mlog_ready, 1)
            act.activation(m.en[:, :, :, :], m.mlog[:, :, :, :], ACT.Exp, scale=-1.0).then_inc(s.en_ready, 1)

            def decay(u):
                b, h = divmod(u, NH0)
                act.wait_ge(s.L_ready, u + 1)
                if u >= 2:
                    act.wait_ge(s.C_ready, u - 1)
                act.activation(m.Dm[:, u % 2, 0:S], bk[u % 2][:, 0:S], ACT.Exp, scale=-1.0, bias=m.at[:, 0, b, h:h + 1])
                act.activation(m.Dm[:, u % 2, S:W0], bk[u % 2][:, S:W0], ACT.Exp, scale=-1.0, bias=m.at[:, 1, b, h:h + 1]).then_inc(s.D_ready, 1)

            def after_x1(b):
                act.wait_ge(s.x1T_ready, b + 1)
                if b >= 1:
                    act.wait_ge(s.g1_ready, b)
                src = bk[6][:, 0:S]
                act.activation(m.xT32[:, :, :].rearrange("p i c -> p (i c)"), src, ACT.Copy).then_inc(s.x1T_f32, 1)
                act.activation(m.xbTh[:, I * b:I * b + I, :].rearrange("p i c -> p (i c)"), src, ACT.Copy).then_inc(s.x1T_hi, 1)

            def gate_exp(b):
                act.wait_ge(s.g1_ready, b + 1)
                if b >= 1:
                    act.wait_ge(s.gate_ready, b)
                act.activation(m.sg[:, :, :].rearrange("p i g -> p (i g)"), bk[7][:, 0:I * 2 * G1], ACT.Exp, scale=-1.0).then_inc(s.g1_exp, 1)

            def normaliser(b):
                act.wait_ge(s.C_free, NH0 * (b + 1))
                if b >= 1:
                    act.wait_ge(s.O0_free, b)
                act.activation(m.absc[:, :], bk[4 + b % 2][:, 0:264].rearrange("p (n c) -> p n c", c=33)[:, :, 32], ACT.Abs).then_inc(s.absc_ready, 1)

            for u in range(UNITS):
                decay(u)
                b, r = divmod(u, NH0)
                if r == 0 and b >= 1:
                    normaliser(b - 1)
                if r == 3 and b >= 1:
                    after_x1(b - 1)
                if r == 0 and b >= 2:
                    gate_exp(b - 2)
            gate_exp(B - 2)
            normaliser(B - 1)
            after_x1(B - 1)
            gate_exp(B - 1)
            act_b(act)
            act_c(act)
            act_d(act)

        @block.gpsimd
        def _(pool):
            ch = Chain(pool, s.pool_chain)
            ch.link(pool.memset(m.ident[:, :], 0.0))
            pool.affine_select(out=m.ident[:, :], in_=m.ident[:, :], compare_op=ALU.not_equal, fill=1.0, base=0,
                               pattern=[[-1, P]], channel_multiplier=1).then_inc(s.const, 1)
            pool.memset(m.mhalf[:, :], -0.5)
            pool.memset(m.identb[:, :], 0.0)
            pool.memset(m.tri[:, :], 1.0)
            pool.memset(m.sel3[:, :], 0.0)
            pool.memset(m.a3[:, :, :], 0.0)
            pool.memset(m.M3[:, :], 0.0)
            ch.link(pool.memset(m.causal[:, :], 0.0))

            def rstd(k, src, dst, ready, done, n=None):
                pool.wait_ge(ready, k)
                settle(pool, s.settled_pool)
                ch.link(pool.tensor_scalar(dst, src, 1.0, EPS, ALU.mult, ALU.add))
                pool.tensor_tensor(dst, dst, m.mhalf[:, 0:dst.shape[1]], ALU.pow).then_inc(done, 1)

            rstd(1, m.mv[:, :, 1], m.rs[:, :], s.x_var, s.x_rstd)
            rstd(2, m.mv2[:, :, 1], m.rs2[:, :], s.x_var, s.x_rstd)
            pool.memset(m.ones[:, :], 1.0)
            pool.memset(m.zero16[:, :], 0.0)
            pool.affine_select(out=m.identb[:, :], in_=m.identb[:, :], compare_op=ALU.not_equal, fill=1.0, base=0,
                               pattern=[[-1, P]], channel_multiplier=1)
            for part in range(3):
                ins = pool.affine_select(out=m.sel3[:, :], in_=m.sel3[:, :], compare_op=ALU.not_equal, fill=1.0,
                                         base=-PART_AT * part, pattern=[[-1, PART_AT]], channel_multiplier=1)
                ch.link(ins)
            pool.affine_select(out=m.tri[:, :], in_=m.tri[:, :], compare_op=ALU.is_ge, fill=0.0, base=0,
                               pattern=[[1, P]], channel_multiplier=-1)
            for c in (0, S):
                pool.affine_select(out=m.causal[:, c:c + P], in_=m.causal[:, c:c + P], compare_op=ALU.is_ge, fill=BIG,
                                   base=0, pattern=[[1, P]], channel_multiplier=-1)
            pool.memset(m.vx[:, :, :, :], 1.0).then_inc(s.const, 1)
            pool.wait_ge(s.const, 2)
            pool.tensor_scalar(m.vx[:, :, :, 0:DH0], m.ct[:, :, :].rearrange("p t (h c) -> p t h c", h=NH0), 1.0, 0.0,
                               ALU.mult, ALU.add).then_inc(s.vx_ready, 1)

            def split(n):
                src, w, hi, lo = chunks[n]
                raw = m.stage[:, n % N_STAGE, 0:w]
                if len(src.shape) == 3:
                    raw = raw.rearrange("p (e n) -> p e n", e=src.shape[1])
                pool.wait_ge(stage_in[n % N_STAGE], 16 * (n // N_STAGE + 1))
                pool.tensor_scalar(hi, raw, 1.0, 0.0, ALU.mult, ALU.add).then_inc(s.w_hi, 1)
                pool.wait_ge(s.w_hi, n + 1)
                pool.tensor_tensor(lo, raw, hi, ALU.subtract).then_inc(s.w_split, 1)

            for j in range(2):
                pool.wait_ge(s.kv_f, j + 1)
                src = m.sm[:, j, :].rearrange("p (b c) -> p b c", b=2)
                hi, lo = m.kvTh[:, 2 * j:2 * j + 2, 0:S], m.kvTl[:, 2 * j:2 * j + 2, 0:S]
                ch.link(pool.tensor_scalar(hi, src, 1.0, 0.0, ALU.mult, ALU.add))
                pool.tensor_tensor(lo, src, hi, ALU.subtract).then_inc(s.kv_free, 1)
            for n in range(3):
                split(n)
            for b in range(B):
                rstd(b + 1, m.v32[:, :], m.r32[:, :], s.var0, s.rstd0)
                rstd(b + 1, m.mv[:, 0:I, 1], m.rs[:, 0:I], s.x1_var, s.x1_rstd)
                if b < 3:
                    split(3 + b)
            pool.memset(m.maskb[:, :, S:2 * S], 0.0)
            pool.wait_ge(s.small2_in, 16 * N_SMALL2)
            pool.tensor_scalar(m.maskb[:, :, 0:S], m.mask_u8[:, :, :], BIG, -BIG, ALU.mult, ALU.add).then_inc(s.maskb_ready, 1)
            pool.iota(m.iota_i[:, :], pattern=[[1, E3]], base=0, channel_multiplier=0).then_inc(s.const, 1)
            pool.wait_ge(s.const, 3)
            pool.tensor_copy(m.iota_f[:, :], m.iota_i[:, :])
            pool.memset(m.v1h[:, :, :, DH1], 1.0)
            pool.memset(m.v1l[:, :, :, DH1], 0.0).then_inc(s.const, 1)
            latent_rstd = pool_b(pool, ch, rstd, split)
            pool_c(pool, ch, rstd, split, latent_rstd)
            pool_d(pool)

        @block.tensor
        def _(pe):
            def turn(dst, src):
                return pe.transpose(dst, src, m.ident[0:src.shape[0], 0:src.shape[0]])

            pe.wait_ge(s.const, 1)
            pe.wait_ge(s.small_in, 16 * N_SMALL)
            for c in range(3):
                for g, row in enumerate((m.wi_row, m.wf_row)):
                    t = turn(bk[7][:, c * 8 + 4 * g:c * 8 + 4 * g + 4], row[:, c * D:(c + 1) * D])
            t.then_inc(s.wg_T, 1)
            pe.wait_ge(s.ctx_in, 16)
            for t in range(NT):
                ins = turn(bk[2 + t // 4][:, t % 4 * P:(t % 4 + 1) * P], m.ct[:, t, :])
                if t % 4 == 3:
                    ins.then_inc(s.cT_ready, 1)
            for t in range(NT):
                pe.wait_ge(s.xn_ready, t + 1)
                ins = turn(bk[t // 4][:, t % 4 * P:(t % 4 + 1) * P], m.xn[:, t, :])
                if t % 4 == 3:
                    ins.then_inc(s.xT_ready, 1)
            pe.wait_ge(s.wg_ready, 1)
            pe.wait_ge(s.cT_copied, 2)
            pe.wait_ge(s.xT_copied, 2)
            for t in range(NT):
                g = bk[6][:, t * 8:t * 8 + 8]
                pe.matmul(g, m.xnT[:, t, :], m.wg[:, 0, :], start=True, stop=False)
                ins = pe.matmul(g, m.cT[:, t, :], m.wg_ctx[:, :], start=False, stop=True)
            ins.then_inc(s.gates, 1)
            pe.wait_ge(s.xn_ready, NT + 1)
            for t in range(NT):
                ins = turn(bk[t // 4][:, t % 4 * P:(t % 4 + 1) * P], m.xn[:, t, :])
                if t % 4 == 3:
                    ins.then_inc(s.cn_T, 1)
            pe.wait_ge(s.const, 2)
            pe.wait_ge(s.logf_ready, 1)
            lf = [m.logf[:, i, :, :].rearrange("p b h -> p (b h)") for i in range(I)]
            pe.matmul(bk[7][:, 0:16], m.tri[:, :], lf[0], start=True, stop=True)
            pe.matmul(bk[7][:, 16:32], m.tri[:, :], lf[1], start=True, stop=False)
            pe.matmul(bk[7][:, 16:32], m.ones[:, :], lf[0], start=False, stop=True).then_inc(s.F_ready, 1)
            pe.wait_ge(s.a_ready, 1)
            for i in range(I):
                ins = turn(bk[7][0:M_ROWS, 128 + i * P:128 + (i + 1) * P], m.a3[:, i, :])
            ins.then_inc(s.aT_ready, 1)
            pe.wait_ge(s.M_ready, 1)
            for i in range(I):
                ins = turn(bk[6][:, 128 + 16 * i:144 + 16 * i], m.M16[0:UNITS, i * P:(i + 1) * P])
            ins.then_inc(s.Mt_ready, 1)

            pe.wait_ge(s.M3_ready, 1)
            pe.wait_ge(s.kv_f, 2)

            def scores(u):
                b, h = divmod(u, NH0)
                if u >= 2:
                    pe.wait_ge(s.D_ready, u - 1)
                L = bk[u % 2][:, 0:W0]
                pe.matmul(L, m.sel3[:, u:u + 1].to_broadcast([M_ROWS, P]), m.M3[:, :], start=True, stop=False)
                for c in (0, S):
                    ins = pe.matmul(L[:, c:c + P], m.identb[:, :], m.causal[:, c:c + P], start=False, stop=(c == S))
                ins.then_inc(s.L_ready, 1)
                if u >= 2:
                    pe.wait_ge(s.C_ready, u - 1)
                r = slice(DH0 * h, DH0 * (h + 1))
                q = m.xnT[r, I * b:I * b + I, :].rearrange("p i c -> p (i c)")
                Sb = bk[2 + u % 2]
                pe.matmul(Sb[:, 0:S], m.cT[r, I * b, :], q, start=True, stop=True)
                pe.matmul(Sb[:, S:W0], m.cT[r, I * b + 1, :], m.xnT[r, I * b + 1, :], start=True, stop=True).then_inc(s.S0_ready, 1)

            def values(u):
                b, h = divmod(u, NH0)
                if h == 0 and b >= 2:
                    pe.wait_ge(s.O0_free, b - 1)
                pe.wait_ge(s.C_ready, u + 1)
                C = m.C[:, u % 2, :]
                O = bk[4 + b % 2][:, 0:264].rearrange("p (i h c) -> p i h c", i=I, h=NH0)
                pe.matmul(O[:, 0, h, :], C[:, 0:P], m.vx[:, I * b, h, :], start=True, stop=True)
                pe.matmul(O[:, 1, h, :], C[:, P:S], m.vx[:, I * b, h, :], start=True, stop=False)
                ins = pe.matmul(O[:, 1, h, :], C[:, S:W0], m.vx[:, I * b + 1, h, :], start=False, stop=True)
                ins.then_inc(s.C_free, 1)

            def x1_turn(b):
                pe.wait_ge(s.x1n_ready, b + 1)
                if b >= 1:
                    pe.wait_ge(s.x1T_lo, b)
                if b == 0:
                    pe.wait_ge(s.mlog_ready, 1)
                for i in range(I):
                    ins = turn(bk[6][:, i * P:(i + 1) * P], m.n2[:, i, :])
                ins.then_inc(s.x1T_ready, 1)

            def x1_gates(b):
                pe.wait_ge(s.x1T_f32, b + 1)
                if b >= 1:
                    pe.wait_ge(s.g1_exp, b)
                for i in range(I):
                    ins = pe.matmul(bk[7][:, i * 2 * G1:(i + 1) * 2 * G1], m.xT32[:, i, :], m.wsd[:, :], start=True, stop=True)
                ins.then_inc(s.g1_ready, 1)

            pe.wait_ge(s.vx_ready, 1)
            scores(0)
            for u in range(UNITS):
                if u + 1 < UNITS:
                    scores(u + 1)
                values(u)
                b, r = divmod(u, NH0)
                if r == 3 and b >= 1:
                    x1_turn(b - 1)
                if r == 0 and b >= 2:
                    x1_gates(b - 2)

            def b1_turn():
                pe.wait_ge(s.small2_in, 16 * N_SMALL2)
                pe.wait_ge(s.C_ready, UNITS)
                turn(bk[2][:, 0:E3 * FT], m.b1_row[:, :]).then_inc(s.b1T_ready, 1)

            pe.wait_ge(s.D_ready, UNITS)
            pe_b(pe, turn, {0: lambda: x1_gates(B - 2), 2: b1_turn, 8: lambda: x1_turn(B - 1), 12: lambda: x1_gates(B - 1)})
            pe_c(pe, turn)
            pe_d(pe, turn)

        @block.vector
        def _(dve):
            ch = Chain(dve, s.dve_chain)

            def stats(src, n, st, mv, done):
                settle(dve, s.settled_dve)
                for t in range(n):
                    ins = dve.bn_stats(st[:, t, :], src(t))
                ch.link(ins)
                settle(dve, s.settled_dve)
                for t in range(n):
                    ins = dve.bn_aggr(mv[:, t, :], st[:, t, :])
                ins.then_inc(done, 1)

            dve.wait_ge(s.x_in, 16)
            stats(lambda t: m.xt[:, t, :], NT, m.st, m.mv, s.x_var)
            dve.wait_ge(s.ctx_in, 16)
            stats(lambda t: m.ct[:, t, :], NT, m.st2, m.mv2, s.x_var)
            dve.wait_ge(s.wg_T, 1)
            ch.link(dve.tensor_copy(m.wg[:, :, :].rearrange("p c g -> p (c g)"), bk[7][:, 0:24]))
            dve.tensor_tensor(m.wg_ctx[:, :], m.wg[:, 1, :], m.wg[:, 2, :], ALU.add).then_inc(s.wg_ready, 1)
            dve.wait_ge(s.wg_ready, 1)
            dve.wait_ge(s.x_var, 2)
            dve.wait_ge(s.x_rstd, 1)
            for t in range(NT):
                dve.tensor_scalar(m.xn[:, t, :], m.xt[:, t, :], m.mv[:, t, 0:1], m.rs[:, t:t + 1], ALU.subtract, ALU.mult).then_inc(s.xn_ready, 1)
            for j in range(2):
                dve.wait_ge(s.cT_ready, j + 1)
                dve.tensor_copy(m.cT[:, 4 * j:4 * j + 4, :].rearrange("p t c -> p (t c)"), bk[2 + j][:, :]).then_inc(s.cT_copied, 1)
            dve.wait_ge(s.x_rstd, 2)
            dve.wait_ge(s.xT_ready, 2)
            for t in range(NT):
                ins = dve.tensor_scalar(m.xn[:, t, :], m.ct[:, t, :], m.mv2[:, t, 0:1], m.rs2[:, t:t + 1], ALU.subtract, ALU.mult)
            ins.then_inc(s.xn_ready, 1)
            dve.wait_ge(s.tanh_ready, 1)
            dve.tensor_scalar(m.lnw[:, :], m.lnw[:, :], 1.0, m.gx[:, 0:1], ALU.add, ALU.mult)
            dve.wait_ge(s.gates, 1)
            G = bk[6][:, 0:64].rearrange("p (b i g) -> p b i g", b=B, i=I)

            def by_bi(a):
                return a[:, :, :, :].rearrange("p i b h -> p b i h")

            def bias(a):
                return a[:, :].unsqueeze(1).unsqueeze(1).to_broadcast([P, B, I, NH0])

            dve.tensor_tensor(by_bi(m.fg), G[:, :, :, NH0:2 * NH0], bias(m.bf), ALU.add).then_inc(s.gates_b, 1)
            ch.link(dve.tensor_tensor(by_bi(m.ig), G[:, :, :, 0:NH0], bias(m.bi), ALU.add))
            dve.wait_ge(s.softplus, 1)
            flat = lambda a: a[:, :, :, :].rearrange("p i b h -> p (i b h)")
            dve.scalar_tensor_tensor(flat(m.logf), flat(m.fg), 0.0, flat(m.tmp_a), ALU.min, ALU.subtract).then_inc(s.logf_ready, 1)
            dve.wait_ge(s.F_ready, 1)
            ch.link(dve.tensor_copy(flat(m.Ft), bk[7][:, 0:32]))
            ch.link(dve.tensor_tensor(flat(m.at), flat(m.ig), flat(m.Ft), ALU.subtract))
            for part in range(3):
                ins = dve.tensor_copy(m.a3[:, :, PART_AT * part:PART_AT * part + UNITS], m.at[:, :, :, :].rearrange("p i b h -> p i (b h)"))
            ins.then_inc(s.a_ready, 1)
            dve.wait_ge(s.const, 2)
            dve.wait_ge(s.aT_ready, 1)
            ch.link(dve.tensor_tensor_scan(m.M16[:, 0:S], m.zero16[:, :], bk[7][0:M_ROWS, 128:128 + S], -3e38, ALU.add, ALU.max))
            dve.tensor_copy(m.M16[:, S:W0], m.M16[:, P:S]).then_inc(s.M_ready, 1)
            dve.wait_ge(s.M_ready, 1)
            rest = m.M16[:, :]
            for part in range(3):
                ch.link(dve.tensor_copy(m.Mp[:, part, :], rest))
                if part < 2:
                    ch.link(dve.tensor_tensor(m.M_rest[:, part, :], rest, m.Mp[:, part, :], ALU.subtract))
                    rest = m.M_rest[:, part, :]
            for part in range(3):
                r = slice(PART_AT * part, PART_AT * part + UNITS)
                ins = dve.tensor_copy(m.M3[r, :], m.Mp[r, part, :])
            ins.then_inc(s.M3_ready, 1)
            dve.wait_ge(s.Mt_ready, 1)
            dve.tensor_tensor(flat(m.mlog), flat(m.Ft), bk[6][:, 128:160], ALU.add).then_inc(s.mlog_ready, 1)

            def weigh(u):
                dve.wait_ge(s.S0_ready, u + 1)
                dve.wait_ge(s.D_ready, u + 1)
                if u >= 2:
                    dve.wait_ge(s.C_free, u - 1)
                dve.scalar_tensor_tensor(m.C[:, u % 2, :], bk[2 + u % 2][:, 0:W0], DH0 ** -0.5, m.Dm[:, u % 2, :],
                                         ALU.mult, ALU.mult).then_inc(s.C_ready, 1)

            def finish1(b):
                O = bk[4 + b % 2][:, 0:264].rearrange("p (n c) -> p n c", c=DH0 + 1)
                nrm, en = m.nrm[:, :].rearrange("p (i h) -> p i h", i=I), m.en[:, :, b, :]
                dve.wait_ge(s.en_ready, 1)
                dve.wait_ge(s.absc_ready, b + 1)
                ch.link(dve.tensor_tensor(nrm, m.absc[:, :].rearrange("p (i h) -> p i h", i=I), en, ALU.max))
                ch.link(dve.tensor_scalar(m.nrm[:, :], m.nrm[:, :], EPS0, None, ALU.add))
                ch.link(dve.reciprocal(m.rn[:, :], m.nrm[:, :]))
                ins = dve.tensor_tensor(m.hh[:, :, :], O[:, :, 0:DH0], wide(m.rn[:, :], DH0), ALU.mult)
                ins.then_inc(s.O0_free, 1)
                dve.wait_ge(s.O0_free, b + 1)
                ch.link(dve.tensor_reduce(m.s32[:, :], m.hh[:, :, :], AX.X, ALU.add))
                ch.link(dve.scalar_tensor_tensor(m.hc[:, :, :], wide(m.s32[:, :], DH0), -1.0 / DH0, m.hh[:, :, :], ALU.mult, ALU.add))
                ch.link(dve.tensor_tensor(m.sq[:, :, :], m.hc[:, :, :], m.hc[:, :, :], ALU.mult))
                ch.link(dve.tensor_reduce(m.s32[:, :], m.sq[:, :, :], AX.X, ALU.add))
                dve.tensor_scalar(m.v32[:, :], m.s32[:, :], 1.0 / DH0, None, ALU.mult).then_inc(s.var0, 1)

            def finish2(b):
                dve.wait_ge(s.rstd0, b + 1)
                ch.link(dve.tensor_tensor(m.sq[:, :, :], m.hc[:, :, :], wide(m.r32[:, :], DH0), ALU.mult))
                y = m.sq[:, :, :].rearrange("p (i h) c -> p i (h c)", i=I)
                ch.link(dve.tensor_tensor(y, y, m.lnw[:, :].unsqueeze(1).to_broadcast([P, I, D]), ALU.mult))
                xb = m.xt[:, I * b:I * b + I, :]
                ch.link(dve.tensor_tensor(xb, xb, y, ALU.add))
                stats(lambda t: m.xt[:, I * b + t, :], I, m.st, m.mv, s.x1_var)

            def finish3(b):
                dve.wait_ge(s.x1_var, b + 1)
                dve.wait_ge(s.x1_rstd, b + 1)
                if b >= 1:
                    dve.wait_ge(s.x1T_ready, b)
                for i in range(I):
                    ins = dve.tensor_scalar(m.n2[:, i, :], m.xt[:, I * b + i, :], m.mv[:, i, 0:1], m.rs[:, i:i + 1], ALU.subtract, ALU.mult)
                ins.then_inc(s.x1n_ready, 1)

            def x1_low(b):
                dve.wait_ge(s.x1T_hi, b + 1)
                dve.tensor_tensor(m.xbTl[:, I * b:I * b + I, :].rearrange("p i c -> p (i c)"), bk[6][:, 0:S],
                                  m.xbTh[:, I * b:I * b + I, :].rearrange("p i c -> p (i c)"), ALU.subtract).then_inc(s.x1T_lo, 1)

            def top3(b):
                dve.wait_ge(s.g1_exp, b + 1)
                sgf = m.sg[:, :, :].rearrange("p i g -> p (i g)")
                ch.link(dve.tensor_scalar(sgf, sgf, 1.0, None, ALU.add))
                ch.link(dve.reciprocal(sgf, sgf))
                sg = sgf.rearrange("p (n e) -> p n e", e=E1)
                N = I * 2 * H1
                for e in range(E1):
                    if e > 0:
                        ins = dve.tensor_tensor(m.cmp[:, :, e, 0:e], sg[:, :, 0:e], sg[:, :, e:e + 1].to_broadcast([P, N, e]), ALU.is_ge)
                    if e < E1 - 1:
                        ins = dve.tensor_tensor(m.cmp[:, :, e, e:E1 - 1], sg[:, :, e + 1:E1], sg[:, :, e:e + 1].to_broadcast([P, N, E1 - 1 - e]), ALU.is_gt)
                ch.link(ins)
                ch.link(dve.tensor_reduce(m.cnt[:, :], m.cmp[:, :, :, :].rearrange("p n e c -> p (n e) c"), AX.X, ALU.add))
                g = slice(I * b, I * b + I)
                dve.tensor_scalar(m.topm[:, g, :].rearrange("p i g -> p (i g)"), m.cnt[:, :], TOP - 0.5, None, ALU.is_lt)
                dve.scalar_tensor_tensor(m.gatev[:, g, :].rearrange("p i g -> p (i g)"), m.cnt[:, :], TOP - 0.5, sgf,
                                         ALU.is_lt, ALU.mult).then_inc(s.gate_ready, 1)

            for u in range(UNITS):
                weigh(u)
                b, r = divmod(u, NH0)
                if r == 0 and b >= 2:
                    x1_low(b - 2)
                if b >= 1 and r < 3:
                    (finish1, finish2, finish3)[r](b - 1)
                if r == 2 and b >= 2:
                    top3(b - 2)
            x1_low(B - 2)

            def b1_copy():
                dve.wait_ge(s.b1T_ready, 1)
                dve.tensor_copy(m.b1T[:, :, :].rearrange("p e f -> p (e f)"), bk[2][:, 0:E3 * FT]).then_inc(s.b1T_copied, 1)

            finish1(B - 1)
            dve_b(dve, ch, stats, {3: lambda: finish2(B - 1), 5: b1_copy, 6: lambda: finish3(B - 1), 10: lambda: top3(B - 2),
                                   13: lambda: x1_low(B - 1), 18: lambda: top3(B - 1)})
            dve_c(dve, ch, stats)
            dve_d(dve, ch)
            dve.wait_ge(s.y_free, NT * (E3 + 1) + YR)
            dve.sem_inc(s.out_ready, 1)


INS = ["x", "ctx_1024", "mask_BxS2_bf1", "g_xattn", "g_ffn", "L0_xattn_w_igate", "L0_xattn_b_igate", "L0_xattn_w_fgate",
       "L0_xattn_b_fgate", "L0_xattn_ln_weight", "L0_ffn_Wq", "L0_ffn_Wkv", "L0_ffn_Ws", "L0_ffn_Wd", "L0_ffn_Wo",
       "L1_xattn_gm", "L1_xattn_bm", "L1_xattn_gl", "L1_xattn_bl", "L1_xattn_Wq", "L1_xattn_Wk", "L1_xattn_Wv", "L1_xattn_Wo",
       "L1_ffn_gate_w", "L1_ffn_w1", "L1_ffn_b1", "L1_ffn_w2", "L1_ffn_b2"]


OUTS = [((B, S, D), "float32")]


def kernel(**inputs):
    import numpy as np
    import concourse.bacc as bacc
    from concourse.bass_utils import run_bass_kernel_spmd as run

    nc = bacc.Bacc("TRN2", target_bir_lowering=False, num_devices=1)
    arrays, args = {}, []
    for name in INS:
        a = np.ascontiguousarray(inputs[name])
        arrays[f"in_{name}"] = a
        args.append(nc.dram_tensor(f"in_{name}", a.shape, mybir.dt.from_np(a.dtype), kind="ExternalInput").ap())
    for i, (shape, dtype) in enumerate(OUTS):
        args.append(nc.dram_tensor(f"out_{i}", shape, mybir.dt.from_np(np.dtype(dtype)), kind="ExternalOutput").ap())
    build(nc, *args)
    r = run(nc, [arrays], core_ids=[0])
    return r.results[0]["out_0"]
```

```python
from contextlib import ExitStack

import concourse.bass as bass
from concourse import mybir

ALU = mybir.AluOpType
ACT = mybir.ActivationFunctionType
AX = mybir.AxisListType
F32 = mybir.dt.float32
F16 = mybir.dt.float16
BF16 = mybir.dt.bfloat16
U8 = mybir.dt.uint8
U32 = mybir.dt.uint32

P = 128
B, S, D = 4, 256, 128
I = S // P
NT = B * I
BIG = 1e30
EPS = 1e-5

NH0, DH0 = 4, 32
UNITS = B * NH0
W0 = S + P
EPS0 = 1e-6
PART_AT = 32
M_ROWS = 2 * PART_AT + UNITS

H1, E1, DH1, TOP = 8, 5, 64, 3
HD1 = H1 * DH1
G1 = H1 * E1
PARTS = ("q", "k", "v")

H2, DH2 = 16, 64
KT = 2 * S // P
HP2 = H2 // 2
INNER = H2 * DH2

E3, FF = 8, 512
FT = FF // P

STAGE = 1280
N_STAGE = 3


def settle(eng, sem):
    eng.sem_inc(sem, 1)


class Names:
    pass


class Chain:

    def __init__(self, eng, sem):
        self.eng, self.sem, self.base, self.k, self.turn, self.per = eng, sem, 0, 0, 0, 0

    def loop(self, turn, per):
        self.base, self.k, self.turn, self.per = self.base + self.k, 0, turn, per

    def end_loop(self, turns):
        assert self.k == self.per, (self.k, self.per)
        self.base, self.k, self.turn, self.per = self.base + turns * self.per, 0, 0, 0

    def link(self, instruction):
        self.k += 1
        instruction.then_inc(self.sem, 1)
        self.eng.wait_ge(self.sem, self.turn * self.per + (self.base + self.k) if self.per else self.base + self.k)


def weight_chunks(m, d):
    out = []
    for c in range(2):
        out.append((d.Wq0[:, c * 1280:(c + 1) * 1280], 1280, m.wq0h[:, c * 1280:(c + 1) * 1280], m.wq0l[:, c * 1280:(c + 1) * 1280]))
    for c in range(4):
        out.append((d.Wkv0[:, c * 1280:(c + 1) * 1280], 1280, m.wkv0h[:, c * 1280:(c + 1) * 1280], m.wkv0l[:, c * 1280:(c + 1) * 1280]))
    for src, hi, lo in ((d.Wv1, m.wv1h, m.wv1l), (d.Wq1, m.wq1h, m.wq1l), (d.Wk1, m.wk1h, m.wk1l)):
        out.append((src, INNER, hi[:, :], lo[:, :]))
    for c in range(E3 // 2):
        out.append((d.w1[2 * c:2 * c + 2, :, :].rearrange("e p n -> p e n"), 2 * FF,
                    m.w1h[:, 2 * c:2 * c + 2, :], m.w1l[:, 2 * c:2 * c + 2, :]))
    for c in range(E3 // 2):
        out.append((d.w2[2 * c:2 * c + 2, :, :].rearrange("e (f p) n -> p (e f) n", p=P), 2 * FT * D,
                    m.w2h[:, 2 * c:2 * c + 2, :, :].rearrange("p e f n -> p (e f) n"),
                    m.w2l[:, 2 * c:2 * c + 2, :, :].rearrange("p e f n -> p (e f) n")))
    return out


N_W0 = 6
N_W1 = 9
N_WALL = 17
DVE_STEPS_B, POOL_STEPS_B, DVE_STEPS_C = 4, 16, 8


def build(nc, x, ctx_in, mask, g_x, g_f, w_i, b_i, w_f, b_f, ln_w, Wq0, Wkv0, Ws, Wd, Wo0,
          gm, bm, gl, bl, Wq1, Wk1, Wv1, Wo1, gate_w, w1, b1, w2, b2, out):
    with ExitStack() as stack:
        m, s, d = Names(), Names(), Names()

        def sb(name, shape, dt=F32):
            return stack.enter_context(nc.sbuf_tensor(name, shape, dt))

        def share(arena, words, *parts):
            area = stack.enter_context(nc.sbuf_tensor(arena, [P, words], F32))
            views = []
            for at, shape, dt in parts:
                n = 1
                for k in shape:
                    n *= k
                used = n if dt == F32 else n // 2
                assert at + used <= words, arena
                v = area[:, at:at + used]
                if dt != F32:
                    v = v.bitcast(dt)
                if len(shape) > 1:
                    names = "abcd"[:len(shape)]
                    v = v.rearrange("p (%s) -> p %s" % (" ".join(names), " ".join(names)), **dict(zip(names, shape)))
                views.append(v)
            return views

        def sem(name):
            return stack.enter_context(nc.semaphore("s_" + name))

        d.Wq0, d.Wkv0, d.Wq1, d.Wk1, d.Wv1, d.w1, d.w2 = Wq0, Wkv0, Wq1, Wk1, Wv1, w1, w2
        bk = [stack.enter_context(nc.psum_tensor(f"bank{i}", [P, 512], F32)) for i in range(8)]

        m.ident = sb("ident", [P, P])
        m.ones = sb("ones", [P, P])
        m.tri = sb("tri", [P, P])
        m.identb = sb("identb", [P, P], BF16)
        m.causal = sb("causal", [P, W0], BF16)
        m.zero16 = sb("zero16", [M_ROWS, S])
        m.mhalf = sb("mhalf", [P, 16])
        m.iota_i = sb("iota_i", [P, E3], mybir.dt.int32)
        m.iota_f = sb("iota_f", [P, E3])
        m.wi_row = sb("wi_row", [NH0, 3 * D])
        m.wf_row = sb("wf_row", [NH0, 3 * D])
        m.wg = sb("wg", [P, 3, 2 * NH0])
        m.wg_ctx = sb("wg_ctx", [P, 2 * NH0])
        m.bi = sb("bi", [P, NH0])
        m.bf = sb("bf", [P, NH0])
        m.lnw = sb("lnw", [P, D])
        m.gx = sb("gx", [P, 2])
        m.gf = sb("gf", [P, 2])
        m.cols = sb("cols", [P, 4])
        m.mask_u8 = sb("mask_u8", [P, B, S], U8)
        m.maskb = sb("maskb", [P, B, 2 * S], BF16)
        m.maskrow = sb("maskrow", [P, 2 * S], BF16)
        m.wsd = sb("wsd", [P, 2 * G1])
        m.wo0 = sb("wo0", [P, 3, D])
        m.wo1 = sb("wo1", [P, HP2, D])
        m.gate = sb("gate", [P, E3])
        m.b1_row = sb("b1_row", [E3 * FT, P])
        m.b1T = sb("b1T", [P, E3, FT])
        m.b2 = sb("b2", [E3, D])
        m.stage = sb("stage", [P, N_STAGE, STAGE])
        m.wq1h, m.wq1l, m.wk1h, m.wk1l, m.wv1h, m.wv1l = (
            sb(n, [P, INNER], F16) for n in ("wq1h", "wq1l", "wk1h", "wk1l", "wv1h", "wv1l"))
        NQ, NW = H1 * E1 * DH1, E3 * FF // 2
        m.wq0h, m.wq0l, m.wkv0h, m.wkv0l, m.w1h, m.w1l, m.w2h, m.w2l = share("weights", 4 * NW,
              (0, (NQ,), F16), (NQ // 2, (NQ,), F16), (NQ, (2 * NQ,), F16), (2 * NQ, (2 * NQ,), F16),
              (0, (E3, FF), F16), (NW, (E3, FF), F16), (2 * NW, (E3, FT, D), F16), (3 * NW, (E3, FT, D), F16))
        NV = KT * H2 * (DH2 + 1) // 2
        HALVES_AT = I * M_ROWS + 5 * W0
        m.prod, m.acc, m.v2h, m.v2l, m.ao, m.hTh, m.hTl, m.hf, *work_early = share("work", 16 * HD1,
              (0, (2, E1, HD1), F32), (2 * E1 * HD1, (3, I, HD1), F32),
              (0, (KT, H2, DH2 + 1), F16), (NV, (KT, H2, DH2 + 1), F16), (2 * NV, (I, INNER), F32),
              (0, (2, FT, 512), F16), (2048, (2, FT, 512), F16), (4096, (4, 512), F32),
              (0, (I, M_ROWS), F32), (I * M_ROWS, (W0,), F32), (I * M_ROWS + W0, (2, W0), F32), (I * M_ROWS + 3 * W0, (3, W0), BF16),
              *((HALVES_AT + k * NT * P // 2, (NT, P), F16) for k in range(4)))
        m.xnT, m.cT, m.vx, m.ho, m.aoT, m.xdTh, m.xdTl = share("work0", 3 * NT * P + NT * NH0,
              (0, (NT, P), F32), (NT * P, (NT, P), F32), (2 * NT * P, (NT, NH0, DH0 + 1), F32),
              (0, (I, HD1), F32), (0, (I, HP2, P), F32),
              (2 * NT * P, (NT, P), F16), (2 * NT * P + NT * P // 2, (NT, P), F16))
        m.xt = sb("xt", [P, NT, D])
        m.ct = sb("ct", [P, NT, D])
        m.st = sb("st", [P, NT, 6])
        m.mv = sb("mv", [P, NT, 2])
        m.rs = sb("rs", [P, NT])
        m.st2 = sb("st2", [P, NT, 6])
        m.mv2 = sb("mv2", [P, NT, 2])
        m.rs2 = sb("rs2", [P, NT])
        m.kvTh = sb("kvTh", [P, B, 2 * S], F16)
        m.kvTl = sb("kvTl", [P, B, 2 * S], F16)
        m.xbTh = sb("xbTh", [P, NT, P], F16)
        m.xbTl = sb("xbTl", [P, NT, P], F16)
        m.ig, m.fg, m.tmp_a, m.tmp_b, m.logf, m.Ft, m.at, m.mlog, m.en = (
            sb(n, [P, I, B, NH0]) for n in ("ig", "fg", "tmp_a", "tmp_b", "logf", "Ft", "at", "mlog", "en"))
        m.a3, m.M16, m.M_rest, m.Mp, m.xTh, m.xTl, m.cTh, m.cTl = work_early
        m.M16, m.M_rest, m.Mp = (a[0:M_ROWS] for a in (m.M16, m.M_rest, m.Mp))
        m.M3 = sb("M3", [M_ROWS, W0], BF16)
        m.sel3 = sb("sel3", [M_ROWS, PART_AT], BF16)
        m.Dm = sb("Dm", [P, 2, W0])
        m.C = sb("C", [P, 2, W0])
        m.absc, m.nrm, m.rn, m.s32, m.v32, m.r32 = (
            sb(n, [P, I * NH0]) for n in ("absc", "nrm", "rn", "s32", "v32", "r32"))
        m.hh = sb("hh", [P, I * NH0, DH0])
        m.hc = sb("hc", [P, I * NH0, DH0])
        m.sq = sb("sq", [P, I * NH0, DH0])
        m.sg = sb("sg", [P, I, 2 * G1])
        m.cmp = sb("cmp", [P, I * 2 * H1, E1, E1 - 1], BF16)
        m.cnt = sb("cnt", [P, I * 2 * G1])
        m.topm = sb("topm", [P, NT, 2 * G1])
        m.gatev = sb("gatev", [P, NT, 2 * G1])
        m.qTh = sb("qTh", [P, 4, S], F16)
        m.qTl = sb("qTl", [P, 4, S], F16)
        m.kTh = sb("kTh", [P, 4, S], F16)
        m.kTl = sb("kTl", [P, 4, S], F16)
        m.v1h = sb("v1h", [P, I, H1, DH1 + 1], F16)
        m.v1l = sb("v1l", [P, I, H1, DH1 + 1], F16)
        m.nm = sb("nm", [P, 4, 2])
        m.xn, m.Pr = share("work1", NT * D, (0, (NT, D), F32), (0, (2, 512), F32))
        m.PTh = sb("PTh", [P, 2, 4, P], F16)
        m.PTl = sb("PTl", [P, 2, 4, P], F16)
        m.den = sb("den", [P, 8])
        m.z = sb("z", [P, I, E1 * DH1])
        m.zT = sb("zT", [P, 3, P])
        m.xT32 = sb("xT32", [P, I, P])
        m.n2 = sb("n2", [P, I, D])
        m.q2h = sb("q2h", [P, 2, S], F16)
        m.q2l = sb("q2l", [P, 2, S], F16)
        m.k2h = sb("k2h", [P, 2, 2 * S], F16)
        m.k2l = sb("k2l", [P, 2, 2 * S], F16)
        m.sm = sb("sm", [P, 2, 512])
        m.lg = sb("lg", [P, NT, E3])
        m.m8 = sb("m8", [P, NT, 8])
        m.ix8 = sb("ix8", [P, NT, 8], U32)
        m.ixf = sb("ixf", [P, NT])
        m.lgm = sb("lgm", [P, NT, E3])
        m.ex8 = sb("ex8", [P, NT, E3])
        m.sum8 = sb("sum8", [P, NT])
        m.wmax = sb("wmax", [P, NT])
        m.we1 = sb("we1", [P, NT, E3])
        m.we = sb("we", [P, E3, NT])
        m.weT = sb("weT", [E3, NT, P])

        s.x_in = sem("x_in")
        s.ctx_in = sem("ctx_in")
        s.wg_in = sem("wg_in")
        s.small_in = sem("small_in")
        s.small2_in = sem("small2_in")
        s.w_hi = sem("w_hi")
        s.w_split = sem("w_split")
        s.settled_act = sem("settled_act")
        s.settled_dve = sem("settled_dve")
        s.settled_pool = sem("settled_pool")
        s.const = sem("const")
        s.pool_chain = sem("pool_chain")
        s.dve_chain = sem("dve_chain")
        s.act_chain = sem("act_chain")
        s.out_done = sem("out_done")
        s.x_var = sem("x_var")
        s.x_rstd = sem("x_rstd")
        s.xn_ready = sem("xn_ready")
        s.xT_ready = sem("xT_ready")
        s.cT_ready = sem("cT_ready")
        s.xT_copied = sem("xT_copied")
        s.cT_copied = sem("cT_copied")
        s.wg_T = sem("wg_T")
        s.wg_ready = sem("wg_ready")
        s.gates = sem("gates")
        s.gates_b = sem("gates_b")
        s.softplus = sem("softplus")
        s.logf_ready = sem("logf_ready")
        s.F_ready = sem("F_ready")
        s.a_ready = sem("a_ready")
        s.aT_ready = sem("aT_ready")
        s.M_ready = sem("M_ready")
        s.M3_ready = sem("M3_ready")
        s.halves_ready = sem("halves_ready")
        s.Mt_ready = sem("Mt_ready")
        s.mlog_ready = sem("mlog_ready")
        s.en_ready = sem("en_ready")
        s.L_ready = sem("L_ready")
        s.S0_ready = sem("S0_ready")
        s.D_ready = sem("D_ready")
        s.C_ready = sem("C_ready")
        s.C_free = sem("C_free")
        s.absc_ready = sem("absc_ready")
        s.O0_free = sem("O0_free")
        s.var0 = sem("var0")
        s.rstd0 = sem("rstd0")
        s.vx_ready = sem("vx_ready")
        s.tanh_ready = sem("tanh_ready")
        s.cn_T = sem("cn_T")
        s.kv_f = sem("kv_f")
        s.kv_free = sem("kv_free")
        s.maskb_ready = sem("maskb_ready")
        s.maskrow_ready = sem("maskrow_ready")
        s.x1_var = sem("x1_var")
        s.x1_rstd = sem("x1_rstd")
        s.x1n_ready = sem("x1n_ready")
        s.x1T_ready = sem("x1T_ready")
        s.x1T_f32 = sem("x1T_f32")
        s.x1T_hi = sem("x1T_hi")
        s.x1T_lo = sem("x1T_lo")
        s.g1_ready = sem("g1_ready")
        s.g1_exp = sem("g1_exp")
        s.sg_ready = sem("sg_ready")
        s.gate_ready = sem("gate_ready")
        s.b1T_ready = sem("b1T_ready")
        s.b1T_copied = sem("b1T_copied")
        s.pj_ready = sem("pj_ready")
        s.prod_ready = sem("prod_ready")
        s.prod_free = sem("prod_free")
        s.acc_ready = sem("acc_ready")
        s.pair_ready = sem("pair_ready")
        s.T_ready = sem("T_ready")
        s.T_hi = sem("T_hi")
        s.T_free = sem("T_free")
        s.v1hi_ready = sem("v1hi_ready")
        s.v1lo_ready = sem("v1lo_ready")
        s.S_ready = sem("S_ready")
        s.exp_done = sem("exp_done")
        s.nm_ready = sem("nm_ready")
        s.wo_ready = sem("wo_ready")
        s.O_ready = sem("O_ready")
        s.O_free = sem("O_free")
        s.z_ready = sem("z_ready")
        s.z_sum = sem("z_sum")
        s.z_last = sem("z_last")
        s.zT_ready = sem("zT_ready")
        s.zT_copied = sem("zT_copied")
        s.x2_ready = sem("x2_ready")
        s.latT_ready = sem("latT_ready")
        s.lat_lo = sem("lat_lo")
        s.x2_var = sem("x2_var")
        s.x2_rstd = sem("x2_rstd")
        s.x2n_ready = sem("x2n_ready")
        s.lat_ready = sem("lat_ready")
        s.lat_hi = sem("lat_hi")
        s.c_pj_ready = sem("c_pj_ready")
        s.c_pj_hi = sem("c_pj_hi")
        s.c_pj_free = sem("c_pj_free")
        s.c_S_ready = sem("c_S_ready")
        s.c_max_done = sem("c_max_done")
        s.c_exp_done = sem("c_exp_done")
        s.c_T_ready = sem("c_T_ready")
        s.c_T_hi = sem("c_T_hi")
        s.c_T_free = sem("c_T_free")
        s.c_O_ready = sem("c_O_ready")
        s.c_O_free = sem("c_O_free")
        s.v2_ones = sem("v2_ones")
        s.c_wo_ready = sem("c_wo_ready")
        s.ao_copied = sem("ao_copied")
        s.xdT_ready = sem("xdT_ready")
        s.xd_lo = sem("xd_lo")
        s.weT_ready = sem("weT_ready")
        s.weT_copied = sem("weT_copied")
        s.x3_var = sem("x3_var")
        s.x3_rstd = sem("x3_rstd")
        s.x3n_ready = sem("x3n_ready")
        s.xd_f32 = sem("xd_f32")
        s.xd_hi = sem("xd_hi")
        s.rt_ready = sem("rt_ready")
        s.rt_nmax = sem("rt_nmax")
        s.rt_exp = sem("rt_exp")
        s.we_ready = sem("we_ready")
        s.h_ready = sem("h_ready")
        s.gelu_done = sem("gelu_done")
        s.h_hi = sem("h_hi")
        s.h_lo = sem("h_lo")
        s.y_ready = sem("y_ready")
        s.y_free = sem("y_free")
        s.out_ready = sem("out_ready")

        stage_in = [stack.enter_context(nc.semaphore(f"s_stage_in{n}")) for n in range(N_STAGE)]
        N_SMALL, N_SMALL2 = 9, 2 + 1 + E1 + 4
        block = stack.enter_context(nc.Block())
        chunks = weight_chunks(m, d)

        def staged(n):
            src, w, _, _ = chunks[n]
            raw = m.stage[:, n % N_STAGE, 0:w]
            return raw if len(src.shape) == 2 else raw.rearrange("p (e n) -> p e n", e=src.shape[1])

        xf = x.rearrange("b (i p) c -> p (b i) c", p=P)
        cf = ctx_in.rearrange("b (i p) c -> p (b i) c", p=P)
        outf = out.rearrange("b (i p) c -> p (b i) c", p=P)

        RING = 2
        T1, O1, X1 = 4 + H1, H1 // 2, len(PARTS) * I * E1
        STEPS = H1 + 4
        HEAD_STEPS = 5
        CHUNKS = (2, 3, 5, 5, 5, 5, 5)
        assert sum(CHUNKS) == X1 and len(CHUNKS) == STEPS - HEAD_STEPS
        SUMS = len(PARTS) * I
        GROUPS = SUMS + I
        bank_pj, bank_S, bank_T, bank_O = bk[0:2], bk[2:4], bk[4:6], bk[6:8]
        wq0 = [w.rearrange("p (h e c) -> p h e c", h=H1, e=E1) for w in (m.wq0h, m.wq0l)]
        wkv0 = [w.rearrange("p (a h e c) -> p a h e c", a=2, h=H1, e=E1) for w in (m.wkv0h, m.wkv0l)]

        def chunk(c):
            return c // (I * E1), c // E1 % I, c % E1

        def chunks_of(step):
            k = step - HEAD_STEPS
            mine = list(range(X1))[sum(CHUNKS[:k]):sum(CHUNKS[:k + 1])]
            return mine[:2], mine[2:3], mine[3:]

        def turns_of(step):
            return {STEPS - 3: (0, 1), STEPS - 2: (2,), STEPS - 1: (3,)}.get(step, ())

        def heads8(a):
            return a.rearrange("p (h c) -> p h c", h=H1)

        def wide(a, n):
            return a.unsqueeze(2).to_broadcast([P, a.shape[1], n])

        def pe_b(pe, turn, between):
            pe.sem_inc(s.O_ready, RING)
            pe.sem_inc(s.wo_ready, 1)

            def project(b, c):
                part, i, e = chunk(c)
                if c >= 2 or not isinstance(b, int) or b > 0:
                    pe.wait_ge(s.prod_ready, b * X1 + (c - 1))
                wh, wl = (w[:, :, e, :] for w in wq0) if part == 0 else (w[:, part - 1, :, e, :] for w in wkv0)
                o = heads8(bank_pj[c % 2][:, :])
                xh, xl = m.xbTh[:, b * I + i, :], m.xbTl[:, b * I + i, :]
                pe.matmul(o, xh, wh, start=True, stop=False)
                pe.matmul(o, xh, wl, start=False, stop=False)
                pe.matmul(o, xl, wh, start=False, stop=True).then_inc(s.pj_ready, 1)

            def take_T(b, k):
                pe.wait_ge(s.T_free, b * T1 + (k + 1))
                return bank_T[k % 2]

            def turn_qk(b, k):
                pe.wait_ge(s.acc_ready, b * SUMS + (k + 1))
                bank = take_T(b, k)
                for hp in range(4):
                    ins = turn(bank[:, hp * P:(hp + 1) * P], m.acc[:, k // I, k % I, hp * P:(hp + 1) * P])
                ins.then_inc(s.T_ready, 1)

            def scores(b, h):
                if h == 0:
                    pe.wait_ge(s.T_free, b * T1 + (4 + RING))
                pe.wait_ge(s.nm_ready, b * H1 + (h + 1))
                pe.wait_ge(s.exp_done, b * H1 + (h + 1))
                r = slice(DH1 * (h % 2), DH1 * (h % 2) + DH1)
                for i in range(I):
                    o = bank_S[h % 2][:, i * S:(i + 1) * S]
                    qh, ql = (q[r, h // 2, i * P:(i + 1) * P] for q in (m.qTh, m.qTl))
                    kh, kl = (k[r, h // 2, :] for k in (m.kTh, m.kTl))
                    pe.matmul(o, qh, kh, start=True, stop=False)
                    pe.matmul(o, qh, kl, start=False, stop=False)
                    ins = pe.matmul(o, ql, kh, start=False, stop=True)
                ins.then_inc(s.S_ready, 1)

            def step(b, h, more):
                chunks3 = chunks_of(h) if more else ((), (), ())
                if h + 1 < H1:
                    scores(b, h + 1)
                for c in chunks3[0]:
                    project(b + 1, c)
                if 3 <= h < H1 + 3:
                    g = h - 3
                    pe.wait_ge(s.T_free, b * T1 + (4 + g + 1 + RING))
                    if g == 0:
                        pe.wait_ge(s.v1lo_ready, b * I + I)
                    if g % 2 == 0:
                        pe.wait_ge(s.O_free, b * O1 + (g // 2 + 1))
                    for i in range(I):
                        col = (g % 2 * I + i) * (DH1 + 1)
                        o = bank_O[g // 2 % 2][:, col:col + DH1 + 1]
                        for j in range(I):
                            ph, pl = (p[:, g % 2, j * I + i, :] for p in (m.PTh, m.PTl))
                            vh, vl = (v[:, j, g, :] for v in (m.v1h, m.v1l))
                            pe.matmul(o, ph, vh, start=(j == 0), stop=False)
                            pe.matmul(o, ph, vl, start=False, stop=False)
                            ins = pe.matmul(o, pl, vh, start=False, stop=(j == I - 1))
                    ins.then_inc(s.O_ready, 1)
                for c in chunks3[1]:
                    project(b + 1, c)
                if 1 <= h <= H1:
                    g = h - 1
                    pe.wait_ge(s.exp_done, b * H1 + (g + 1 + RING))
                    bank = take_T(b, 4 + g)
                    for i in range(I):
                        for j in range(I):
                            ins = turn(bank[:, (j * I + i) * P:(j * I + i + 1) * P], m.Pr[:, g % 2, i * S + j * P:i * S + (j + 1) * P])
                    ins.then_inc(s.T_ready, 1)
                for c in chunks3[2]:
                    project(b + 1, c)
                if more:
                    for k in turns_of(h):
                        turn_qk(b + 1, k)

            def turn_z(b, i):
                if isinstance(b, int) and i == 1:
                    pe.wait_ge(s.z_last, 1)
                else:
                    pe.wait_ge(s.z_sum, b * I + (i + 1))
                for c in range(3):
                    w = min(P, E1 * DH1 - c * P)
                    ins = turn(bank_pj[i][0:w, c * P:(c + 1) * P], m.z[:, i, c * P:c * P + w])
                ins.then_inc(s.zT_ready, 1)

            def project_z(b, i):
                pe.wait_ge(s.zT_copied, b * I + (i + 1))
                for c in range(3):
                    w = min(P, E1 * DH1 - c * P)
                    ins = pe.matmul(bank_pj[i][:, 3 * P:3 * P + D], m.zT[0:w, c, :], m.wo0[0:w, c, :], start=(c == 0), stop=(c == 2))
                ins.then_inc(s.wo_ready, 1)

            def turn_latents(batches):
                pe.wait_ge(s.exp_done, B * H1 + RING)
                pe.wait_ge(s.x2n_ready, 2)
                for b in batches:
                    if b >= I:
                        pe.wait_ge(s.lat_ready, b - I + 1)
                    turn_latent(pe, turn, b, bank_S[b % 2])

            for c in range(X1):
                if c in between:
                    between[c]()
                if c % (I * E1) == 0:
                    pe.wait_ge(s.w_split, 2 * chunk(c)[0] + 2)
                project(0, c)
            pe.wait_ge(s.b1T_copied, 1)
            pe.wait_ge(s.O0_free, B)
            pe.wait_ge(s.x1T_lo, B)
            pe.wait_ge(s.g1_exp, B)
            for k in range(4):
                turn_qk(0, k)
            scores(0, 0)
            for h in range(HEAD_STEPS):
                step(0, h, False)
            with pe.Fori(0, B - 1) as b:
                pe.wait_ge(s.x2_ready, b * I + I)
                for h in range(HEAD_STEPS, STEPS):
                    step(b, h, True)
                scores(b + 1, 0)
                for h in range(HEAD_STEPS):
                    step(b + 1, h, False)
                    if h == 3:
                        turn_z(b, 0)
                    if h == 4:
                        project_z(b, 0)
                    if h == 4:
                        turn_z(b, 1)
                        project_z(b, 1)
            for h in range(HEAD_STEPS, STEPS):
                step(B - 1, h, False)
                if h == STEPS - 1:
                    turn_latents(range(B - 1))
            pe.wait_ge(s.x2_ready, B * I)
            for i in range(I):
                turn_z(B - 1, i)
                project_z(B - 1, i)

        def turn_latent(pe, turn, b, bank):
            for i in range(I):
                ins = turn(bank[:, i * P:(i + 1) * P], m.ct[:, b * I + i, :])
            ins.then_inc(s.latT_ready, 1)

        def act_b(act):
            act.sem_inc(s.exp_done, RING)

            def high_qk(b, k):
                act.wait_ge(s.T_ready, b * T1 + (k + 1))
                dst = (m.qTh, m.kTh)[k // I][:, :, (k % I) * P:(k % I + 1) * P]
                act.activation(dst, bank_T[k % 2][:, :].rearrange("p (h c) -> p h c", h=4), ACT.Copy,
                               scale=DH1 ** -0.5 if k < I else 1.0).then_inc(s.T_hi, 1)

            def high_v(b):
                act.wait_ge(s.O_ready, b * H1 + RING)
                for i in range(I):
                    act.wait_ge(s.acc_ready, b * SUMS + (4 + i + 1))
                    act.activation(m.v1h[:, i, :, 0:DH1], heads8(m.acc[:, 2, i, :]), ACT.Copy).then_inc(s.v1hi_ready, 1)

            def step(b, h, more):
                if 2 <= h < H1 + 2:
                    g = h - 2
                    act.wait_ge(s.T_ready, b * T1 + (4 + g + 1))
                    act.wait_ge(s.O_ready, b * H1 + (g + 1))
                    act.activation(m.PTh[:, g % 2, :, :].rearrange("p n c -> p (n c)"), bank_T[g % 2][:, :], ACT.Copy).then_inc(s.T_hi, 1)
                if h < H1:
                    act.wait_ge(s.nm_ready, b * H1 + (h + 1 + RING))
                    act.wait_ge(s.T_ready, b * T1 + (4 + h - 1))
                    for i in range(I):
                        ins = act.activation(m.Pr[:, h % 2, i * S:(i + 1) * S], bank_S[h % 2][:, i * S:(i + 1) * S], ACT.Exp,
                                             bias=m.nm[:, h % 4, i:i + 1])
                    ins.then_inc(s.exp_done, 1)
                if more:
                    for k in turns_of(h):
                        high_qk(b + 1, k)

            def copy_z(b, i):
                act.wait_ge(s.zT_ready, b * I + (i + 1))
                act.wait_ge(s.wo_ready, b * I + (i + 1))
                act.activation(m.zT[:, 0:2, :].rearrange("p n c -> p (n c)"), bank_pj[i][:, 0:2 * P], ACT.Copy)
                act.activation(m.zT[0:DH1, 2, :], bank_pj[i][0:DH1, 2 * P:3 * P], ACT.Copy).then_inc(s.zT_copied, 1)

            for k in range(4):
                high_qk(0, k)
            high_v(0)
            for h in range(HEAD_STEPS):
                step(0, h, False)
            with act.Fori(0, B - 1) as b:
                for h in range(HEAD_STEPS, STEPS):
                    step(b, h, True)
                for h in range(HEAD_STEPS):
                    step(b + 1, h, False)
                    if h == 0:
                        high_v(b + 1)
                    if h == 3:
                        copy_z(b, 0)
                    if h == 4:
                        copy_z(b, 1)
            for h in range(HEAD_STEPS, STEPS):
                step(B - 1, h, False)
                if h == STEPS - 1:
                    for b in range(B - 1):
                        latent_high(act, b)
            for i in range(I):
                copy_z(B - 1, i)

        def latent_high(act, b):
            act.wait_ge(s.lat_ready, b + 1)
            act.activation(m.kvTh[:, b, S:2 * S], m.ct[:, b * I:(b + 1) * I, :].rearrange("p i c -> p (i c)"), ACT.Copy).then_inc(s.lat_hi, 1)

        def latent_stats(dve, stats, batches, k):
            tiles = range(batches[0] * I, (batches[-1] + 1) * I)
            if k % 2 == 0:
                dve.wait_ge(s.x2_ready, I + tiles[-1] + 1)
            else:
                dve.wait_ge(s.x2n_ready, k)
            src = m.ct if k % 2 else m.xt
            stats(lambda t: src[:, tiles[t], :], len(tiles), m.st, m.mv, s.x2_var)

        def latent_norm(dve, batches, k):
            tiles = range(batches[0] * I, (batches[-1] + 1) * I)
            src = m.ct if k % 2 else m.xt
            dve.wait_ge(s.x2_var, k + 1)
            dve.wait_ge(s.x2_rstd, k + 1)
            for t in range(len(tiles)):
                ins = dve.tensor_scalar(m.ct[:, tiles[t], :], src[:, tiles[t], :], m.mv[:, t, 0:1], m.rs[:, t:t + 1], ALU.subtract, ALU.mult)
            ins.then_inc(s.x2n_ready, 1)

        def latent_split(dve, b, bank):
            dve.wait_ge(s.latT_ready, b + 1)
            lat = m.ct[:, b * I:(b + 1) * I, :].rearrange("p i c -> p (i c)")
            dve.tensor_scalar(lat, bank[:, 0:S], m.cols[:, 2:3], m.cols[:, 3:4], ALU.mult, ALU.add).then_inc(s.lat_ready, 1)
            dve.wait_ge(s.lat_hi, b + 1)
            dve.tensor_tensor(m.kvTl[:, b, S:2 * S], lat, m.kvTh[:, b, S:2 * S], ALU.subtract).then_inc(s.lat_lo, 1)

        def dve_b(dve, ch, stats, between):
            dve.sem_inc(s.T_free, RING)
            dve.sem_inc(s.O_free, RING)
            dve.sem_inc(s.nm_ready, RING)
            dve.wait_ge(s.gate_ready, 1)

            def gate_products(b, c, group):
                part, i, e = chunk(c)
                sel = G1 if part == 0 else 0
                dve.wait_ge(s.pj_ready, b * X1 + (c + 1))
                if e == 0 and (group >= 2 if isinstance(group, int) else True):
                    dve.wait_ge(s.prod_free, group - 1)
                k = c // E1 % 2
                g = m.gatev[:, b * I + i, sel:sel + G1].rearrange("p (h e) -> p h e", h=H1)[:, :, e]
                dve.tensor_tensor(heads8(m.prod[:, k, e, :]), heads8(bank_pj[c % 2][:, :]), wide(g, DH1), ALU.mult).then_inc(s.prod_ready, 1)
                if e == E1 - 1:
                    dve.wait_ge(s.prod_ready, b * X1 + (c + 1))
                    dve.tensor_tensor(m.prod[:, k, 3, :], m.prod[:, k, 3, :], m.prod[:, k, 4, :], ALU.add).then_inc(s.pair_ready, 1)

            def split_qk(b, k):
                dve.wait_ge(s.T_hi, b * T1 + (k + 1))
                hi, lo = ((m.qTh, m.qTl), (m.kTh, m.kTl))[k // I]
                r = slice((k % I) * P, (k % I + 1) * P)
                turned = bank_T[k % 2][:, :].rearrange("p (h c) -> p h c", h=4)
                if k < I:
                    ins = dve.scalar_tensor_tensor(lo[:, :, r], turned, DH1 ** -0.5, hi[:, :, r], ALU.mult, ALU.subtract)
                else:
                    ins = dve.tensor_tensor(lo[:, :, r], turned, hi[:, :, r], ALU.subtract)
                ins.then_inc(s.T_free, 1)

            def split_v(b):
                for i in range(I):
                    dve.wait_ge(s.v1hi_ready, b * I + (i + 1))
                    dve.tensor_tensor(m.v1l[:, i, :, 0:DH1], heads8(m.acc[:, 2, i, :]), m.v1h[:, i, :, 0:DH1], ALU.subtract).then_inc(s.v1lo_ready, 1)

            def step(b, h, more):
                chunks3 = chunks_of(h) if more else ((), (), ())
                if h < H1:
                    dve.wait_ge(s.S_ready, b * H1 + (h + 1))
                    dve.tensor_reduce(m.nm[:, h % 4, :], bank_S[h % 2][:, :].rearrange("p (i c) -> p i c", i=I), AX.X, ALU.max, negate=True)\
                        .then_inc(s.nm_ready, 1)
                for c in chunks3[0]:
                    gate_products(b + 1, c, SUMS + b * GROUPS + c // E1)
                if 2 <= h < H1 + 2:
                    g = h - 2
                    dve.wait_ge(s.T_hi, b * T1 + (4 + g + 1))
                    dve.tensor_tensor(m.PTl[:, g % 2, :, :].rearrange("p n c -> p (n c)"), bank_T[g % 2][:, :],
                                      m.PTh[:, g % 2, :, :].rearrange("p n c -> p (n c)"), ALU.subtract).then_inc(s.T_free, 1)
                for c in chunks3[1]:
                    gate_products(b + 1, c, SUMS + b * GROUPS + c // E1)
                if h >= 5 and h % 2 == 1:
                    o = (h - 5) // 2
                    dve.wait_ge(s.O_ready, b * H1 + (2 * o + 2 + RING))
                    O = bank_O[o % 2][:, 0:4 * (DH1 + 1)].rearrange("p (h i c) -> p h i c", h=2, i=I)
                    den = m.den[:, 4 * (o % 2):4 * (o % 2) + 4]
                    ch.link(dve.reciprocal(den.rearrange("p (h i) -> p h i", h=2), O[:, :, :, DH1]))
                    dst = m.ho[:, :, 2 * o * DH1:(2 * o + 2) * DH1].rearrange("p i (h c) -> p h i c", h=2)
                    for hh in range(2):
                        ins = dve.tensor_tensor(dst[:, hh, :, :], O[:, hh, :, 0:DH1], wide(den[:, 2 * hh:2 * hh + 2], DH1), ALU.mult)
                    ins.then_inc(s.O_free, 1)
                for c in chunks3[2]:
                    gate_products(b + 1, c, SUMS + b * GROUPS + c // E1)
                if more:
                    for k in turns_of(h):
                        split_qk(b + 1, k)

            def copies_z(b, i, z_group):
                if i == 0:
                    dve.wait_ge(s.O_free, b * O1 + (O1 + RING))
                dve.wait_ge(s.prod_free, z_group - 1)
                md = m.topm[:, b * I + i, G1:2 * G1].rearrange("p (h e) -> p h e", h=H1)
                for e in range(E1):
                    ins = dve.tensor_tensor(heads8(m.prod[:, i, e, :]), heads8(m.ho[:, i, :]), wide(md[:, :, e], DH1), ALU.mult)
                ins.then_inc(s.z_ready, 1)

            def add_x2(b, i):
                dve.wait_ge(s.wo_ready, b * I + (i + 1 + 1))
                xi = m.xt[:, b * I + i, :]
                dve.scalar_tensor_tensor(xi, bank_pj[i][:, 3 * P:3 * P + D], m.gf[:, 0:1], xi, ALU.mult, ALU.add).then_inc(s.x2_ready, 1)

            dve.sem_inc(s.x2_ready, I)
            for c in range(X1):
                if c in between:
                    between[c]()
                gate_products(0, c, c // E1)
            dve.wait_ge(s.gate_ready, B)
            dve.wait_ge(s.small2_in, 16 * N_SMALL2)
            for k in range(4):
                split_qk(0, k)
            split_v(0)
            for h in range(HEAD_STEPS):
                step(0, h, False)
            with dve.Fori(0, B - 1) as b:
                ch.loop(b, DVE_STEPS_B)
                for h in range(HEAD_STEPS, STEPS):
                    step(b, h, True)
                z_group = SUMS + b * GROUPS + SUMS
                copies_z(b, 0, z_group)
                for h in range(HEAD_STEPS):
                    step(b + 1, h, False)
                    if h == 0:
                        copies_z(b, 1, z_group + 1)
                    if h == 1:
                        split_v(b + 1)
                    if h == 4:
                        add_x2(b, 0)
                add_x2(b, 1)
            ch.end_loop(B - 1)
            early = range(B - 1)
            for h in range(HEAD_STEPS, STEPS):
                step(B - 1, h, False)
                k, r = divmod(h - HEAD_STEPS, 2)
                if r == 0 and 0 < k < 3:
                    latent_norm(dve, early, k - 1)
                if r == 0 and k < 2:
                    latent_stats(dve, stats, early, k)
            z_group = SUMS + (B - 1) * GROUPS
            for i in range(I):
                copies_z(B - 1, i, z_group + i)
            dve.wait_ge(s.z_ready, B * I)
            t = m.prod[:, 1, :, :].rearrange("p e (h c) -> p e h c", h=H1)
            ch.link(dve.tensor_tensor(t[:, :, 0:4, :], t[:, :, 0:4, :], t[:, :, 4:8, :], ALU.add))
            ch.link(dve.tensor_tensor(t[:, :, 0:2, :], t[:, :, 0:2, :], t[:, :, 2:4, :], ALU.add))
            dve.tensor_tensor(m.z[:, 1, :].rearrange("p (e c) -> p e c", e=E1), t[:, :, 0, :], t[:, :, 1, :], ALU.add).then_inc(s.z_last, 1)
            for b in early:
                latent_split(dve, b, bank_S[b % 2])
            for i in range(I):
                add_x2(B - 1, i)

        def pool_b(pool, ch, rstd, split):
            def sums(b, k):
                kk = k % 2
                pr, acc = m.prod[:, kk, :, :], m.acc[:, k // I, k % I, :]
                pool.wait_ge(s.prod_ready, b * X1 + (k * E1 + 2))
                if not (isinstance(b, int) and b == 0):
                    if k < 4:
                        pool.wait_ge(s.T_ready, (b - 1) * T1 + (k + 1))
                    else:
                        pool.wait_ge(s.v1lo_ready, (b - 1) * I + (k - 4 + 1))
                ch.link(pool.tensor_tensor(acc, pr[:, 0, :], pr[:, 1, :], ALU.add))
                pool.wait_ge(s.prod_ready, b * X1 + (k * E1 + 3))
                ch.link(pool.tensor_tensor(acc, acc, pr[:, 2, :], ALU.add))
                pool.wait_ge(s.pair_ready, b * SUMS + (k + 1))
                pool.tensor_tensor(acc, acc, pr[:, 3, :], ALU.add).then_inc(s.acc_ready, 1)
                pool.wait_ge(s.acc_ready, b * SUMS + (k + 1))
                pool.sem_inc(s.prod_free, 1)

            def latent_rstd(k):
                n = (B - 1) * I if k < 2 else I
                rstd(k + 1, m.mv[:, 0:n, 1], m.rs[:, 0:n], s.x2_var, s.x2_rstd)

            def attend(b, more):
                if more:
                    for k in range(SUMS):
                        sums(b + 1, k)
                else:
                    latent_rstd(0)
                    latent_rstd(1)
                for i in range(I if more else 1):
                    pool.wait_ge(s.z_ready, b * I + (i + 1))
                    t = m.prod[:, i, :, :].rearrange("p e (h c) -> p e h c", h=H1)
                    ch.link(pool.tensor_tensor(t[:, :, 0:4, :], t[:, :, 0:4, :], t[:, :, 4:8, :], ALU.add))
                    ch.link(pool.tensor_tensor(t[:, :, 0:2, :], t[:, :, 0:2, :], t[:, :, 2:4, :], ALU.add))
                    pool.tensor_tensor(m.z[:, i, :].rearrange("p (e c) -> p e c", e=E1), t[:, :, 0, :], t[:, :, 1, :], ALU.add).then_inc(s.z_sum, 1)
                    pool.wait_ge(s.z_sum, b * I + (i + 1))
                    pool.sem_inc(s.prod_free, 1)

            for k in range(SUMS):
                sums(0, k)
            with pool.Fori(0, B - 1) as b:
                ch.loop(b, POOL_STEPS_B)
                attend(b, True)
            ch.end_loop(B - 1)
            for n in range(N_W0, N_W1):
                split(n)
            attend(B - 1, False)
            return latent_rstd

        HALF = NT // 2

        UN = H2 * I
        SPLIT_AT = UN // 2
        TILES_AO = I * 2
        TC, OC = UN + TILES_AO, HP2
        TURN_AO_AFTER = (3, 4, 6, 7)
        LAT_AT = 3
        ADD_PAIR = 1
        heads2 = lambda a: a.rearrange("p (h c) -> p h c", h=H2 // 2)

        def T_use(u, first):
            seen = TILES_AO if first else sum(after < u for after in TURN_AO_AFTER)
            return u + seen - TILES_AO

        def ao_use(p):
            return TURN_AO_AFTER[p] + 1 + p - TILES_AO

        PJ0, PJ_GROUP = KT + 2, 3
        PJ = UN // 4 * PJ_GROUP

        NORM_TILES = [(0, HALF), (HALF, NT - I)]
        NEW_TILES = (NT - I, NT)

        def pj_use(g, r, last):
            return PJ0 + g * PJ_GROUP + r - (max(0, g - KT - len(NORM_TILES)) if last else 0)

        def projection(t, last):
            g, r = t // 4, t % 4
            if r == 2 or t >= UN:
                return None
            use = pj_use(g, min(r, 2), last)
            if r < 2:
                return use, "qk", (g + 1) // HP2, (g + 1) % HP2, 1 - r
            return use, "v", g // KT, g % KT, 1 - g // KT

        def jobs(t, last):
            job = projection(t, last)
            if job and last and job[2]:
                slot = t // 4 - KT
                return [(job[0], "norm", 0, slot, 0)] if job[1] == "v" and slot < len(NORM_TILES) else []
            return [job] if job else []

        PAST_JOB = (PJ0 - 1, "v", 0, KT - 1, 0)
        FIRST_JOBS = [(n, "v", 0, n, 0) for n in range(KT - 1)] + [(KT - 1, "qk", 0, 0, 0), (KT, "qk", 0, 0, 1), (KT + 1, "v", 0, KT - 1, 0)]

        def pe_c(pe, turn):
            pe.sem_inc(s.c_T_ready, RING)
            pe.sem_inc(s.c_O_ready, RING)
            pe.wait_ge(s.T_free, B * T1 + RING)
            pe.wait_ge(s.O_free, B * O1 + RING)
            pe.wait_ge(s.x2_ready, I + B * I)
            pe.wait_ge(s.lat_lo, B - 1)
            for n in range(N_W0, N_W1):
                pe.wait_ge(s.w_split, n + 1)
            pe.wait_ge(s.kv_free, 2)

            def three(o, ah, al, bh, bl):
                pe.matmul(o, ah, bh, start=True, stop=False)
                pe.matmul(o, ah, bl, start=False, stop=False)
                return pe.matmul(o, al, bh, start=False, stop=True)

            def turn_norm(bank, tiles):
                for t in range(*tiles):
                    ins = turn(bank[:, (t - tiles[0]) * P:(t - tiles[0] + 1) * P], m.ct[:, t, :])
                return ins

            def project(b, job):
                n, kind, on, a, k = job
                pe.wait_ge(s.c_pj_free, b * PJ + (n + 1))
                if kind == "v":
                    r, w = slice(a * P, (a + 1) * P), slice(k * 512, (k + 1) * 512)
                    ins = three(bank_pj[n % 2][:, :], m.kvTh[:, b + on, r], m.kvTl[:, b + on, r], m.wv1h[:, w], m.wv1l[:, w])
                elif kind == "norm":
                    pe.wait_ge(s.x3n_ready, 1)
                    ins = turn_norm(bank_pj[n % 2], NORM_TILES[a])
                else:
                    w = slice(a * P, (a + 1) * P)
                    wh, wl = (m.wq1h, m.wq1l) if k == 0 else (m.wk1h, m.wk1l)
                    cols = slice(S, 2 * S) if k == 0 else slice(0, 2 * S)
                    o = bank_pj[n % 2][:, 0:S] if k == 0 else bank_pj[n % 2][:, :]
                    ins = three(o, wh[:, w], wl[:, w], m.kvTh[:, b + on, cols], m.kvTl[:, b + on, cols])
                ins.then_inc(s.c_pj_ready, 1)

            def scores(b, t, last=False):
                hp, hh, i = t // 4, t // 2 % 2, t % 2
                if t % 4 == 0:
                    pe.wait_ge(s.c_pj_free, b * PJ + (pj_use(hp - 1, 1, last) + 1 + RING))
                pe.wait_ge(s.c_max_done, b * UN + (t + 1))
                r, q = slice(DH2 * hh, DH2 * hh + DH2), slice(i * P, (i + 1) * P)
                three(bank_S[t % 2][:, :], m.q2h[r, hp % 2, q], m.q2l[r, hp % 2, q], m.k2h[r, hp % 2, :], m.k2l[r, hp % 2, :])\
                    .then_inc(s.c_S_ready, 1)

            def turn_ao(b, p, use):
                pe.wait_ge(s.c_O_free, b * OC + RING)
                pe.wait_ge(s.c_T_free, b * TC + (use + 1))
                bank = bank_T[use % 2]
                for j in range(4):
                    c = 4 * (p // I) + j
                    ins = turn(bank[:, j * P:(j + 1) * P], m.ao[:, p % I, c * P:(c + 1) * P])
                ins.then_inc(s.c_T_ready, 1)

            def project_ao(b, i, bank):
                pe.wait_ge(s.ao_copied, b * TILES_AO + (i + I + 1 - TILES_AO))
                for c in range(HP2):
                    ins = pe.matmul(bank[:, 4 * (DH2 + 1):4 * (DH2 + 1) + D], m.aoT[:, i, c, :], m.wo1[:, c, :], start=(c == 0), stop=(c == HP2 - 1))
                ins.then_inc(s.c_wo_ready, 1)

            def step(b, t, first=False, last=False):
                if t + 1 < UN or not last:
                    scores(b, t + 1, last)
                u = t - 3
                if u < UN and (u >= 0 or not first):
                    hp = u // 4
                    pe.wait_ge(s.c_T_free, b * TC + (T_use(u, first) + 1 + RING))
                    if u % 4 == 0:
                        pe.wait_ge(s.c_O_free, b * OC + (hp + 1))
                    if u % 4 == 3 and not first and hp - ADD_PAIR in range(I):
                        project_ao(b, hp - ADD_PAIR, bank_O[hp % 2])
                    o = bank_O[hp % 2][:, (u % 4) * (DH2 + 1):(u % 4 + 1) * (DH2 + 1)]
                    for j in range(KT):
                        ph, pl = (p[:, u % 2, j, :] for p in (m.PTh, m.PTl))
                        vh, vl = (v[:, j, u // 2 % H2, :] for v in (m.v2h, m.v2l))
                        pe.matmul(o, ph, vh, start=(j == 0), stop=False)
                        pe.matmul(o, ph, vl, start=False, stop=False)
                        ins = pe.matmul(o, pl, vh, start=False, stop=(j == KT - 1))
                    ins.then_inc(s.c_O_ready, 1)
                for job in jobs(t, last):
                    project(b, job)
                u = t - 1
                if u < UN and (u >= 0 or not first):
                    use = T_use(u, first)
                    pe.wait_ge(s.c_exp_done, b * UN + (u + 1 + RING))
                    pe.wait_ge(s.c_T_free, b * TC + (use + 1))
                    bank = bank_T[use % 2]
                    for j in range(KT):
                        ins = turn(bank[:, j * P:(j + 1) * P], m.Pr[:, u % 2, j * P:(j + 1) * P])
                    ins.then_inc(s.c_T_ready, 1)
                    if not first and u in TURN_AO_AFTER:
                        p = TURN_AO_AFTER.index(u)
                        turn_ao(b, p, ao_use(p))

            for job in FIRST_JOBS:
                project(0, job)
            scores(0, 0)
            for t in range(SPLIT_AT):
                step(0, t, first=True)
                if t == LAT_AT + 1:
                    pe.wait_ge(s.x2n_ready, 4)
                    turn_latent(pe, turn, B - 1, bank_O[1])
                if t == 6:
                    pe.wait_ge(s.lat_lo, B)
            with pe.Fori(0, B - 1) as b:
                for t in range(SPLIT_AT, UN):
                    step(b, t)
                for t in range(SPLIT_AT):
                    step(b + 1, t)
            for t in range(SPLIT_AT, UN + 3):
                step(B - 1, t, last=True)
            for p in range(TILES_AO):
                turn_ao(B, p, p - TILES_AO)
            for i in range(I):
                pe.wait_ge(s.c_O_free, B * OC + (i + 1))
                project_ao(B, i, bank_O[i])
            hidden(pe, 0, 0)
            pe.wait_ge(s.x3n_ready, 2)
            pe.wait_ge(s.c_T_free, B * TC + RING)
            turn_norm(bank_T[0], NEW_TILES).then_inc(s.xdT_ready, 1)
            pe.wait_ge(s.xd_f32, len(NORM_TILES) + 1)
            for t in range(NT):
                ins = pe.matmul(bank_T[1][:, t * E3:(t + 1) * E3], m.ct[:, t, :], m.gate[:, :], start=True, stop=True)
            ins.then_inc(s.rt_ready, 1)

        def act_c(act):
            act.sem_inc(s.c_exp_done, RING)
            act.sem_inc(s.gelu_done, HR)

            def high_norm(bank, tiles, done):
                w = (tiles[1] - tiles[0]) * P
                act.activation(m.ct[:, slice(*tiles), :].rearrange("p t c -> p (t c)"), bank[:, 0:w], ACT.Copy).then_inc(s.xd_f32, 1)
                act.activation(m.xdTh[:, slice(*tiles), :].rearrange("p t c -> p (t c)"), bank[:, 0:w], ACT.Copy).then_inc(done, 1)

            def high(b, job):
                n, kind, on, a, k = job
                act.wait_ge(s.c_pj_ready, b * PJ + (n + 1))
                if kind == "norm":
                    high_norm(bank_pj[n % 2], NORM_TILES[a], s.c_pj_hi)
                    return
                if kind == "v":
                    dst, src = m.v2h[:, a, k * 8:k * 8 + 8, 0:DH2], heads2(bank_pj[n % 2][:, :])
                    act.wait_ge(s.c_O_ready, b * UN + (UN // 2 * on + RING))
                else:
                    dst, w = ((m.q2h, S), (m.k2h, 2 * S))[k]
                    dst, src = dst[:, a % 2, :], bank_pj[n % 2][:, 0:w]
                act.activation(dst, src, ACT.Copy).then_inc(s.c_pj_hi, 1)

            def copy_ao(b, p, use):
                act.wait_ge(s.c_T_ready, b * TC + (use + 1 + RING))
                c = 4 * (p // I)
                act.activation(m.aoT[:, p % I, c:c + 4, :].rearrange("p n c -> p (n c)"), bank_T[use % 2][:, :], ACT.Copy).then_inc(s.ao_copied, 1)

            def step(b, t, first=False, last=False):
                u = t - 2
                if u < UN and (u >= 0 or not first):
                    use = T_use(u, first)
                    act.wait_ge(s.c_T_ready, b * TC + (use + 1 + RING))
                    act.wait_ge(s.c_O_ready, b * UN + (u + 1))
                    act.activation(m.PTh[:, u % 2, :, :].rearrange("p n c -> p (n c)"), bank_T[use % 2][:, :], ACT.Copy).then_inc(s.c_T_hi, 1)
                if not first and u in TURN_AO_AFTER:
                    p = TURN_AO_AFTER.index(u)
                    copy_ao(b, p, ao_use(p))
                if t < UN:
                    act.wait_ge(s.c_max_done, b * UN + (t + 1 + RING))
                    act.wait_ge(s.c_T_ready, b * TC + (T_use(u, first) + 1 + RING))
                    act.activation(m.Pr[:, t % 2, :], m.sm[:, t % 2, :], ACT.Exp, scale=-1.0, bias=m.nm[:, t % 4, 0:1]).then_inc(s.c_exp_done, 1)
                for job in jobs(t, last):
                    high(b, job)

            for job in FIRST_JOBS:
                high(0, job)
            for t in range(SPLIT_AT):
                step(0, t, first=True)
                if t == LAT_AT + 2:
                    latent_high(act, B - 1)
            with act.Fori(0, B - 1) as b:
                for t in range(SPLIT_AT, UN):
                    step(b, t)
                for t in range(SPLIT_AT):
                    step(b + 1, t)
            for t in range(SPLIT_AT, UN + 2):
                step(B - 1, t, last=True)
            for p in range(TILES_AO):
                copy_ao(B, p, p - TILES_AO)

            for f in range(FT):
                gelu(act, 0, f)
            act.wait_ge(s.xdT_ready, 1)
            high_norm(bank_T[0], NEW_TILES, s.xd_hi)
            act.wait_ge(s.rt_nmax, 1)
            act.activation(m.ex8[:, :, :], m.lgm[:, :, :], ACT.Exp).then_inc(s.rt_exp, 1)

        def dve_c(dve, ch, stats):
            dve.sem_inc(s.c_pj_free, RING)
            dve.sem_inc(s.c_max_done, RING)
            dve.sem_inc(s.c_T_free, RING)
            dve.sem_inc(s.c_O_free, RING)
            dve.sem_inc(s.h_lo, HR)
            dve.wait_ge(s.maskb_ready, 1)
            dve.wait_ge(s.v2_ones, 1)
            dve.wait_ge(s.tanh_ready, 1)

            def low_norm(bank, tiles):
                w = (tiles[1] - tiles[0]) * P
                return dve.tensor_tensor(m.xdTl[:, slice(*tiles), :].rearrange("p t c -> p (t c)"), bank[:, 0:w],
                                         m.xdTh[:, slice(*tiles), :].rearrange("p t c -> p (t c)"), ALU.subtract)

            def norm_stats(tiles):
                stats(lambda t: m.xt[:, tiles[0] + t, :], tiles[1] - tiles[0], m.st, m.mv, s.x3_var)

            def norm(k, tiles):
                dve.wait_ge(s.x3_var, k)
                dve.wait_ge(s.x3_rstd, k)
                for t in range(*tiles):
                    c = t - tiles[0]
                    ins = dve.tensor_scalar(m.ct[:, t, :], m.xt[:, t, :], m.mv[:, c, 0:1], m.rs[:, c:c + 1], ALU.subtract, ALU.mult)
                ins.then_inc(s.x3n_ready, 1)

            def low(b, job):
                n, kind, on, a, k = job
                dve.wait_ge(s.c_pj_hi, b * PJ + (n + 1))
                if kind == "norm":
                    low_norm(bank_pj[n % 2], NORM_TILES[a]).then_inc(s.c_pj_free, 1)
                    return
                if kind == "v":
                    v = (slice(None), a, slice(k * 8, k * 8 + 8), slice(0, DH2))
                    dst, src, hi = m.v2l[v], heads2(bank_pj[n % 2][:, :]), m.v2h[v]
                else:
                    hi, lo, w = ((m.q2h, m.q2l, S), (m.k2h, m.k2l, 2 * S))[k]
                    dst, src, hi = lo[:, a % 2, :], bank_pj[n % 2][:, 0:w], hi[:, a % 2, :]
                dve.tensor_tensor(dst, src, hi, ALU.subtract).then_inc(s.c_pj_free, 1)

            def take_mask(b):
                dve.wait_ge(s.c_max_done, b * UN + RING)
                dve.tensor_copy(m.maskrow[:, :], m.maskb[:, b, :]).then_inc(s.maskrow_ready, 1)
                dve.wait_ge(s.maskrow_ready, b + 1)

            def free_ao(b, p, use):
                dve.wait_ge(s.c_T_free, b * TC + (use + RING))
                dve.wait_ge(s.ao_copied, b * TILES_AO + (p + 1 - TILES_AO))
                dve.sem_inc(s.c_T_free, 1)

            def add_x3(b, i, bank):
                dve.wait_ge(s.c_wo_ready, b * I + (i + 1 - I))
                xi = m.xt[:, b * I + (i - I), :]
                return dve.scalar_tensor_tensor(xi, bank[:, 4 * (DH2 + 1):4 * (DH2 + 1) + D], m.gx[:, 1:2], xi, ALU.mult, ALU.add)

            def step(b, t, first=False, last=False):
                if t < UN:
                    dve.wait_ge(s.c_S_ready, b * UN + (t + 1))
                    dve.wait_ge(s.c_exp_done, b * UN + (t + 1))
                    settle(dve, s.settled_dve)
                    dve.tensor_tensor_reduce(m.sm[:, t % 2, :], bank_S[t % 2][:, :], m.maskrow[:, :], -(DH2 ** -0.5), 3e38,
                                             ALU.add, ALU.min, m.nm[:, t % 4, 0:1]).then_inc(s.c_max_done, 1)
                for job in jobs(t - 1, last) if t > 0 else ([] if first else [PAST_JOB]):
                    low(b, job)
                u = t - 2
                if u < UN and (u >= 0 or not first):
                    use = T_use(u, first)
                    dve.wait_ge(s.c_T_hi, b * UN + (u + 1))
                    dve.tensor_tensor(m.PTl[:, u % 2, :, :].rearrange("p n c -> p (n c)"), bank_T[use % 2][:, :],
                                      m.PTh[:, u % 2, :, :].rearrange("p n c -> p (n c)"), ALU.subtract).then_inc(s.c_T_free, 1)
                if not first and u in TURN_AO_AFTER:
                    p = TURN_AO_AFTER.index(u)
                    free_ao(b, p, ao_use(p))
                hp = (t - 7) // 4
                if t % 4 == 3 and (hp >= 0 or not first):
                    dve.wait_ge(s.c_O_ready, b * UN + (4 * hp + 4 + RING))
                    O = bank_O[hp % 2][:, 0:4 * (DH2 + 1)].rearrange("p (h i c) -> p h i c", h=2, i=I)
                    den = m.den[:, 4 * (hp % 2):4 * (hp % 2) + 4]
                    ch.link(dve.reciprocal(den.rearrange("p (h i) -> p h i", h=2), O[:, :, :, DH2]))
                    at = hp % HP2 * P
                    dst = m.ao[:, :, at:at + P].rearrange("p i (h c) -> p h i c", h=2)
                    for hh in range(2):
                        ins = dve.tensor_tensor(dst[:, hh, :, :], O[:, hh, :, 0:DH2], wide(den[:, 2 * hh:2 * hh + 2], DH2), ALU.mult)
                    if not first and t < SPLIT_AT and hp - ADD_PAIR in range(I):
                        ins = add_x3(b, hp - ADD_PAIR, bank_O[hp % 2])
                    ins.then_inc(s.c_O_free, 1)

            for job in FIRST_JOBS:
                low(0, job)
            take_mask(0)
            for t in range(SPLIT_AT):
                step(0, t, first=True)
                if LAT_AT - 2 <= t <= LAT_AT:
                    if t > LAT_AT - 2:
                        latent_norm(dve, [B - 1], 1 + t - LAT_AT + 2)
                    if t < LAT_AT:
                        latent_stats(dve, stats, [B - 1], 2 + t - LAT_AT + 2)
                if t == LAT_AT + 2:
                    latent_split(dve, B - 1, bank_O[1])
            with dve.Fori(0, B - 1) as b:
                ch.loop(b, DVE_STEPS_C)
                for t in range(SPLIT_AT, UN):
                    step(b, t)
                take_mask(b + 1)
                for t in range(SPLIT_AT):
                    step(b + 1, t)
            ch.end_loop(B - 1)
            OLD_TILES = (0, NT - I)
            for t in range(SPLIT_AT, UN + 4):
                step(B - 1, t, last=True)
                if t == SPLIT_AT:
                    dve.wait_ge(s.c_O_free, (B - 1) * OC + (ADD_PAIR + I + RING))
                    norm_stats(OLD_TILES)
                if t == SPLIT_AT + 2:
                    norm(1, OLD_TILES)
            for p in range(TILES_AO):
                free_ao(B, p, p - TILES_AO)
            for i in range(I):
                ins = add_x3(B, i, bank_O[i])
            ch.link(ins)

            norm_stats(NEW_TILES)
            norm(2, NEW_TILES)
            dve.wait_ge(s.xd_hi, 1)
            low_norm(bank_T[0], NEW_TILES).then_inc(s.xd_lo, 1)
            hidden_low(dve, 0, 0)
            dve.wait_ge(s.rt_ready, 1)
            ch.link(dve.tensor_copy(m.lg[:, :, :].rearrange("p t e -> p (t e)"), bank_T[1][:, 0:NT * E3]))
            for t in range(NT):
                ins = dve.max(m.m8[:, t, :], m.lg[:, t, :])
            ch.link(ins)
            dve.tensor_tensor(m.lgm[:, :, :], m.lg[:, :, :], m.m8[:, :, 0:1].to_broadcast([P, NT, E3]), ALU.subtract).then_inc(s.rt_nmax, 1)
            for t in range(NT):
                ins = dve.max_index(m.ix8[:, t, :], m.m8[:, t, :], m.lg[:, t, :])
            ch.link(ins)
            ch.link(dve.tensor_copy(m.ixf[:, :], m.ix8[:, :, 0]))
            ch.link(dve.tensor_tensor(m.we1[:, :, :], m.iota_f[:, :].unsqueeze(1).to_broadcast([P, NT, E3]), wide(m.ixf[:, :], E3), ALU.is_equal))
            dve.wait_ge(s.rt_exp, 1)
            ch.link(dve.tensor_reduce(m.sum8[:, :], m.ex8[:, :, :], AX.X, ALU.add))
            ch.link(dve.reciprocal(m.wmax[:, :], m.sum8[:, :]))
            ch.link(dve.tensor_scalar(m.wmax[:, :], m.wmax[:, :], m.gf[:, 1:2], None, ALU.mult))
            dve.tensor_tensor(m.we[:, :, :].rearrange("p e t -> p t e"), m.we1[:, :, :], wide(m.wmax[:, :], E3), ALU.mult).then_inc(s.we_ready, 1)
            dve.wait_ge(s.we_ready, 1)

        def pool_c(pool, ch, rstd, split, latent_rstd):
            pool.wait_ge(s.z_sum, B * I - 1)
            pool.wait_ge(s.z_last, 1)
            pool.memset(m.v2h[:, :, :, DH2], 1.0)
            pool.memset(m.v2l[:, :, :, DH2], 0.0).then_inc(s.v2_ones, 1)
            latent_rstd(2)
            latent_rstd(3)
            pool.wait_ge(s.pj_ready, B * X1)
            for n in range(N_W1, N_WALL):
                split(n)
            for k, n in enumerate((NT - I, I)):
                rstd(k + 1, m.mv[:, 0:n, 1], m.rs[:, 0:n], s.x3_var, s.x3_rstd)

        YR = 4
        HR = 4
        bank_h, bank_y = bk[0:HR], bk[4:8]
        HU = 2 * FT

        def hidden(pe, e, a):
            if isinstance(e, int) and e == 0 and a == 0:
                pe.wait_ge(s.c_pj_free, B * PJ + len(NORM_TILES) + RING)
                for n in range(N_W1, N_WALL):
                    pe.wait_ge(s.w_split, n + 1)
            for f in range(FT):
                use = a * FT + f
                pe.wait_ge(s.gelu_done, e * HU + (use + 1))
                o, w = bank_h[use % HR][:, :], slice(f * P, (f + 1) * P)
                xh, xl = (x_[:, a * HALF:(a + 1) * HALF, :].rearrange("p t c -> p (t c)") for x_ in (m.xdTh, m.xdTl))
                pe.matmul(o, m.w1h[:, e, w], xh, start=True, stop=False)
                pe.matmul(o, m.w1h[:, e, w], xl, start=False, stop=False)
                pe.matmul(o, m.w1l[:, e, w], xh, start=False, stop=True).then_inc(s.h_ready, 1)

        def gelu(act, e, use):
            act.wait_ge(s.h_ready, e * HU + (use + 1))
            act.wait_ge(s.h_lo, e * HU + (use + 1))
            settle(act, s.settled_act)
            act.activation(m.hf[:, use % HR, :], bank_h[use % HR][:, :], ACT.Gelu, bias=m.b1T[:, e, use % FT:use % FT + 1]).then_inc(s.gelu_done, 1)

        def hidden_low(dve, e, a):
            for f in range(FT):
                use = a * FT + f
                dve.wait_ge(s.h_hi, e * HU + (use + 1))
                dve.tensor_tensor(m.hTl[:, a, f, :], m.hf[:, use % HR, :], m.hTh[:, a, f, :], ALU.subtract).then_inc(s.h_lo, 1)

        def pe_d(pe, turn):
            pe.sem_inc(s.y_ready, NT)
            pe.wait_ge(s.xd_lo, 1)

            def outputs(e, a, late=0):
                for t in range(HALF):
                    use = a * HALF + t
                    pe.wait_ge(s.y_free, e * NT + (use + late + 1))
                    o = bank_y[use % YR][:, 0:D]
                    for f in range(FT):
                        if t == 0:
                            pe.wait_ge(s.h_lo, e * HU + (a * FT + f + 1 + HR))
                        hh, hl = (h_[:, a, f, t * P:(t + 1) * P] for h_ in (m.hTh, m.hTl))
                        pe.matmul(o, hh, m.w2h[:, e, f, :], start=(f == 0), stop=False)
                        pe.matmul(o, hh, m.w2l[:, e, f, :], start=False, stop=False)
                        ins = pe.matmul(o, hl, m.w2h[:, e, f, :], start=False, stop=(f == FT - 1))
                    ins.then_inc(s.y_ready, 1)

            def second_bias(a):
                pe.wait_ge(s.weT_copied, 2)
                for t in range(a * HALF, (a + 1) * HALF):
                    pe.wait_ge(s.y_free, E3 * NT + (a * HALF - HALF + t + 1))
                    pe.matmul(bank_y[t % YR][:, 0:D], m.weT[:, t, :], m.b2[:, :], start=True, stop=True).then_inc(s.y_ready, 1)

            hidden(pe, 0, 1)
            pe.wait_ge(s.we_ready, 1)
            with pe.Fori(0, E3 - 1) as e:
                outputs(e, 0)
                hidden(pe, e + 1, 0)
                outputs(e, 1)
                hidden(pe, e + 1, 1)
            outputs(E3 - 1, 0)
            pe.wait_ge(s.gelu_done, E3 * HU - 2 + HR)
            for t in range(NT):
                ins = turn(bank_h[t // HALF][0:E3, t % HALF * P:(t % HALF + 1) * P], m.we[:, :, t])
                if t % HALF == HALF - 1:
                    ins.then_inc(s.weT_ready, 1)
            second_bias(0)
            outputs(E3 - 1, 1, HALF)
            second_bias(1)

        def act_d(act):
            with act.Fori(0, E3 - 1) as e:
                for use in range(FT, HU):
                    gelu(act, e, use)
                for use in range(FT):
                    gelu(act, e + 1, use)
            for use in range(FT, HU):
                gelu(act, E3 - 1, use)

        def pool_d(pool):
            pool.wait_ge(s.c_O_ready, B * UN + RING)
            with pool.Fori(0, E3) as e:
                for use in range(HU):
                    pool.wait_ge(s.gelu_done, e * HU + (use + 1 + HR))
                    if use % FT == 0:
                        pool.wait_ge(s.y_ready, e * NT + (use // FT * HALF + HALF))
                    settle(pool, s.settled_pool)
                    pool.tensor_scalar(m.hTh[:, use // FT, use % FT, :], m.hf[:, use % HR, :], 1.0, 0.0, ALU.mult, ALU.add).then_inc(s.h_hi, 1)

        def dve_d(dve, ch):
            dve.sem_inc(s.y_free, YR)

            def add(e, a, late=0):
                for t in range(a * HALF, (a + 1) * HALF):
                    dve.wait_ge(s.y_ready, e * NT + (NT + t + late + 1))
                    dve.scalar_tensor_tensor(m.xt[:, t, :], bank_y[t % YR][:, 0:D], m.we[:, e, t:t + 1], m.xt[:, t, :], ALU.mult, ALU.add)\
                        .then_inc(s.y_free, 1)

            def add_bias(a):
                for t in range(a * HALF, (a + 1) * HALF):
                    dve.wait_ge(s.y_ready, E3 * NT + (NT + a * HALF - HALF + t + 1))
                    dve.tensor_tensor(m.xt[:, t, :], m.xt[:, t, :], bank_y[t % YR][:, 0:D], ALU.add).then_inc(s.y_free, 1)
                dve.wait_ge(s.y_free, E3 * NT + (NT * a + YR))
                dve.sem_inc(s.out_ready, 1)

            with dve.Fori(0, E3 - 1) as e:
                hidden_low(dve, e, 1)
                add(e, 0)
                hidden_low(dve, e + 1, 0)
                add(e, 1)
            hidden_low(dve, E3 - 1, 1)
            add(E3 - 1, 0)
            for a in range(2):
                dve.wait_ge(s.weT_ready, a + 1)
                dve.tensor_copy(m.weT[:, a * HALF:(a + 1) * HALF, :].rearrange("p t c -> p (t c)"), bank_h[a][0:E3, :]).then_inc(s.weT_copied, 1)
            add_bias(0)
            add(E3 - 1, 1, HALF)
            add_bias(1)

        @block.sync
        def _(sp):
            sp.dma_start(m.xt[:, :, :], xf).then_inc(s.x_in, 16)
            sp.dma_start(m.ct[:, :, :], cf).then_inc(s.ctx_in, 16)
            for dst, src in ((m.wi_row, w_i), (m.wf_row, w_f)):
                sp.dma_start(dst[:, :], src).then_inc(s.wg_in, 16)
            SMALL = [(m.bi[:, :], b_i.partition_broadcast(P)), (m.bf[:, :], b_f.partition_broadcast(P)),
                     (m.lnw[:, :], ln_w.partition_broadcast(P)), (m.gx[:, :], g_x.partition_broadcast(P)),
                     (m.gf[:, :], g_f.partition_broadcast(P)),
                     (m.cols[:, 0:1], gm.rearrange("(p a) -> p a", a=1)), (m.cols[:, 1:2], bm.rearrange("(p a) -> p a", a=1)),
                     (m.wsd[:, 0:G1], Ws), (m.wsd[:, G1:2 * G1], Wd)]
            for dst, src in SMALL:
                sp.dma_start(dst, src).then_inc(s.small_in, 16)
            def later_inputs():
                for c, v in enumerate((gl, bl)):
                    sp.dma_start(m.cols[:, 2 + c:3 + c], v.rearrange("(p a) -> p a", a=1)).then_inc(s.small2_in, 16)
                sp.dma_start(m.mask_u8[:, :, :], mask.partition_broadcast(P)).then_inc(s.small2_in, 16)
                wo = Wo0.rearrange("d (e n) -> e d n", e=E1)
                for e in range(E1):
                    sp.dma_start(m.wo0[DH1 * (e % 2):DH1 * (e % 2) + DH1, e // 2, :], wo[e, :, :]).then_inc(s.small2_in, 16)
                sp.dma_start(m.wo1[:, :, :], Wo1.rearrange("(t p) n -> p t n", p=P)).then_inc(s.small2_in, 16)
                sp.dma_start(m.gate[:, :], gate_w).then_inc(s.small2_in, 16)
                sp.dma_start(m.b1_row[:, :], b1.rearrange("e (f p) -> (e f) p", p=P)).then_inc(s.small2_in, 16)
                sp.dma_start(m.b2[:, :], b2).then_inc(s.small2_in, 16)

            for n, (src, w, _, _) in enumerate(chunks):
                if n == N_STAGE:
                    later_inputs()
                if n >= N_STAGE:
                    sp.wait_ge(s.w_split, n - N_STAGE + 1)
                dst = m.stage[:, n % N_STAGE, 0:w]
                if len(src.shape) == 3:
                    dst = dst.rearrange("p (e n) -> p e n", e=src.shape[1])
                sp.dma_start(dst, src).then_inc(stage_in[n % N_STAGE], 16)
            for a in range(2):
                sp.wait_ge(s.out_ready, a + 1)
                sp.dma_start(outf[:, a * HALF:(a + 1) * HALF, :], m.xt[:, a * HALF:(a + 1) * HALF, :]).then_inc(s.out_done, 16)
            sp.wait_ge(s.out_done, 32)

        @block.scalar
        def _(act):
            for j in range(2):
                act.wait_ge(s.cT_ready, j + 1)
                act.activation(m.cT[:, 4 * j:4 * j + 4, :].rearrange("p t c -> p (t c)"), bk[2 + j][:, :], ACT.Copy).then_inc(s.cT_copied, 1)
            for j in range(2):
                act.wait_ge(s.xT_ready, j + 1)
                act.activation(m.xnT[:, 4 * j:4 * j + 4, :].rearrange("p t c -> p (t c)"), bk[j][:, :], ACT.Copy).then_inc(s.xT_copied, 1)
            act.wait_ge(s.small_in, 16 * N_SMALL)
            act.activation(m.gx[:, :], m.gx[:, :], ACT.Tanh)
            act.activation(m.gf[:, :], m.gf[:, :], ACT.Tanh).then_inc(s.tanh_ready, 1)
            act.wait_ge(s.gates_b, 1)
            act.activation(m.tmp_a[:, :, :, :], m.fg[:, :, :, :], ACT.Abs).then_inc(s.act_chain, 1)
            act.wait_ge(s.act_chain, 1)
            act.activation(m.tmp_b[:, :, :, :], m.tmp_a[:, :, :, :], ACT.Exp, scale=-1.0).then_inc(s.act_chain, 1)
            act.wait_ge(s.act_chain, 2)
            act.activation(m.tmp_a[:, :, :, :], m.tmp_b[:, :, :, :], ACT.Ln, bias=1.0).then_inc(s.softplus, 1)
            for j in range(2):
                act.wait_ge(s.cn_T, j + 1)
                act.activation(m.sm[:, j, :], bk[j][:, :], ACT.Identity, scale=m.cols[:, 0:1], bias=m.cols[:, 1:2]).then_inc(s.kv_f, 1)

            def weights_high(n):
                act.wait_ge(stage_in[n % N_STAGE], 16 * (n // N_STAGE + 1))
                act.activation(chunks[n][2], staged(n), ACT.Copy).then_inc(s.w_hi, 1)

            for n in range(2):
                weights_high(n)
            act.wait_ge(s.mlog_ready, 1)
            act.activation(m.en[:, :, :, :], m.mlog[:, :, :, :], ACT.Exp, scale=-1.0).then_inc(s.en_ready, 1)

            def decay(u):
                b, h = divmod(u, NH0)
                act.wait_ge(s.L_ready, u + 1)
                if u >= 2:
                    act.wait_ge(s.C_ready, u - 1)
                act.activation(m.Dm[:, u % 2, 0:S], bk[u % 2][:, 0:S], ACT.Exp, scale=-1.0, bias=m.at[:, 0, b, h:h + 1])
                act.activation(m.Dm[:, u % 2, S:W0], bk[u % 2][:, S:W0], ACT.Exp, scale=-1.0, bias=m.at[:, 1, b, h:h + 1]).then_inc(s.D_ready, 1)

            def after_x1(b):
                act.wait_ge(s.x1T_ready, b + 1)
                if b >= 1:
                    act.wait_ge(s.g1_ready, b)
                src = bk[6][:, 0:S]
                act.activation(m.xT32[:, :, :].rearrange("p i c -> p (i c)"), src, ACT.Copy).then_inc(s.x1T_f32, 1)
                act.activation(m.xbTh[:, I * b:I * b + I, :].rearrange("p i c -> p (i c)"), src, ACT.Copy).then_inc(s.x1T_hi, 1)

            def gate_exp(b):
                act.wait_ge(s.g1_ready, b + 1)
                if b >= 1:
                    act.wait_ge(s.gate_ready, b)
                act.activation(m.sg[:, :, :].rearrange("p i g -> p (i g)"), bk[7][:, 0:I * 2 * G1], ACT.Exp, scale=-1.0).then_inc(s.g1_exp, 1)

            def normaliser(b):
                act.wait_ge(s.C_free, NH0 * (b + 1))
                if b >= 1:
                    act.wait_ge(s.O0_free, b)
                act.activation(m.absc[:, :], bk[4 + b % 2][:, 0:264].rearrange("p (n c) -> p n c", c=33)[:, :, 32], ACT.Abs).then_inc(s.absc_ready, 1)

            for u in range(UNITS):
                decay(u)
                b, r = divmod(u, NH0)
                if r == 0 and b >= 1:
                    normaliser(b - 1)
                if r == 0 and b >= 2:
                    after_x1(b - 2)
                if r == 2 and b >= 2:
                    gate_exp(b - 2)
                if r == 3:
                    weights_high(2 + b)
            normaliser(B - 1)
            after_x1(B - 2)
            gate_exp(B - 2)
            after_x1(B - 1)
            gate_exp(B - 1)
            act_b(act)
            act_c(act)
            act_d(act)

        @block.gpsimd
        def _(pool):
            ch = Chain(pool, s.pool_chain)
            ch.link(pool.memset(m.ident[:, :], 0.0))
            pool.affine_select(out=m.ident[:, :], in_=m.ident[:, :], compare_op=ALU.not_equal, fill=1.0, base=0,
                               pattern=[[-1, P]], channel_multiplier=1).then_inc(s.const, 1)
            pool.memset(m.mhalf[:, :], -0.5)
            pool.memset(m.identb[:, :], 0.0)
            pool.memset(m.tri[:, :], 1.0)
            pool.memset(m.sel3[:, :], 0.0)
            pool.memset(m.a3[:, :, :], 0.0)
            pool.memset(m.M3[:, :], 0.0)
            ch.link(pool.memset(m.causal[:, :], 0.0))

            def rstd(k, src, dst, ready, done, n=None):
                pool.wait_ge(ready, k)
                settle(pool, s.settled_pool)
                ch.link(pool.tensor_scalar(dst, src, 1.0, EPS, ALU.mult, ALU.add))
                pool.tensor_tensor(dst, dst, m.mhalf[:, 0:dst.shape[1]], ALU.pow).then_inc(done, 1)

            rstd(1, m.mv[:, :, 1], m.rs[:, :], s.x_var, s.x_rstd)
            pool.memset(m.ones[:, :], 1.0)
            pool.memset(m.zero16[:, :], 0.0)
            pool.affine_select(out=m.identb[:, :], in_=m.identb[:, :], compare_op=ALU.not_equal, fill=1.0, base=0,
                               pattern=[[-1, P]], channel_multiplier=1)
            for part in range(3):
                ins = pool.affine_select(out=m.sel3[:, :], in_=m.sel3[:, :], compare_op=ALU.not_equal, fill=1.0,
                                         base=-PART_AT * part, pattern=[[-1, PART_AT]], channel_multiplier=1)
                ch.link(ins)
            pool.affine_select(out=m.tri[:, :], in_=m.tri[:, :], compare_op=ALU.is_ge, fill=0.0, base=0,
                               pattern=[[1, P]], channel_multiplier=-1)
            for c in (0, S):
                pool.affine_select(out=m.causal[:, c:c + P], in_=m.causal[:, c:c + P], compare_op=ALU.is_ge, fill=BIG,
                                   base=0, pattern=[[1, P]], channel_multiplier=-1)
            pool.memset(m.vx[:, :, :, :], 1.0).then_inc(s.const, 1)
            rstd(2, m.mv2[:, :, 1], m.rs2[:, :], s.x_var, s.x_rstd)
            pool.wait_ge(s.const, 2)
            pool.tensor_scalar(m.vx[:, :, :, 0:DH0], m.ct[:, :, :].rearrange("p t (h c) -> p t h c", h=NH0), 1.0, 0.0,
                               ALU.mult, ALU.add).then_inc(s.vx_ready, 1)

            def split(n):
                _, _, hi, lo = chunks[n]
                raw = staged(n)
                pool.wait_ge(stage_in[n % N_STAGE], 16 * (n // N_STAGE + 1))
                if n >= N_W0:
                    pool.tensor_scalar(hi, raw, 1.0, 0.0, ALU.mult, ALU.add).then_inc(s.w_hi, 1)
                pool.wait_ge(s.w_hi, n + 1)
                pool.tensor_tensor(lo, raw, hi, ALU.subtract).then_inc(s.w_split, 1)

            for j in range(2):
                pool.wait_ge(s.kv_f, j + 1)
                src = m.sm[:, j, :].rearrange("p (b c) -> p b c", b=2)
                hi, lo = m.kvTh[:, 2 * j:2 * j + 2, 0:S], m.kvTl[:, 2 * j:2 * j + 2, 0:S]
                ch.link(pool.tensor_scalar(hi, src, 1.0, 0.0, ALU.mult, ALU.add))
                pool.tensor_tensor(lo, src, hi, ALU.subtract).then_inc(s.kv_free, 1)
            for n in range(3):
                split(n)
            for b in range(B):
                rstd(b + 1, m.v32[:, :], m.r32[:, :], s.var0, s.rstd0)
                rstd(b + 1, m.mv[:, 0:I, 1], m.rs[:, 0:I], s.x1_var, s.x1_rstd)
                if b < 3:
                    split(3 + b)
            pool.memset(m.maskb[:, :, S:2 * S], 0.0)
            pool.wait_ge(s.small2_in, 16 * N_SMALL2)
            pool.tensor_scalar(m.maskb[:, :, 0:S], m.mask_u8[:, :, :], BIG, -BIG, ALU.mult, ALU.add).then_inc(s.maskb_ready, 1)
            pool.iota(m.iota_i[:, :], pattern=[[1, E3]], base=0, channel_multiplier=0).then_inc(s.const, 1)
            pool.wait_ge(s.const, 3)
            pool.tensor_copy(m.iota_f[:, :], m.iota_i[:, :])
            pool.memset(m.v1h[:, :, :, DH1], 1.0)
            pool.memset(m.v1l[:, :, :, DH1], 0.0).then_inc(s.const, 1)
            latent_rstd = pool_b(pool, ch, rstd, split)
            pool_c(pool, ch, rstd, split, latent_rstd)
            pool_d(pool)

        @block.tensor
        def _(pe):
            def turn(dst, src):
                return pe.transpose(dst, src, m.ident[0:src.shape[0], 0:src.shape[0]])

            pe.wait_ge(s.const, 1)
            pe.wait_ge(s.ctx_in, 16)
            for t in range(NT):
                ins = turn(bk[2 + t // 4][:, t % 4 * P:(t % 4 + 1) * P], m.ct[:, t, :])
                if t % 4 == 3:
                    ins.then_inc(s.cT_ready, 1)
            pe.wait_ge(s.wg_in, 16 * 2)
            for c in range(3):
                for g, row in enumerate((m.wi_row, m.wf_row)):
                    t = turn(bk[7][:, c * 8 + 4 * g:c * 8 + 4 * g + 4], row[:, c * D:(c + 1) * D])
            t.then_inc(s.wg_T, 1)
            G = [bk[6][:, t * 8:t * 8 + 8] for t in range(NT)]
            pe.wait_ge(s.wg_ready, 1)
            for t in range(NT):
                if t % 4 == 0:
                    pe.wait_ge(s.cT_copied, t // 4 + 1)
                pe.matmul(G[t], m.cT[:, t, :], m.wg_ctx[:, :], start=(t == 0), stop=False)
            for t in range(NT):
                pe.wait_ge(s.xn_ready, t + 1)
                ins = turn(bk[t // 4][:, t % 4 * P:(t % 4 + 1) * P], m.xn[:, t, :])
                if t % 4 == 3:
                    ins.then_inc(s.xT_ready, 1)
            for t in range(NT):
                if t % 4 == 0:
                    pe.wait_ge(s.xT_copied, t // 4 + 1)
                ins = pe.matmul(G[t], m.xnT[:, t, :], m.wg[:, 0, :], start=False, stop=(t == NT - 1))
            ins.then_inc(s.gates, 1)
            pe.wait_ge(s.xn_ready, NT + 1)
            for t in range(NT):
                ins = turn(bk[t // 4][:, t % 4 * P:(t % 4 + 1) * P], m.xn[:, t, :])
                if t % 4 == 3:
                    ins.then_inc(s.cn_T, 1)
            pe.wait_ge(s.const, 2)
            pe.wait_ge(s.logf_ready, 1)
            lf = [m.logf[:, i, :, :].rearrange("p b h -> p (b h)") for i in range(I)]
            pe.matmul(bk[7][:, 0:16], m.tri[:, :], lf[0], start=True, stop=True)
            pe.matmul(bk[7][:, 16:32], m.tri[:, :], lf[1], start=True, stop=False)
            pe.matmul(bk[7][:, 16:32], m.ones[:, :], lf[0], start=False, stop=True).then_inc(s.F_ready, 1)
            pe.wait_ge(s.a_ready, 1)
            for i in range(I):
                ins = turn(bk[7][0:M_ROWS, 128 + i * P:128 + (i + 1) * P], m.a3[:, i, :])
            ins.then_inc(s.aT_ready, 1)
            pe.wait_ge(s.M_ready, 1)
            for i in range(I):
                ins = turn(bk[6][:, 128 + 16 * i:144 + 16 * i], m.M16[0:UNITS, i * P:(i + 1) * P])
            ins.then_inc(s.Mt_ready, 1)

            pe.wait_ge(s.M3_ready, 1)
            pe.wait_ge(s.halves_ready, 2)
            pe.wait_ge(s.kv_f, 2)

            def scores(u):
                b, h = divmod(u, NH0)
                if u >= 2:
                    pe.wait_ge(s.D_ready, u - 1)
                L = bk[u % 2][:, 0:W0]
                pe.matmul(L, m.sel3[:, u:u + 1].to_broadcast([M_ROWS, P]), m.M3[:, :], start=True, stop=False)
                for c in (0, S):
                    ins = pe.matmul(L[:, c:c + P], m.identb[:, :], m.causal[:, c:c + P], start=False, stop=(c == S))
                ins.then_inc(s.L_ready, 1)
                if u >= 2:
                    pe.wait_ge(s.C_ready, u - 1)
                r = slice(DH0 * h, DH0 * (h + 1))
                Sb = bk[2 + u % 2]
                for i, at, w in ((0, 0, S), (1, S, P)):
                    qh, ql = (q[r, I * b + i:I * b + I, :].rearrange("p i c -> p (i c)") for q in (m.xTh, m.xTl))
                    kh, kl = (k[r, I * b + i, :] for k in (m.cTh, m.cTl))
                    pe.matmul(Sb[:, at:at + w], kh, qh, start=True, stop=False)
                    pe.matmul(Sb[:, at:at + w], kh, ql, start=False, stop=False)
                    ins = pe.matmul(Sb[:, at:at + w], kl, qh, start=False, stop=True)
                ins.then_inc(s.S0_ready, 1)

            def values(u):
                b, h = divmod(u, NH0)
                if h == 0 and b >= 2:
                    pe.wait_ge(s.O0_free, b - 1)
                pe.wait_ge(s.C_ready, u + 1)
                C = m.C[:, u % 2, :]
                O = bk[4 + b % 2][:, 0:264].rearrange("p (i h c) -> p i h c", i=I, h=NH0)
                pe.matmul(O[:, 0, h, :], C[:, 0:P], m.vx[:, I * b, h, :], start=True, stop=True)
                pe.matmul(O[:, 1, h, :], C[:, P:S], m.vx[:, I * b, h, :], start=True, stop=False)
                ins = pe.matmul(O[:, 1, h, :], C[:, S:W0], m.vx[:, I * b + 1, h, :], start=False, stop=True)
                ins.then_inc(s.C_free, 1)

            def x1_turn(b):
                pe.wait_ge(s.x1n_ready, b + 1)
                if b >= 1:
                    pe.wait_ge(s.x1T_lo, b)
                if b == 0:
                    pe.wait_ge(s.mlog_ready, 1)
                for i in range(I):
                    ins = turn(bk[6][:, i * P:(i + 1) * P], m.n2[:, i, :])
                ins.then_inc(s.x1T_ready, 1)

            def x1_gates(b):
                pe.wait_ge(s.x1T_f32, b + 1)
                if b >= 1:
                    pe.wait_ge(s.g1_exp, b)
                for i in range(I):
                    ins = pe.matmul(bk[7][:, i * 2 * G1:(i + 1) * 2 * G1], m.xT32[:, i, :], m.wsd[:, :], start=True, stop=True)
                ins.then_inc(s.g1_ready, 1)

            pe.wait_ge(s.vx_ready, 1)
            scores(0)
            for u in range(UNITS):
                if u + 1 < UNITS:
                    scores(u + 1)
                values(u)
                b, r = divmod(u, NH0)
                if r == 0 and b >= 2:
                    x1_turn(b - 2)
                if r == 1 and b >= 2:
                    x1_gates(b - 2)

            def b1_turn():
                pe.wait_ge(s.small2_in, 16 * N_SMALL2)
                pe.wait_ge(s.C_ready, UNITS)
                turn(bk[2][:, 0:E3 * FT], m.b1_row[:, :]).then_inc(s.b1T_ready, 1)

            pe.wait_ge(s.D_ready, UNITS)
            pe_b(pe, turn, {0: lambda: x1_turn(B - 2), 2: lambda: x1_gates(B - 2), 4: b1_turn,
                             9: lambda: x1_turn(B - 1), 13: lambda: x1_gates(B - 1)})
            pe_c(pe, turn)
            pe_d(pe, turn)

        @block.vector
        def _(dve):
            ch = Chain(dve, s.dve_chain)

            def stats(src, n, st, mv, done):
                settle(dve, s.settled_dve)
                for t in range(n):
                    ins = dve.bn_stats(st[:, t, :], src(t))
                ch.link(ins)
                settle(dve, s.settled_dve)
                for t in range(n):
                    ins = dve.bn_aggr(mv[:, t, :], st[:, t, :])
                ins.then_inc(done, 1)

            dve.wait_ge(s.x_in, 16)
            stats(lambda t: m.xt[:, t, :], NT, m.st, m.mv, s.x_var)
            dve.wait_ge(s.wg_T, 1)
            ch.link(dve.tensor_copy(m.wg[:, :, :].rearrange("p c g -> p (c g)"), bk[7][:, 0:24]))
            dve.tensor_tensor(m.wg_ctx[:, :], m.wg[:, 1, :], m.wg[:, 2, :], ALU.add).then_inc(s.wg_ready, 1)
            dve.wait_ge(s.x_var, 1)
            dve.wait_ge(s.x_rstd, 1)
            for t in range(NT):
                dve.tensor_scalar(m.xn[:, t, :], m.xt[:, t, :], m.mv[:, t, 0:1], m.rs[:, t:t + 1], ALU.subtract, ALU.mult).then_inc(s.xn_ready, 1)
            dve.wait_ge(s.ctx_in, 16)
            stats(lambda t: m.ct[:, t, :], NT, m.st2, m.mv2, s.x_var)
            dve.wait_ge(s.x_var, 2)
            dve.wait_ge(s.x_rstd, 2)
            dve.wait_ge(s.xT_ready, 2)
            for t in range(NT):
                ins = dve.tensor_scalar(m.xn[:, t, :], m.ct[:, t, :], m.mv2[:, t, 0:1], m.rs2[:, t:t + 1], ALU.subtract, ALU.mult)
            ins.then_inc(s.xn_ready, 1)
            dve.wait_ge(s.tanh_ready, 1)
            dve.tensor_scalar(m.lnw[:, :], m.lnw[:, :], 1.0, m.gx[:, 0:1], ALU.add, ALU.mult)
            dve.wait_ge(s.gates, 1)
            G = bk[6][:, 0:64].rearrange("p (b i g) -> p b i g", b=B, i=I)

            def by_bi(a):
                return a[:, :, :, :].rearrange("p i b h -> p b i h")

            def bias(a):
                return a[:, :].unsqueeze(1).unsqueeze(1).to_broadcast([P, B, I, NH0])

            dve.tensor_tensor(by_bi(m.fg), G[:, :, :, NH0:2 * NH0], bias(m.bf), ALU.add).then_inc(s.gates_b, 1)
            ch.link(dve.tensor_tensor(by_bi(m.ig), G[:, :, :, 0:NH0], bias(m.bi), ALU.add))
            def halves(src, hi, lo):
                ch.link(dve.tensor_copy(hi[:, :, :], src[:, :, :]))
                dve.tensor_tensor(lo[:, :, :], src[:, :, :], hi[:, :, :], ALU.subtract).then_inc(s.halves_ready, 1)

            dve.wait_ge(s.cT_copied, 2)
            halves(m.cT, m.cTh, m.cTl)
            dve.wait_ge(s.softplus, 1)
            flat = lambda a: a[:, :, :, :].rearrange("p i b h -> p (i b h)")
            dve.scalar_tensor_tensor(flat(m.logf), flat(m.fg), 0.0, flat(m.tmp_a), ALU.min, ALU.subtract).then_inc(s.logf_ready, 1)
            dve.wait_ge(s.xT_copied, 2)
            halves(m.xnT, m.xTh, m.xTl)
            dve.wait_ge(s.F_ready, 1)
            ch.link(dve.tensor_copy(flat(m.Ft), bk[7][:, 0:32]))
            ch.link(dve.tensor_tensor(flat(m.at), flat(m.ig), flat(m.Ft), ALU.subtract))
            for part in range(3):
                ins = dve.tensor_copy(m.a3[:, :, PART_AT * part:PART_AT * part + UNITS], m.at[:, :, :, :].rearrange("p i b h -> p i (b h)"))
            ins.then_inc(s.a_ready, 1)
            dve.wait_ge(s.const, 2)
            dve.wait_ge(s.aT_ready, 1)
            ch.link(dve.tensor_tensor_scan(m.M16[:, 0:S], m.zero16[:, :], bk[7][0:M_ROWS, 128:128 + S], -3e38, ALU.add, ALU.max))
            dve.tensor_copy(m.M16[:, S:W0], m.M16[:, P:S]).then_inc(s.M_ready, 1)
            dve.wait_ge(s.M_ready, 1)
            rest = m.M16[:, :]
            for part in range(3):
                ch.link(dve.tensor_copy(m.Mp[:, part, :], rest))
                if part < 2:
                    ch.link(dve.tensor_tensor(m.M_rest[:, part, :], rest, m.Mp[:, part, :], ALU.subtract))
                    rest = m.M_rest[:, part, :]
            for part in range(3):
                r = slice(PART_AT * part, PART_AT * part + UNITS)
                ins = dve.tensor_copy(m.M3[r, :], m.Mp[r, part, :])
            ins.then_inc(s.M3_ready, 1)
            dve.wait_ge(s.Mt_ready, 1)
            dve.tensor_tensor(flat(m.mlog), flat(m.Ft), bk[6][:, 128:160], ALU.add).then_inc(s.mlog_ready, 1)

            def weigh(u):
                dve.wait_ge(s.S0_ready, u + 1)
                dve.wait_ge(s.D_ready, u + 1)
                if u >= 2:
                    dve.wait_ge(s.C_free, u - 1)
                dve.scalar_tensor_tensor(m.C[:, u % 2, :], bk[2 + u % 2][:, 0:W0], DH0 ** -0.5, m.Dm[:, u % 2, :],
                                         ALU.mult, ALU.mult).then_inc(s.C_ready, 1)

            def finish1(b):
                O = bk[4 + b % 2][:, 0:264].rearrange("p (n c) -> p n c", c=DH0 + 1)
                nrm, en = m.nrm[:, :].rearrange("p (i h) -> p i h", i=I), m.en[:, :, b, :]
                dve.wait_ge(s.en_ready, 1)
                dve.wait_ge(s.absc_ready, b + 1)
                ch.link(dve.tensor_tensor(nrm, m.absc[:, :].rearrange("p (i h) -> p i h", i=I), en, ALU.max))
                ch.link(dve.tensor_scalar(m.nrm[:, :], m.nrm[:, :], EPS0, None, ALU.add))
                ch.link(dve.reciprocal(m.rn[:, :], m.nrm[:, :]))
                ins = dve.tensor_tensor(m.hh[:, :, :], O[:, :, 0:DH0], wide(m.rn[:, :], DH0), ALU.mult)
                ins.then_inc(s.O0_free, 1)
                dve.wait_ge(s.O0_free, b + 1)
                ch.link(dve.tensor_reduce(m.s32[:, :], m.hh[:, :, :], AX.X, ALU.add))
                ch.link(dve.scalar_tensor_tensor(m.hc[:, :, :], wide(m.s32[:, :], DH0), -1.0 / DH0, m.hh[:, :, :], ALU.mult, ALU.add))

            def variance(b):
                ch.link(dve.tensor_tensor(m.sq[:, :, :], m.hc[:, :, :], m.hc[:, :, :], ALU.mult))
                ch.link(dve.tensor_reduce(m.s32[:, :], m.sq[:, :, :], AX.X, ALU.add))
                dve.tensor_scalar(m.v32[:, :], m.s32[:, :], 1.0 / DH0, None, ALU.mult).then_inc(s.var0, 1)

            def finish2(b):
                dve.wait_ge(s.rstd0, b + 1)
                ch.link(dve.tensor_tensor(m.sq[:, :, :], m.hc[:, :, :], wide(m.r32[:, :], DH0), ALU.mult))
                y = m.sq[:, :, :].rearrange("p (i h) c -> p i (h c)", i=I)
                ch.link(dve.tensor_tensor(y, y, m.lnw[:, :].unsqueeze(1).to_broadcast([P, I, D]), ALU.mult))
                xb = m.xt[:, I * b:I * b + I, :]
                ch.link(dve.tensor_tensor(xb, xb, y, ALU.add))
                stats(lambda t: m.xt[:, I * b + t, :], I, m.st, m.mv, s.x1_var)

            def finish3(b):
                dve.wait_ge(s.x1_var, b + 1)
                dve.wait_ge(s.x1_rstd, b + 1)
                if b >= 1:
                    dve.wait_ge(s.x1T_ready, b)
                for i in range(I):
                    ins = dve.tensor_scalar(m.n2[:, i, :], m.xt[:, I * b + i, :], m.mv[:, i, 0:1], m.rs[:, i:i + 1], ALU.subtract, ALU.mult)
                ins.then_inc(s.x1n_ready, 1)

            def x1_low(b):
                dve.wait_ge(s.x1T_hi, b + 1)
                dve.tensor_tensor(m.xbTl[:, I * b:I * b + I, :].rearrange("p i c -> p (i c)"), bk[6][:, 0:S],
                                  m.xbTh[:, I * b:I * b + I, :].rearrange("p i c -> p (i c)"), ALU.subtract).then_inc(s.x1T_lo, 1)

            def sigmoids(b):
                dve.wait_ge(s.g1_exp, b + 1)
                sgf = m.sg[:, :, :].rearrange("p i g -> p (i g)")
                ch.link(dve.tensor_scalar(sgf, sgf, 1.0, None, ALU.add))
                dve.reciprocal(sgf, sgf).then_inc(s.sg_ready, 1)

            def compare(b):
                dve.wait_ge(s.sg_ready, b + 1)
                sgf = m.sg[:, :, :].rearrange("p i g -> p (i g)")
                sg = sgf.rearrange("p (n e) -> p n e", e=E1)
                N = I * 2 * H1
                for e in range(E1):
                    if e > 0:
                        ins = dve.tensor_tensor(m.cmp[:, :, e, 0:e], sg[:, :, 0:e], sg[:, :, e:e + 1].to_broadcast([P, N, e]), ALU.is_ge)
                    if e < E1 - 1:
                        ins = dve.tensor_tensor(m.cmp[:, :, e, e:E1 - 1], sg[:, :, e + 1:E1], sg[:, :, e:e + 1].to_broadcast([P, N, E1 - 1 - e]), ALU.is_gt)
                ch.link(ins)

            def top3(b):
                sgf = m.sg[:, :, :].rearrange("p i g -> p (i g)")
                ch.link(dve.tensor_reduce(m.cnt[:, :], m.cmp[:, :, :, :].rearrange("p n e c -> p (n e) c"), AX.X, ALU.add))
                g = slice(I * b, I * b + I)
                dve.tensor_scalar(m.topm[:, g, :].rearrange("p i g -> p (i g)"), m.cnt[:, :], TOP - 0.5, None, ALU.is_lt)
                dve.scalar_tensor_tensor(m.gatev[:, g, :].rearrange("p i g -> p (i g)"), m.cnt[:, :], TOP - 0.5, sgf,
                                         ALU.is_lt, ALU.mult).then_inc(s.gate_ready, 1)

            for u in range(UNITS):
                weigh(u)
                b, r = divmod(u, NH0)
                if b >= 1:
                    (finish1, variance, finish2, finish3)[r](b - 1)
                if b >= 2 and r == 1:
                    x1_low(b - 2)
                if b >= 2 and r == 2:
                    sigmoids(b - 2)
                if b >= 2 and r == 3:
                    compare(b - 2)
                if b >= 3 and r == 0:
                    top3(b - 3)

            def b1_copy():
                dve.wait_ge(s.b1T_ready, 1)
                dve.tensor_copy(m.b1T[:, :, :].rearrange("p e f -> p (e f)"), bk[2][:, 0:E3 * FT]).then_inc(s.b1T_copied, 1)

            finish1(B - 1)
            variance(B - 1)
            dve_b(dve, ch, stats, {1: lambda: x1_low(B - 2), 2: lambda: top3(B - 3), 3: lambda: finish2(B - 1),
                                   4: lambda: sigmoids(B - 2), 5: lambda: compare(B - 2), 6: lambda: finish3(B - 1), 7: b1_copy, 8: lambda: top3(B - 2),
                                   11: lambda: x1_low(B - 1), 14: lambda: sigmoids(B - 1), 16: lambda: compare(B - 1), 18: lambda: top3(B - 1)})
            dve_c(dve, ch, stats)
            dve_d(dve, ch)


INS = ["x", "ctx_1024", "mask_BxS2_bf1", "g_xattn", "g_ffn", "L0_xattn_w_igate", "L0_xattn_b_igate", "L0_xattn_w_fgate",
       "L0_xattn_b_fgate", "L0_xattn_ln_weight", "L0_ffn_Wq", "L0_ffn_Wkv", "L0_ffn_Ws", "L0_ffn_Wd", "L0_ffn_Wo",
       "L1_xattn_gm", "L1_xattn_bm", "L1_xattn_gl", "L1_xattn_bl", "L1_xattn_Wq", "L1_xattn_Wk", "L1_xattn_Wv", "L1_xattn_Wo",
       "L1_ffn_gate_w", "L1_ffn_w1", "L1_ffn_b1", "L1_ffn_w2", "L1_ffn_b2"]


OUTS = [((B, S, D), "float32")]


def kernel(**inputs):
    import numpy as np
    import concourse.bacc as bacc
    from concourse.bass_utils import run_bass_kernel_spmd as run

    nc = bacc.Bacc("TRN2", target_bir_lowering=False, num_devices=1)
    arrays, args = {}, []
    for name in INS:
        a = np.ascontiguousarray(inputs[name])
        arrays[f"in_{name}"] = a
        args.append(nc.dram_tensor(f"in_{name}", a.shape, mybir.dt.from_np(a.dtype), kind="ExternalInput").ap())
    for i, (shape, dtype) in enumerate(OUTS):
        args.append(nc.dram_tensor(f"out_{i}", shape, mybir.dt.from_np(np.dtype(dtype)), kind="ExternalOutput").ap())
    build(nc, *args)
    r = run(nc, [arrays], core_ids=[0])
    return r.results[0]["out_0"]
```
